# Optimizing a Trainium2 kernel written in Bass

```python
import numpy as np
import jax
import jax.numpy as jnp

def _softmax(x, axis=-1):
    return jax.nn.softmax(x, axis=axis)

def _gelu(x):
    return jax.nn.gelu(x, approximate=True)

def _silu(x):
    return jax.nn.silu(x)

def _sigmoid(x):
    return jax.nn.sigmoid(x)

def _layernorm(x, axis=-1, eps=1e-05):
    m = jnp.mean(x, axis=axis, keepdims=True)
    v = jnp.var(x, axis=axis, keepdims=True)
    return (x - m) / jnp.sqrt(v + eps)

def _scatter_add(tgt, idx, src, axis=0):
    return tgt.at[idx].add(src)

def _segment_sum(src, seg, n):
    return jax.ops.segment_sum(src, seg, n)
kernel_name = 'mk_xattn_ffn_d2_seqx_r4_5572fd'

def setup_inputs(seed: int=0):
    np.random.seed(seed)
    _w = jnp.asarray

    def _rec_inputs():
        import jax
        import jax.numpy as jnp
        _rk = jax.random.key(seed)
        x = 0.0003765 + 1 * jax.random.normal(jax.random.fold_in(_rk, 1), (8, 256, 512), jnp.float32)
        _lenS = 256 - jax.random.randint(jax.random.fold_in(_rk, 7), (8,), 0, max(1, 256 // 4) + 1, jnp.int32)
        _lenS2 = 256 - jax.random.randint(jax.random.fold_in(_rk, 8), (8,), 0, max(1, 256 // 4) + 1, jnp.int32)
        _ctx_2048P = jax.random.normal(jax.random.fold_in(_rk, 11), (8, 16, 512), jnp.float32)
        _ctx_2048c = jax.random.dirichlet(jax.random.fold_in(_rk, 511), 0.3 * jnp.ones((16,), jnp.float32), (8, 256))
        _ctx_2048t = jnp.einsum('bsk,bkd->bsd', _ctx_2048c, _ctx_2048P)
        _ctx_2048t = _ctx_2048t * jax.lax.rsqrt(jnp.mean(jnp.square(_ctx_2048t)) + 1e-12) * 0.953939
        ctx_2048 = -0.000292821 + 1.00034 * (_ctx_2048t + 0.3 * jax.random.normal(jax.random.fold_in(_rk, 611), (8, 256, 512), jnp.float32))
        return (x, ctx_2048)
    x, ctx_2048 = _rec_inputs()

    def _L0_xattn_setup():
        import jax, jax.numpy as jnp
        import numpy as np
        key = jax.random.key(seed)
        k1, k2, k3, k4, k5 = jax.random.split(key, 5)
        B, D_MODEL, L = (2, 256, 512)
        HEAD_DIM = 8
        H = D_MODEL // HEAD_DIM
        return {'k': jax.random.normal(k1, (B, D_MODEL, L), dtype=jnp.float32), 'v': jax.random.normal(k2, (B, D_MODEL, L), dtype=jnp.float32), 'q': jax.random.normal(k3, (B, D_MODEL, L), dtype=jnp.float32), 'ssm_kernel': jax.random.normal(k4, (H, L), dtype=jnp.float32), 'D': jax.random.normal(k5, (H,), dtype=jnp.float32), 'head_dim': HEAD_DIM}
    _L0_xattn_all = _L0_xattn_setup()
    _L0_xattn_in = {k: v for k, v in _L0_xattn_all.items() if k in ('ssm_kernel', 'D')}
    del _L0_xattn_all

    def _L0_ffn_setup():
        import jax, jax.numpy as jnp
        import numpy as np
        EPS_LN = 1e-05
        EPS_ACT = 1e-05
        EPS_W = 1e-08

        def _layer_norm(x):
            mu = jnp.mean(x, axis=-1, keepdims=True)
            xc = x - mu
            var = jnp.mean(xc * xc, axis=-1, keepdims=True)
            return xc * jax.lax.rsqrt(var + EPS_LN)

        def _activation_quant(x):
            scale = 127.0 / jnp.clip(jnp.max(jnp.abs(x), axis=-1, keepdims=True), EPS_ACT)
            return jnp.clip(jnp.round(x * scale), -128, 127) / scale

        def _weight_quant(w):
            scale = jnp.clip(jnp.mean(jnp.abs(w)), EPS_W)
            return jnp.clip(jnp.round(w / scale), -1, 1) * scale

        def _bitlinear(x, w, b):
            xn = _layer_norm(x)
            xq = _activation_quant(xn)
            wq = _weight_quant(w)
            return jnp.einsum('bsd,fd->bsf', xq, wq) + b
        key = jax.random.key(seed)
        k1, k2, k3, k4, k5 = jax.random.split(key, 5)
        d_model, d_ff = (512, 2048)
        B, S = (4, 512)
        x = jax.random.normal(k1, (B, S, d_model), dtype=jnp.float32)
        lim1 = 1.0 / np.sqrt(d_model)
        lim2 = 1.0 / np.sqrt(d_ff)
        w1 = jax.random.uniform(k2, (d_ff, d_model), jnp.float32, -lim1, lim1)
        b1 = jax.random.uniform(k3, (d_ff,), jnp.float32, -lim1, lim1)
        w2 = jax.random.uniform(k4, (d_model, d_ff), jnp.float32, -lim2, lim2)
        b2 = jax.random.uniform(k5, (d_model,), jnp.float32, -lim2, lim2)
        return {'x': x, 'w1': w1, 'b1': b1, 'w2': w2, 'b2': b2}
    _L0_ffn_all = _L0_ffn_setup()
    _L0_ffn_in = {k: v for k, v in _L0_ffn_all.items() if k in ('w1', 'b1', 'w2', 'b2')}
    del _L0_ffn_all

    def _L1_xattn_setup():
        import jax, jax.numpy as jnp
        import numpy as np
        DIM = 512
        N_HEADS = 16
        HEAD_DIM = DIM // N_HEADS
        EPS = 1e-06
        IMG_LEN = 257

        def rms_norm(x, g, eps=EPS):
            var = jnp.mean(x * x, axis=-1, keepdims=True)
            return x * jax.lax.rsqrt(var + eps) * g

        def _attend(q, k, v, k_mask=None):
            scale = 1.0 / jnp.sqrt(jnp.asarray(HEAD_DIM, q.dtype))
            scores = jnp.einsum('bqnd,bknd->bnqk', q, k) * scale
            if k_mask is not None:
                neg = jnp.asarray(jnp.finfo(scores.dtype).min, scores.dtype)
                scores = jnp.where(k_mask[:, None, None, :], scores, neg)
            probs = jax.nn.softmax(scores, axis=-1)
            return jnp.einsum('bnqk,bknd->bqnd', probs, v)
        key = jax.random.key(seed)
        ks = jax.random.split(key, 16)
        B, L1, L2 = (1, 4096, 769)
        std = 0.02
        inp = {'x': jax.random.normal(ks[0], (B, L1, DIM), jnp.float32), 'context': jax.random.normal(ks[1], (B, L2, DIM), jnp.float32), 'context_lens': jax.random.randint(ks[2], (B,), 64, 513, jnp.int32), 'Wq': jax.random.normal(ks[3], (DIM, DIM), jnp.float32) * std, 'bq': jnp.zeros((DIM,), jnp.float32), 'gq': jnp.ones((DIM,), jnp.float32), 'Wk': jax.random.normal(ks[4], (DIM, DIM), jnp.float32) * std, 'bk': jnp.zeros((DIM,), jnp.float32), 'gk': jnp.ones((DIM,), jnp.float32), 'Wv': jax.random.normal(ks[5], (DIM, DIM), jnp.float32) * std, 'bv': jnp.zeros((DIM,), jnp.float32), 'Wk_img': jax.random.normal(ks[6], (DIM, DIM), jnp.float32) * std, 'bk_img': jnp.zeros((DIM,), jnp.float32), 'gk_img': jnp.ones((DIM,), jnp.float32), 'Wv_img': jax.random.normal(ks[7], (DIM, DIM), jnp.float32) * std, 'bv_img': jnp.zeros((DIM,), jnp.float32), 'Wo': jax.random.normal(ks[8], (DIM, DIM), jnp.float32) * std, 'bo': jnp.zeros((DIM,), jnp.float32)}
        return inp
    _L1_xattn_all = _L1_xattn_setup()
    _L1_xattn_in = {k: v for k, v in _L1_xattn_all.items() if k in ('context_lens', 'Wq', 'bq', 'gq', 'Wk', 'bk', 'gk', 'Wv', 'bv', 'Wk_img', 'bk_img', 'gk_img', 'Wv_img', 'bv_img', 'Wo', 'bo')}
    del _L1_xattn_all

    def _L1_ffn_setup():
        import jax, jax.numpy as jnp
        import numpy as np
        B, S, D, F, E, SH, K = (2, 512, 512, 256, 16, 2, 2)

        def _experts_all(x, g, gb, w1, b1, w2, b2):
            y = jax.nn.gelu(jnp.einsum('bsd,edf->bsef', x, g) + gb, approximate=False)
            y = y * (jnp.einsum('bsd,edf->bsef', x, w1) + b1)
            return jnp.einsum('bsef,efd->bsed', y, w2) + b2
        key = jax.random.key(seed)
        ks = jax.random.split(key, 8)
        std = 0.02
        mk = lambda k, sh: jax.random.normal(k, sh, jnp.float32) * std
        return {'x': jax.random.normal(ks[0], (B, S, D), jnp.float32), 'wa': mk(ks[1], (D, E)), 'rg': mk(ks[2], (E, D, F)), 'rgb': jnp.zeros((E, F), jnp.float32), 'rw1': mk(ks[3], (E, D, F)), 'rb1': jnp.zeros((E, F), jnp.float32), 'rw2': mk(ks[4], (E, F, D)), 'rb2': jnp.zeros((E, D), jnp.float32), 'sg': mk(ks[5], (SH, D, F)), 'sgb': jnp.zeros((SH, F), jnp.float32), 'sw1': mk(ks[6], (SH, D, F)), 'sb1': jnp.zeros((SH, F), jnp.float32), 'sw2': mk(ks[7], (SH, F, D)), 'sb2': jnp.zeros((SH, D), jnp.float32)}
    _L1_ffn_all = _L1_ffn_setup()
    _L1_ffn_in = {k: v for k, v in _L1_ffn_all.items() if k in ('wa', 'rg', 'rgb', 'rw1', 'rb1', 'rw2', 'rb2', 'sg', 'sgb', 'sw1', 'sb1', 'sw2', 'sb2')}
    del _L1_ffn_all
    return {'x': x, 'ctx_2048': ctx_2048, 'L0_xattn_ssm_kernel': _L0_xattn_in['ssm_kernel'], 'L0_xattn_D': _L0_xattn_in['D'], 'L0_ffn_w1': _L0_ffn_in['w1'], 'L0_ffn_b1': _L0_ffn_in['b1'], 'L0_ffn_w2': _L0_ffn_in['w2'], 'L0_ffn_b2': _L0_ffn_in['b2'], 'L1_xattn_context_lens': _L1_xattn_in['context_lens'], 'L1_xattn_Wq': _L1_xattn_in['Wq'], 'L1_xattn_bq': _L1_xattn_in['bq'], 'L1_xattn_gq': _L1_xattn_in['gq'], 'L1_xattn_Wk': _L1_xattn_in['Wk'], 'L1_xattn_bk': _L1_xattn_in['bk'], 'L1_xattn_gk': _L1_xattn_in['gk'], 'L1_xattn_Wv': _L1_xattn_in['Wv'], 'L1_xattn_bv': _L1_xattn_in['bv'], 'L1_xattn_Wk_img': _L1_xattn_in['Wk_img'], 'L1_xattn_bk_img': _L1_xattn_in['bk_img'], 'L1_xattn_gk_img': _L1_xattn_in['gk_img'], 'L1_xattn_Wv_img': _L1_xattn_in['Wv_img'], 'L1_xattn_bv_img': _L1_xattn_in['bv_img'], 'L1_xattn_Wo': _L1_xattn_in['Wo'], 'L1_xattn_bo': _L1_xattn_in['bo'], 'L1_ffn_wa': _L1_ffn_in['wa'], 'L1_ffn_rg': _L1_ffn_in['rg'], 'L1_ffn_rgb': _L1_ffn_in['rgb'], 'L1_ffn_rw1': _L1_ffn_in['rw1'], 'L1_ffn_rb1': _L1_ffn_in['rb1'], 'L1_ffn_rw2': _L1_ffn_in['rw2'], 'L1_ffn_rb2': _L1_ffn_in['rb2'], 'L1_ffn_sg': _L1_ffn_in['sg'], 'L1_ffn_sgb': _L1_ffn_in['sgb'], 'L1_ffn_sw1': _L1_ffn_in['sw1'], 'L1_ffn_sb1': _L1_ffn_in['sb1'], 'L1_ffn_sw2': _L1_ffn_in['sw2'], 'L1_ffn_sb2': _L1_ffn_in['sb2']}

def reference(x, ctx_2048, L0_xattn_ssm_kernel, L0_xattn_D, L0_ffn_w1, L0_ffn_b1, L0_ffn_w2, L0_ffn_b2, L1_xattn_context_lens, L1_xattn_Wq, L1_xattn_bq, L1_xattn_gq, L1_xattn_Wk, L1_xattn_bk, L1_xattn_gk, L1_xattn_Wv, L1_xattn_bv, L1_xattn_Wk_img, L1_xattn_bk_img, L1_xattn_gk_img, L1_xattn_Wv_img, L1_xattn_bv_img, L1_xattn_Wo, L1_xattn_bo, L1_ffn_wa, L1_ffn_rg, L1_ffn_rgb, L1_ffn_rw1, L1_ffn_rb1, L1_ffn_rw2, L1_ffn_rb2, L1_ffn_sg, L1_ffn_sgb, L1_ffn_sw1, L1_ffn_sb1, L1_ffn_sw2, L1_ffn_sb2):
    import jax
    import jax.numpy as jnp

    def _L0_xattn_ref(k, v, q, ssm_kernel, D, head_dim):
        import jax, jax.numpy as jnp
        import numpy as np
        B, HD, L = k.shape
        H = HD // head_dim
        fft_size = 2 * L
        k_ = k.reshape(B, H, head_dim, L)
        v_ = v.reshape(B, H, head_dim, L)
        q_ = q.reshape(B, H, head_dim, L)
        kv = jnp.einsum('bhil,bhjl->bijhl', k_, v_)
        kv_f = jnp.fft.rfft(kv, n=fft_size)
        kernel_f = jnp.fft.rfft(ssm_kernel, n=fft_size)
        y = jnp.fft.irfft(kv_f * kernel_f, n=fft_size)[..., :L]
        out = y + kv * D[None, None, None, :, None]
        out = jnp.einsum('bijhl,bhil->bjhl', out, q_)
        out = jnp.transpose(out, (0, 2, 1, 3)).reshape(B, H * head_dim, L)
        return out.astype(k.dtype)

    def _L0_ffn_ref(x, w1, b1, w2, b2):
        import jax, jax.numpy as jnp
        import numpy as np
        EPS_LN = 1e-05
        EPS_ACT = 1e-05
        EPS_W = 1e-08

        def _layer_norm(x):
            mu = jnp.mean(x, axis=-1, keepdims=True)
            xc = x - mu
            var = jnp.mean(xc * xc, axis=-1, keepdims=True)
            return xc * jax.lax.rsqrt(var + EPS_LN)

        def _activation_quant(x):
            scale = 127.0 / jnp.clip(jnp.max(jnp.abs(x), axis=-1, keepdims=True), EPS_ACT)
            return jnp.clip(jnp.round(x * scale), -128, 127) / scale

        def _weight_quant(w):
            scale = jnp.clip(jnp.mean(jnp.abs(w)), EPS_W)
            return jnp.clip(jnp.round(w / scale), -1, 1) * scale

        def _bitlinear(x, w, b):
            xn = _layer_norm(x)
            xq = _activation_quant(xn)
            wq = _weight_quant(w)
            return jnp.einsum('bsd,fd->bsf', xq, wq) + b
        h = _bitlinear(x, w1, b1)
        h = jax.nn.gelu(h, approximate=False)
        return _bitlinear(h, w2, b2)

    def _L1_xattn_ref(x, context, context_lens, Wq, bq, gq, Wk, bk, gk, Wv, bv, Wk_img, bk_img, gk_img, Wv_img, bv_img, Wo, bo):
        import jax, jax.numpy as jnp
        import numpy as np
        DIM = 512
        N_HEADS = 16
        HEAD_DIM = DIM // N_HEADS
        EPS = 1e-06
        IMG_LEN = 257

        def rms_norm(x, g, eps=EPS):
            var = jnp.mean(x * x, axis=-1, keepdims=True)
            return x * jax.lax.rsqrt(var + eps) * g

        def _attend(q, k, v, k_mask=None):
            scale = 1.0 / jnp.sqrt(jnp.asarray(HEAD_DIM, q.dtype))
            scores = jnp.einsum('bqnd,bknd->bnqk', q, k) * scale
            if k_mask is not None:
                neg = jnp.asarray(jnp.finfo(scores.dtype).min, scores.dtype)
                scores = jnp.where(k_mask[:, None, None, :], scores, neg)
            probs = jax.nn.softmax(scores, axis=-1)
            return jnp.einsum('bnqk,bknd->bqnd', probs, v)
        b = x.shape[0]
        n, d = (N_HEADS, HEAD_DIM)
        ctx_img = context[:, :IMG_LEN]
        ctx_txt = context[:, IMG_LEN:]
        q = rms_norm(x @ Wq + bq, gq).reshape(b, -1, n, d)
        k = rms_norm(ctx_txt @ Wk + bk, gk).reshape(b, -1, n, d)
        v = (ctx_txt @ Wv + bv).reshape(b, -1, n, d)
        k_img = rms_norm(ctx_img @ Wk_img + bk_img, gk_img).reshape(b, -1, n, d)
        v_img = (ctx_img @ Wv_img + bv_img).reshape(b, -1, n, d)
        img_x = _attend(q, k_img, v_img)
        k_mask = jnp.arange(k.shape[1])[None, :] < context_lens[:, None]
        txt_x = _attend(q, k, v, k_mask)
        out = (txt_x + img_x).reshape(b, -1, n * d)
        return out @ Wo + bo

    def _L1_ffn_ref(x, wa, rg, rgb, rw1, rb1, rw2, rb2, sg, sgb, sw1, sb1, sw2, sb2):
        import jax, jax.numpy as jnp
        import numpy as np
        B, S, D, F, E, SH, K = (2, 512, 512, 256, 16, 2, 2)

        def _experts_all(x, g, gb, w1, b1, w2, b2):
            y = jax.nn.gelu(jnp.einsum('bsd,edf->bsef', x, g) + gb, approximate=False)
            y = y * (jnp.einsum('bsd,edf->bsef', x, w1) + b1)
            return jnp.einsum('bsef,efd->bsed', y, w2) + b2
        aff = jax.nn.sigmoid(jnp.einsum('bsd,de->bse', x, wa))
        topk_p, topk_i = jax.lax.top_k(aff, K)
        topk_p = topk_p / jnp.sum(topk_p, axis=-1, keepdims=True)
        combine = jnp.sum(jax.nn.one_hot(topk_i, E, dtype=x.dtype) * topk_p[..., None], axis=2)
        routed = jnp.einsum('bsed,bse->bsd', _experts_all(x, rg, rgb, rw1, rb1, rw2, rb2), combine)
        shared = jnp.sum(_experts_all(x, sg, sgb, sw1, sb1, sw2, sb2), axis=2)
        return x + shared + routed
    x = x + _L0_xattn_ref(ctx_2048, ctx_2048, _layernorm(x, axis=-1), L0_xattn_ssm_kernel, L0_xattn_D, 8)
    x = x + _L0_ffn_ref(_layernorm(x, axis=-1), L0_ffn_w1, L0_ffn_b1, L0_ffn_w2, L0_ffn_b2)
    x = x + _L1_xattn_ref(_layernorm(x, axis=-1), ctx_2048, L1_xattn_context_lens, L1_xattn_Wq, L1_xattn_bq, L1_xattn_gq, L1_xattn_Wk, L1_xattn_bk, L1_xattn_gk, L1_xattn_Wv, L1_xattn_bv, L1_xattn_Wk_img, L1_xattn_bk_img, L1_xattn_gk_img, L1_xattn_Wv_img, L1_xattn_bv_img, L1_xattn_Wo, L1_xattn_bo)
    x = x + _L1_ffn_ref(_layernorm(x, axis=-1), L1_ffn_wa, L1_ffn_rg, L1_ffn_rgb, L1_ffn_rw1, L1_ffn_rb1, L1_ffn_rw2, L1_ffn_rb2, L1_ffn_sg, L1_ffn_sgb, L1_ffn_sw1, L1_ffn_sb1, L1_ffn_sw2, L1_ffn_sb2)
    return x

_drawn_inputs = setup_inputs


def setup_inputs(seed=0):
    import zlib

    import numpy as np

    out = dict(_drawn_inputs(seed))
    spreads = {'L1_xattn_bq': (0.0, 0.8),
     'L1_xattn_gq': (1.0, 0.6),
     'L1_xattn_bk': (0.0, 0.1),
     'L1_xattn_gk': (1.0, 0.2),
     'L1_xattn_bv': (0.0, 0.1),
     'L1_xattn_bk_img': (0.0, 2.0),
     'L1_xattn_gk_img': (1.0, 0.6),
     'L1_xattn_bv_img': (0.0, 0.8),
     'L1_xattn_bo': (0.0, 0.8),
     'L1_ffn_rgb': (0.0, 0.8),
     'L1_ffn_rb1': (0.0, 0.8),
     'L1_ffn_rb2': (0.0, 2.0),
     'L1_ffn_sgb': (0.0, 0.8),
     'L1_ffn_sb1': (0.0, 0.8),
     'L1_ffn_sb2': (0.0, 2.0)}
    factors = {'L0_ffn_w1': 7.179,
     'L0_ffn_b1': 26.136,
     'L0_ffn_w2': 7.196,
     'L0_ffn_b2': 38.38,
     'L1_xattn_Wq': 8.0,
     'L1_xattn_Wk_img': 8.0,
     'L1_xattn_Wv_img': 8.0,
     'L1_xattn_Wo': 8.0,
     'L1_ffn_wa': 8.0,
     'L1_ffn_rg': 8.0,
     'L1_ffn_rw1': 8.0,
     'L1_ffn_rw2': 8.0,
     'L1_ffn_sg': 8.0,
     'L1_ffn_sw1': 8.0,
     'L1_ffn_sw2': 8.0}
    for name, (base, spread) in spreads.items():
        noise = np.random.default_rng([zlib.crc32(name.encode()), seed]).standard_normal(out[name].shape)
        drawn = base * np.exp(spread * noise) if base else spread * noise
        out[name] = jnp.asarray(drawn.astype(out[name].dtype))
    for name, factor in factors.items():
        out[name] = (out[name] * factor).astype(out[name].dtype)
    return out
```

```python
from contextlib import ExitStack, contextmanager

import numpy as np

import concourse.bass as bass
from concourse import mybir
from concourse.alu_op_type import AluOpType as ALU

ACT = mybir.ActivationFunctionType
AX = mybir.AxisListType
F32 = mybir.dt.float32
BF16 = mybir.dt.bfloat16
I32 = mybir.dt.int32
U32 = mybir.dt.uint32

P = 128
B, S, D = 8, 256, 512
TOK = B * S
NT = TOK // P
DC = D // P
TPB = S // P
FF = 2048
FC = FF // P
HD0 = 8
H0 = S // HD0
PAIRS = HD0 * (HD0 + 1) // 2
PAD = 128
LN_EPS = 1e-5
ACT_EPS = 1e-5
W_EPS = 1e-8
ROUND = 12582912.0


class Link:

    def __init__(self, engine, sem):
        self.engine, self.sem, self.start, self.n, self.i, self.per = engine, sem, 0, 0, None, 0

    def at(self):
        return self.start + self.n if self.i is None else self.i * self.per + (self.start + self.n)

    def __call__(self, instruction, wait=True):
        instruction.then_inc(self.sem, 1)
        self.n += 1
        if wait:
            self.engine.wait_ge(self.sem, self.at())

    @contextmanager
    def loop(self, count, per):
        self.start, self.n, self.per = self.start + self.n, 0, per
        with self.engine.Fori(0, count) as i:
            self.i = i
            yield i
        assert self.n == per, f"{self.n} steps in the loop's body"
        self.start, self.n, self.i = self.start + count * per, 0, None


def pair_at(i):
    return i * HD0 - i * (i - 1) // 2


class Kernel:

    def __init__(self, nc, ins, out, scratch, ctx):
        self.nc, self.ins, self.out, self.scratch = nc, ins, out, scratch
        sb = lambda name, shape, dt: ctx.enter_context(nc.sbuf_tensor(name, shape, dt))
        self.x = sb("x_res", [P, NT, D], F32)
        self.ident = sb("ident", [P, P], F32)
        self.ident_b = sb("ident_b", [P, P], BF16)
        self.reverse = sb("reverse", [P, P], F32)
        self.ones = sb("ones", [P, P], F32)
        self.small = sb("small", [P, 8], F32)
        self.pow_half = sb("pow_half", [P, NT], F32)
        self.vectors = sb("vectors", [P, 24], F32)
        self.w1T = self.w2T = None
        self.open_semaphores, self.semaphores = ExitStack(), []

    def semaphore(self, name):
        self.semaphores.append(self.open_semaphores.enter_context(self.nc.semaphore(name)))
        return self.semaphores[-1]

    def clear_semaphores(self):
        used, self.semaphores = self.semaphores, []
        with self.nc.Block() as block:
            @block.gpsimd
            def _(pool):
                for s in used:
                    pool.sem_clear(s)
        self.open_semaphores.close()


def stage_constants(k):
    nc = k.nc
    with ExitStack() as ctx:
        taps = ctx.enter_context(nc.sbuf_tensor("taps", [H0, PAD + D], F32))
        forwards = ctx.enter_context(nc.sbuf_tensor("taps_forwards", [H0, D], F32))
        skip = ctx.enter_context(nc.sbuf_tensor("skip", [H0, 1], F32))
        sem = k.semaphore
        zeroed, selected = sem("c_zeroed"), sem("c_selected")
        taps_zeroed, taps_loaded, taps_ready, taps_stored = sem("c_tz"), sem("c_tl"), sem("c_tr"), sem("c_ts")
        block = ctx.enter_context(nc.Block())

        @block.gpsimd
        def _(pool):
            pool.memset(k.ident[:, :], 0.0).then_inc(zeroed, 1)
            pool.memset(k.ident_b[:, :], 0.0).then_inc(zeroed, 1)
            pool.memset(k.reverse[:, :], 0.0).then_inc(zeroed, 1)
            pool.memset(k.ones[:, :], 1.0)
            pool.memset(k.small[:, 0:3], ROUND)
            pool.memset(k.small[:, 3:4], RMS_EPS)
            pool.memset(k.pow_half[:, :], -0.5)
            pool.wait_ge(zeroed, 3)
            for m, base, step in ((k.ident, 0, -1), (k.ident_b, 0, -1), (k.reverse, 1 - P, 1)):
                pool.affine_select(out=m[:, :], in_=m[:, :], compare_op=ALU.not_equal, fill=1.0, base=base,
                                   pattern=[[step, P]], channel_multiplier=1).then_inc(selected, 1)

        @block.vector
        def _(dve):
            dve.memset(taps[:, D:], 0.0).then_inc(taps_zeroed, 1)
            dve.wait_ge(taps_loaded, 32)
            dve.tensor_copy(taps[:, D - 2::-1], forwards[:, 1:]).then_inc(taps_ready, 1)
            dve.tensor_tensor(taps[:, D - 1:D], forwards[:, 0:1], skip[:, :], ALU.add).then_inc(taps_ready, 1)

        @block.sync
        def _(sp):
            sp.dma_start(forwards[:, :], k.ins["L0_xattn_ssm_kernel"]).then_inc(taps_loaded, 16)
            sp.dma_start(skip[:, :], k.ins["L0_xattn_D"].rearrange("(h o) -> h o", o=1)).then_inc(taps_loaded, 16)
            sp.wait_ge(taps_zeroed, 1)
            sp.wait_ge(taps_ready, 2)
            sp.dma_start(k.scratch["taps"], taps[:, :]).then_inc(taps_stored, 16)
            sp.wait_ge(taps_stored, 16)


def stage_ternary_weights(k):
    nc = k.nc
    W = FF * D // P
    HALF = 1024
    with ExitStack() as ctx:
        sb = lambda name, shape, dt: ctx.enter_context(nc.sbuf_tensor(name, shape, dt))
        raw = [sb(f"w_raw{i}", [P, W], F32) for i in range(2)]
        tern = [sb(f"w_tern{i}", [P, W], BF16) for i in range(2)]
        total = sb("w_total", [P, 2], F32)
        inv = sb("w_inv", [P, 2], F32)
        ps_sum = ctx.enter_context(nc.psum_tensor("ps_sum", [P, 2], F32))
        ps_t = [ctx.enter_context(nc.psum_tensor(f"ps_wt{i}", [P, HALF], BF16)) for i in range(4)]
        sem = k.semaphore
        loaded = [sem("w_loaded0"), sem("w_loaded1")]
        abs_summed, sum_ready, inv_ready = sem("w_abs"), sem("w_sum"), sem("w_invr")
        scaled, rounded, transposed, copied = sem("w_scaled"), sem("w_rounded"), sem("w_transposed"), sem("w_copied")
        copied_even, dve_step = sem("w_copied_even"), sem("w_dve")
        block = ctx.enter_context(nc.Block())
        GROUPS = W // HALF

        def group(wi, g):
            for j in range(HALF // P):
                col = g * HALF + j * P
                if wi == 0:
                    c, a = col // FF, col % FF // P
                    yield j, a * D + c * P
                else:
                    c, a = col // D, col % D // P
                    yield j, a * FF + c * P

        @block.sync
        def _(sp):
            sp.dma_start(raw[0][:, :].rearrange("p (a n) -> p a n", n=D),
                         k.ins["L0_ffn_w1"].rearrange("(a p) n -> p a n", p=P)).then_inc(loaded[0], 16)
            sp.dma_start(raw[1][:, :].rearrange("p (a n) -> p a n", n=FF),
                         k.ins["L0_ffn_w2"].rearrange("(a p) n -> p a n", p=P)).then_inc(loaded[1], 16)

        @block.scalar
        def _(act):
            for wi in range(2):
                act.wait_ge(loaded[wi], 16)
                act.activation(tern[wi][:, :], raw[wi][:, :], ACT.Abs,
                               accum_out=total[:, wi:wi + 1]).then_inc(abs_summed, 1)
                act.wait_ge(inv_ready, wi + 1)
                act.activation(raw[wi][:, :], raw[wi][:, :], ACT.Identity, bias=k.small[:, 2:3],
                               scale=inv[:, wi:wi + 1]).then_inc(scaled, 1)
            for n in range(1, 2 * GROUPS, 2):
                act.wait_ge(transposed, n + 1)
                dst = (k.w1T, k.w2T)[n // GROUPS]
                act.activation(dst[:, n % GROUPS * HALF:(n % GROUPS + 1) * HALF], ps_t[n % 4][:, :],
                               ACT.Copy).then_inc(copied, 1)

        @block.tensor
        def _(pe):
            for wi in range(2):
                pe.wait_ge(abs_summed, wi + 1)
                pe.matmul(ps_sum[:, wi:wi + 1], k.ones[:, :], total[:, wi:wi + 1], start=True, stop=True)\
                  .then_inc(sum_ready, 1)
            for wi in range(2):
                pe.wait_ge(rounded, wi + 1)
                for g in range(GROUPS):
                    n = wi * GROUPS + g
                    if n >= 4:
                        pe.wait_ge(copied if n % 2 else copied_even, (n - 4) // 2 + 1)
                    for j, at in group(wi, g):
                        last = pe.transpose(ps_t[n % 4][:, j * P:(j + 1) * P], tern[wi][:, at:at + P],
                                            k.ident_b[:, :])
                    last.then_inc(transposed, 1)

        @block.vector
        def _(dve):
            link = Link(dve, dve_step)
            for wi in range(2):
                dve.wait_ge(sum_ready, wi + 1)
                link(dve.tensor_scalar(k.small[:, wi:wi + 1], ps_sum[:, wi:wi + 1], 1.0 / (FF * D), W_EPS,
                                       ALU.mult, ALU.max))
                dve.reciprocal(inv[:, wi:wi + 1], k.small[:, wi:wi + 1]).then_inc(inv_ready, 1)
            for wi in range(2):
                dve.wait_ge(scaled, wi + 1)
                link(dve.tensor_scalar(raw[wi][:, :], raw[wi][:, :], ROUND - 1.0, ROUND + 1.0, ALU.max, ALU.min))
                dve.tensor_scalar(tern[wi][:, :], raw[wi][:, :], ROUND, None, ALU.subtract).then_inc(rounded, 1)
                for n in range(wi * GROUPS, (wi + 1) * GROUPS, 2):
                    dve.wait_ge(transposed, n + 1)
                    dst = (k.w1T, k.w2T)[wi]
                    dve.tensor_copy(dst[:, n % GROUPS * HALF:(n % GROUPS + 1) * HALF], ps_t[n % 4][:, :])\
                       .then_inc(copied_even, 1)


def stage_transposes(k, ctxT, qT):
    nc = k.nc
    with ExitStack() as ctx:
        sb = lambda name, shape, dt: ctx.enter_context(nc.sbuf_tensor(name, shape, dt))
        c_in = [sb(f"c_in{i}", [P, D], F32) for i in range(4)]
        xn = [sb(f"xn{i}", [P, D], F32) for i in range(4)]
        stats = sb("t_stats", [P, NT, 6], F32)
        mean = sb("t_mean", [P, NT], F32)
        var = sb("t_var", [P, NT], F32)
        diff = sb("t_diff", [P, NT], F32)
        rstd = sb("t_rstd", [P, NT], F32)
        ps = [ctx.enter_context(nc.psum_tensor(f"ps_tr{i}", [P, D], F32)) for i in range(4)]
        sem = k.semaphore
        x_loaded = [sem(f"t_x{i}") for i in range(4)]
        c_loaded = [sem(f"t_c{i}") for i in range(4)]
        c_used, transposed, evacuated = sem("t_cused"), sem("t_transposed"), sem("t_evac")
        var_ready, rstd_ready, xn_ready, xn_used, dve_step = sem("t_var"), sem("t_rstd"), sem("t_xn"), sem("t_xnused"), sem("t_dve")
        block = ctx.enter_context(nc.Block())
        c_dram = k.ins["ctx_2048"].rearrange("b s d -> (b s) d")
        x_dram = k.ins["x"].rearrange("b s d -> (b s) d").rearrange("(t p) d -> p t d", p=P)

        @block.sync
        def _(sp):
            for i in range(4):
                sp.dma_start(k.x[:, 4 * i:4 * i + 4, :], x_dram[:, 4 * i:4 * i + 4, :]).then_inc(x_loaded[i], 16)
            with sp.Fori(0, NT // 4) as i:
                for j in range(4):
                    sp.wait_ge(c_used, i * 4 + (j + 1))
                    sp.dma_start(c_in[j][:, :], c_dram[bass.ds(i * (4 * P) + j * P, P), :]).then_inc(c_loaded[j], 16)

        @block.tensor
        def _(pe):
            pe.sem_inc(c_used, 4)
            pe.sem_inc(xn_used, 4)
            with pe.Fori(0, NT // 4) as i:
                for j in range(4):
                    pe.wait_ge(c_loaded[j], i * 16 + 16)
                    pe.wait_ge(evacuated, i * 4 + (j + 1))
                    for c in range(DC):
                        last = pe.transpose(ps[j][:, c * P:(c + 1) * P], c_in[j][:, c * P:(c + 1) * P], k.ident[:, :])
                    last.then_inc(transposed, 1)
                    pe.wait_ge(transposed, i * 4 + (j + 1))
                    pe.sem_inc(c_used, 1)
            with pe.Fori(0, NT // 4) as i:
                for j in range(4):
                    pe.wait_ge(xn_ready, i * 4 + (j + 1))
                    pe.wait_ge(evacuated, i * 4 + (NT + j + 1))
                    for c in range(DC):
                        last = pe.transpose(ps[j][:, c * P:(c + 1) * P], xn[j][:, (DC - 1 - c) * P:(DC - c) * P], k.ident[:, :])
                    last.then_inc(transposed, 1)

        @block.scalar
        def _(act):
            act.sem_inc(evacuated, 4)
            for n, dst in enumerate((ctxT, qT)):
                with act.Fori(0, NT // 4) as i:
                    for j in range(4):
                        act.wait_ge(transposed, i * 4 + (NT * n + j + 1))
                        act.activation(dst[:, :, bass.ds(i * (4 * P) + j * P, P)],
                                       ps[j][:, :].rearrange("p (c t) -> p c t", c=DC), ACT.Copy).then_inc(evacuated, 1)

        @block.vector
        def _(dve):
            link = Link(dve, dve_step)
            for i in range(4):
                dve.wait_ge(x_loaded[i], 16)
                for t in range(4 * i, 4 * i + 4):
                    link(dve.bn_stats(stats[:, t, :], k.x[:, t, :]), wait=False)
            dve.wait_ge(dve_step, NT)
            link(dve.tensor_tensor(mean[:, :], stats[:, :, 1], stats[:, :, 4], ALU.add))
            link(dve.tensor_scalar(mean[:, :], mean[:, :], 0.5, None, ALU.mult))
            link(dve.tensor_tensor(diff[:, :], stats[:, :, 1], stats[:, :, 4], ALU.subtract))
            link(dve.tensor_tensor(diff[:, :], diff[:, :], diff[:, :], ALU.mult))
            link(dve.tensor_tensor(var[:, :], stats[:, :, 2], stats[:, :, 5], ALU.add))
            link(dve.tensor_scalar(var[:, :], var[:, :], 1.0 / D, LN_EPS, ALU.mult, ALU.add))
            link(dve.scalar_tensor_tensor(var[:, :], diff[:, :], 0.25, var[:, :], ALU.mult, ALU.add))
            dve.sem_inc(var_ready, 1)
            dve.wait_ge(rstd_ready, 1)
            with dve.Fori(0, NT // 4) as i:
                for j in range(4):
                    dve.wait_ge(transposed, i * 4 + (NT + j - 3))
                    t = bass.ds(i * 4 + j, 1)
                    dve.tensor_scalar(xn[j][:, ::-1], k.x[:, t, :], mean[:, t], rstd[:, t], ALU.subtract, ALU.mult)\
                       .then_inc(xn_ready, 1)

        @block.gpsimd
        def _(pool):
            pool.wait_ge(var_ready, 1)
            pool.tensor_tensor(rstd[:, :], var[:, :], k.pow_half[:, :], ALU.pow).then_inc(rstd_ready, 1)


def stage_long_conv(k, ctxT, qT, outT):
    nc = k.nc
    BP = B * PAIRS
    with ExitStack() as ctx:
        sb = lambda name, shape, dt: ctx.enter_context(nc.sbuf_tensor(name, shape, dt))
        toep = [sb(f"toep{i}", [P, D], F32) for i in range(2)]
        kv = [sb(f"kv{i}", [P, DC, B, PAIRS], F32) for i in range(2)]
        prod = [sb(f"prod{i}", [P, DC, B, HD0, HD0], F32) for i in range(2)]
        Y = [ctx.enter_context(nc.psum_tensor(f"ps_y{i}", [P, DC, 512], F32)) for i in range(2)]
        sem = k.semaphore
        toep_loaded = [sem("a_toep0"), sem("a_toep1")]
        kv_ready, conv_done, y_read, prod_ready, reduced = (sem(f"a_{n}") for n in ("kv", "conv", "yread", "prod", "red"))
        block = ctx.enter_context(nc.Block())
        taps = k.scratch["taps"]
        ctx4 = ctxT[:, :, :].rearrange("p c (b s) -> p c b s", b=B)
        q4 = qT[:, :, :].rearrange("p c (b s) -> p c b s", b=B)
        o4 = outT[:, :, :].rearrange("p c (b s) -> p c b s", b=B)

        @block.sync
        def _(sp):
            with sp.Fori(0, H0 // 2) as i:
                for p in range(2):
                    sp.wait_ge(conv_done, i * 2 + (p + 1))
                    row = taps[bass.ds(i * 2 + p, 1), 0:D]
                    src = bass.AP(tensor=row.tensor, offset=row.offset, ap=[[1, P], [1, D]])
                    sp.dma_start(toep[p][:, :], src).then_inc(toep_loaded[p], 16)

        @block.gpsimd
        def _(pool):
            with pool.Fori(0, H0 // 2) as i:
                for p in range(2):
                    pool.wait_ge(conv_done, i * 2 + (p + 1))
                    for c in range(HD0):
                        n = HD0 - c
                        at = i * (2 * HD0) + (p * HD0 + c)
                        last = pool.tensor_tensor(kv[p][:, :, :, pair_at(c):pair_at(c) + n],
                                                  ctx4[:, :, :, bass.ds(at, 1)].broadcast_to([P, DC, B, n]),
                                                  ctx4[:, :, :, bass.ds(at, n)], ALU.mult)
                    last.then_inc(kv_ready, 1)

        @block.tensor
        def _(pe):
            pe.sem_inc(conv_done, 2)
            with pe.Fori(0, H0 // 2) as i:
                for p in range(2):
                    pe.wait_ge(toep_loaded[p], i * 16 + 16)
                    pe.wait_ge(kv_ready, i * 2 + (p + 1))
                    pe.wait_ge(y_read, i * 2 + (p + 1))
                    for l in range(DC):
                        for m in range(l + 1):
                            last = pe.matmul(Y[p][:, l, 0:BP], toep[p][:, (DC - 1 - l + m) * P:(DC - l + m) * P],
                                             kv[p][:, m, :, :].rearrange("p b n -> p (b n)"),
                                             start=(m == 0), stop=(m == l))
                    last.then_inc(conv_done, 1)

        @block.vector
        def _(dve):
            dve.sem_inc(y_read, 2)
            with dve.Fori(0, H0 // 2) as i:
                for p in range(2):
                    dve.wait_ge(conv_done, i * 2 + (p + 3))
                    y = Y[p][:, :, 0:BP].rearrange("p c (b n) -> p c b n", b=B)
                    for c in range(HD0):
                        n = HD0 - c
                        at = i * (2 * HD0) + (p * HD0 + c)
                        dve.tensor_tensor(prod[p][:, :, :, c:, c], y[:, :, :, pair_at(c):pair_at(c) + n],
                                          q4[:, :, :, bass.ds(at, 1)].broadcast_to([P, DC, B, n]), ALU.mult)\
                           .then_inc(prod_ready, 1)
                        if n > 1:
                            last = dve.tensor_tensor(prod[p][:, :, :, c, c + 1:],
                                                     y[:, :, :, pair_at(c) + 1:pair_at(c) + n],
                                                     q4[:, :, :, bass.ds(at + 1, n - 1)], ALU.mult)
                            last.then_inc(prod_ready, 1)
                    per = 2 * HD0 - 1
                    dve.wait_ge(prod_ready, i * (2 * per) + (p + 1) * per)
                    dve.sem_inc(y_read, 1)
                    dve.tensor_reduce(o4[:, :, :, bass.ds(i * (2 * HD0) + p * HD0, HD0)], prod[p][:, :, :, :, :],
                                      AX.X, ALU.add).then_inc(reduced, 1)


def mean_var(link, dve, stats, mean, var, tmp, eps):
    link(dve.tensor_tensor(mean, stats[:, :, 1], stats[:, :, 4], ALU.add))
    link(dve.tensor_scalar(mean, mean, 0.5, None, ALU.mult))
    link(dve.tensor_tensor(tmp, stats[:, :, 1], stats[:, :, 4], ALU.subtract))
    link(dve.tensor_tensor(tmp, tmp, tmp, ALU.mult))
    link(dve.tensor_tensor(var, stats[:, :, 2], stats[:, :, 5], ALU.add))
    link(dve.tensor_scalar(var, var, 1.0 / D, eps, ALU.mult, ALU.add))
    link(dve.scalar_tensor_tensor(var, tmp, 0.25, var, ALU.mult, ALU.add))


def stage_ffn_entry(k, outT, mean, quant, dequant):
    nc = k.nc
    with ExitStack() as ctx:
        sb = lambda name, shape, dt: ctx.enter_context(nc.sbuf_tensor(name, shape, dt))
        part = [sb(f"e_part{i}", [P, DC, P], F32) for i in range(4)]
        stats = sb("e_stats", [P, NT, 6], F32)
        hi, lo, var, tmp, r1, r2 = (sb(f"e_{n}", [P, NT], F32) for n in ("hi", "lo", "var", "tmp", "r1", "r2"))
        ps = [ctx.enter_context(nc.psum_tensor(f"ps_e{i}", [P, D], F32)) for i in range(4)]
        sem = k.semaphore
        staged, transposed, added, seen, dve_step, var_ready, r_ready = (
            sem(f"e_{n}") for n in ("staged", "transposed", "added", "seen", "dve", "varr", "rr"))
        block = ctx.enter_context(nc.Block())

        @block.gpsimd
        def _(pool):
            with pool.Fori(0, NT // 4) as i:
                for j in range(4):
                    pool.wait_ge(transposed, i * 4 + (j + 1))
                    pool.tensor_copy(part[j][:, :, :], outT[:, :, bass.ds(i * (4 * P) + j * P, P)]).then_inc(staged, 1)
            for n, r in enumerate((r1, r2)):
                pool.wait_ge(var_ready, n + 1)
                pool.tensor_tensor(r[:, :], var[:, :], k.pow_half[:, :], ALU.pow).then_inc(r_ready, 1)

        @block.tensor
        def _(pe):
            pe.sem_inc(transposed, 4)
            with pe.Fori(0, NT // 4) as i:
                for j in range(4):
                    pe.wait_ge(staged, i * 4 + (j + 1))
                    pe.wait_ge(added, i * 4 + (j + 1))
                    for c in range(DC):
                        last = pe.matmul(ps[j][:, c * P:(c + 1) * P], part[j][:, c, :], k.reverse[:, :], start=True, stop=True)
                    last.then_inc(transposed, 1)

        @block.vector
        def _(dve):
            link = Link(dve, dve_step)
            dve.sem_inc(added, 4)
            with dve.Fori(0, NT // 4) as i:
                for j in range(4):
                    t = bass.ds(i * 4 + j, 1)
                    dve.wait_ge(transposed, i * 4 + (j + 5))
                    dve.tensor_tensor(k.x[:, t, :], k.x[:, t, :], ps[j][:, :].unsqueeze(1), ALU.add).then_inc(added, 1)
                    dve.wait_ge(added, i * 4 + (j + 5))
                    dve.bn_stats(stats[:, t, :], k.x[:, t, :]).then_inc(seen, 1)
                    dve.tensor_reduce(hi[:, t], k.x[:, t, :], AX.X, ALU.max).then_inc(seen, 1)
                    dve.tensor_reduce(lo[:, t], k.x[:, t, :], AX.X, ALU.min).then_inc(seen, 1)
            dve.wait_ge(seen, 3 * NT)
            mean_var(link, dve, stats, mean[:, :], var[:, :], tmp[:, :], LN_EPS)
            dve.sem_inc(var_ready, 1)
            link(dve.tensor_tensor(hi[:, :], hi[:, :], mean[:, :], ALU.subtract))
            link(dve.tensor_tensor(lo[:, :], mean[:, :], lo[:, :], ALU.subtract))
            link(dve.tensor_tensor(hi[:, :], hi[:, :], lo[:, :], ALU.max))
            dve.wait_ge(r_ready, 1)
            link(dve.tensor_scalar(tmp[:, :], var[:, :], LN_EPS, None, ALU.subtract))
            link(dve.tensor_tensor(tmp[:, :], tmp[:, :], r1[:, :], ALU.mult))
            link(dve.tensor_tensor(tmp[:, :], tmp[:, :], r1[:, :], ALU.mult))
            link(dve.tensor_scalar(var[:, :], tmp[:, :], LN_EPS, None, ALU.add))
            dve.sem_inc(var_ready, 1)
            dve.wait_ge(r_ready, 2)
            link(dve.tensor_tensor(r1[:, :], r1[:, :], r2[:, :], ALU.mult))
            link(dve.tensor_tensor(hi[:, :], hi[:, :], r1[:, :], ALU.mult))
            link(dve.tensor_scalar(hi[:, :], hi[:, :], ACT_EPS, None, ALU.max))
            link(dve.reciprocal(tmp[:, :], hi[:, :]))
            link(dve.tensor_tensor(tmp[:, :], tmp[:, :], r1[:, :], ALU.mult))
            link(dve.tensor_scalar(quant[:, :], tmp[:, :], 127.0, None, ALU.mult))
            link(dve.tensor_scalar(dequant[:, :], hi[:, :], 1.0 / 127.0, k.small[:, 0:1], ALU.mult, ALU.mult))


def stage_ffn(k, mean, quant, dequant):
    nc = k.nc
    with ExitStack() as ctx:
        sb = lambda name, shape, dt: ctx.enter_context(nc.sbuf_tensor(name, shape, dt))
        b1 = sb("f_b1", [P, FF], F32)
        b2 = sb("f_b2", [P, D], F32)
        scaled = [sb(f"f_scaled{i}", [P, D], F32) for i in range(2)]
        qa = [sb(f"f_qa{i}", [P, D], BF16) for i in range(2)]
        qaT = [sb(f"f_qaT{i}", [P, DC, P], BF16) for i in range(2)]
        h = [sb(f"f_h{i}", [P, FF], F32) for i in range(2)]
        qb = [sb(f"f_qb{i}", [P, FF], BF16) for i in range(2)]
        qbT = [sb(f"f_qbT{i}", [P, FC, P], BF16) for i in range(2)]
        stats = [sb(f"f_stats{i}", [P, DC, 6], F32) for i in range(2)]
        mv = [sb(f"f_mv{i}", [P, 2], F32) for i in range(2)]
        NEG_MEAN, VAR, RSTD, AMAX, INV, QUANT, DEQUANT = range(7)
        sc = [sb(f"f_sc{i}", [P, 7], F32) for i in range(2)]
        col = lambda p, c: sc[p][:, c:c + 1]
        psT = ctx.enter_context(nc.psum_tensor("ps_fT", [P, DC, P], BF16))
        psH = [ctx.enter_context(nc.psum_tensor(f"ps_fH{i}", [P, 512], F32)) for i in range(DC)]
        psQ = [ctx.enter_context(nc.psum_tensor(f"ps_fQ{i}", [P, 8, P], BF16)) for i in range(2)]
        psY = ctx.enter_context(nc.psum_tensor("ps_fY", [P, D], F32))
        sem = lambda name: k.semaphore(("f_" + name))
        b_loaded, dve_step, aggregate_turn, zeros_set, zeroed = (sem(n) for n in ("bload", "dve", "aggr", "zs", "zd"))
        zeros = sb("f_zeros", [P, 2 * D], F32)
        qa_ready, qaT_psum, qaT_ready, h_psum, hb_ready, gelu_done = (
            sem(n) for n in ("qa", "qaTp", "qaT", "hp", "hb", "gelu"))
        stat_ready, rstd_ready, centred, quant_ready, h_scaled, qb_ready = (
            sem(n) for n in ("stat", "rstd", "cent", "quant", "hsc", "qb"))
        qbT_psum, qbT_ready, y_psum, y_added, biased = (sem(n) for n in ("qbTp", "qbT", "yp", "ya", "biased"))
        block = ctx.enter_context(nc.Block())
        tile = lambda t: k.x[:, bass.ds(t, 1), :]
        one = lambda a, t: a[:, bass.ds(t, 1)]

        known = lambda n: isinstance(n, int)
        runs = lambda n, ahead: not known(n) or 0 <= n + ahead < NT

        @block.sync
        def _(sp):
            for dst, name, n in ((b1, "L0_ffn_b1", FF), (b2, "L0_ffn_b2", D)):
                src = k.ins[name]
                sp.dma_start(dst[:, :], bass.AP(tensor=src.tensor, offset=0, ap=[[0, P], [1, n]])).then_inc(b_loaded, 16)
            sp.wait_ge(zeros_set, 1)
            rows = k.scratch["rows"].rearrange("(j p) d -> j p d", p=2 * P)
            with sp.Fori(0, NBLK * BLK // (2 * P)) as i:
                sp.dma_start(rows[bass.ds(i, 1), :, :].rearrange("o (p s) d -> (o p) (s d)", s=2), zeros[:, :]).then_inc(zeroed, 16)
            sp.wait_ge(zeroed, 16 * (NBLK * BLK // (2 * P)))

        @block.vector
        def _(dve):
            link = Link(dve, dve_step)
            dve.wait_ge(b_loaded, 32)

            def quantise_x(t, p):
                link(dve.tensor_scalar(scaled[p][:, :], tile(t), one(mean, t), one(quant, t), ALU.subtract, ALU.mult))
                dve.tensor_scalar(qa[p][:, :], scaled[p][:, :], ROUND, ROUND, ALU.add, ALU.subtract).then_inc(qa_ready, 1)

            def add_bias1(t, p):
                dve.wait_ge(h_psum, t + 1)
                for c in range(DC):
                    dve.scalar_tensor_tensor(h[p][:, c * 512:(c + 1) * 512], psH[c][:, :], one(dequant, t),
                                             b1[:, c * 512:(c + 1) * 512], ALU.mult, ALU.add).then_inc(hb_ready, 1)

            def statistics(t, p):
                dve.wait_ge(gelu_done, t + 1)
                for c in range(DC):
                    link(dve.bn_stats(stats[p][:, c, :], h[p][:, c * 512:(c + 1) * 512]), wait=c == DC - 1)
                dve.sem_inc(aggregate_turn, 1)
                link(dve.bn_aggr(mv[p][:, :], stats[p][:, :, :]))
                dve.tensor_scalar(col(p, NEG_MEAN), mv[p][:, 0:1], -1.0, None, ALU.mult).then_inc(stat_ready, 1)
                dve.tensor_scalar(col(p, VAR), mv[p][:, 1:2], LN_EPS, None, ALU.add).then_inc(stat_ready, 1)

            def scale_of(t, p):
                dve.wait_ge(centred, t + 1)
                link(dve.tensor_reduce(col(p, AMAX), h[p][:, :], AX.X, ALU.max, apply_absolute_value=True))
                dve.wait_ge(rstd_ready, t + 1)
                link(dve.tensor_scalar(col(p, AMAX), col(p, AMAX), col(p, RSTD), ACT_EPS, ALU.mult, ALU.max))
                link(dve.reciprocal(col(p, INV), col(p, AMAX)))
                dve.tensor_scalar(col(p, QUANT), col(p, INV), 127.0, col(p, RSTD), ALU.mult, ALU.mult).then_inc(quant_ready, 1)
                link(dve.tensor_scalar(col(p, DEQUANT), col(p, AMAX), 1.0 / 127.0, k.small[:, 1:2], ALU.mult, ALU.mult), wait=False)

            def round_h(t, p):
                dve.wait_ge(h_scaled, t + 1)
                dve.tensor_scalar(qb[p][:, :], h[p][:, :], ROUND, None, ALU.subtract).then_inc(qb_ready, 1)

            def add_y(t, p):
                dve.wait_ge(y_psum, t + 1)
                dve.wait_ge(biased, t + 1)
                dve.scalar_tensor_tensor(tile(t), psY[:, :].unsqueeze(1), col(p, DEQUANT), tile(t), ALU.mult, ALU.add)\
                   .then_inc(y_added, 1)

            def step(n, p):
                if runs(n, -2):
                    add_y(n - 2, p)
                if runs(n, 0):
                    add_bias1(n, p)
                if known(n) and n + 1 < NT:
                    quantise_x(n + 1, 1 - p)
                elif not known(n):
                    quantise_x(n + 1, 1 - p)
                if runs(n, -1):
                    scale_of(n - 1, 1 - p)
                if runs(n, 0):
                    statistics(n, p)
                if runs(n, -1):
                    round_h(n - 1, 1 - p)

            quantise_x(0, 0)
            step(0, 0)
            step(1, 1)
            with link.loop((NT - 4) // 2, 20) as i:
                for p in range(2):
                    step(i * 2 + (p + 2), p)
            for n in range(NT - 2, NT + 2):
                step(n, n % 2)

        @block.scalar
        def _(act):
            def copy_qaT(t, p):
                act.wait_ge(qaT_psum, t + 1)
                act.activation(qaT[p][:, :, :], psT[:, :, :], ACT.Copy).then_inc(qaT_ready, 1)

            def gelu(t, p):
                act.wait_ge(hb_ready, t * 4 + 4)
                act.activation(h[p][:, :], h[p][:, :], ACT.Gelu).then_inc(gelu_done, 1)

            def centre(t, p):
                act.wait_ge(stat_ready, t * 2 + 2)
                act.activation(h[p][:, :], h[p][:, :], ACT.Identity, bias=col(p, NEG_MEAN)).then_inc(centred, 1)

            def scale(t, p):
                act.wait_ge(quant_ready, t + 1)
                act.activation(h[p][:, :], h[p][:, :], ACT.Identity, bias=k.small[:, 2:3],
                               scale=col(p, QUANT)).then_inc(h_scaled, 1)

            def copy_qbT(t, p):
                for g in range(2):
                    act.wait_ge(qbT_psum, t * 2 + (g + 1))
                    act.activation(qbT[p][:, 8 * g:8 * g + 8, :], psQ[g][:, :, :], ACT.Copy).then_inc(qbT_ready, 1)

            def step(n, p):
                if runs(n, 0):
                    gelu(n, p)
                if runs(n, 1):
                    copy_qaT(n + 1, 1 - p)
                if runs(n, -1):
                    scale(n - 1, 1 - p)
                if runs(n, 0):
                    centre(n, p)
                if runs(n, -1):
                    copy_qbT(n - 1, 1 - p)

            copy_qaT(0, 0)
            step(0, 0)
            step(1, 1)
            with act.Fori(0, (NT - 4) // 2) as i:
                for p in range(2):
                    step(i * 2 + (p + 2), p)
            for n in range(NT - 2, NT + 1):
                step(n, n % 2)

        @block.gpsimd
        def _(pool):
            pool.memset(zeros[:, :], 0.0).then_inc(zeros_set, 1)
            pool.wait_ge(b_loaded, 32)

            def step(t, p):
                pool.wait_ge(qa_ready, t + 1)
                pool.tensor_tensor(tile(t), tile(t), b2[:, :].unsqueeze(1), ALU.add).then_inc(biased, 1)
                pool.wait_ge(stat_ready, t * 2 + 2)
                pool.tensor_tensor(col(p, RSTD), col(p, VAR), k.pow_half[:, 0:1], ALU.pow).then_inc(rstd_ready, 1)

            with pool.Fori(0, NT // 2) as i:
                for p in range(2):
                    step(i * 2 + p, p)

        @block.tensor
        def _(pe):
            def transpose_qa(t, p):
                pe.wait_ge(qa_ready, t + 1)
                if not known(t) or t:
                    pe.wait_ge(qaT_ready, t)
                for c in range(DC):
                    last = pe.transpose(psT[:, c, :], qa[p][:, c * P:(c + 1) * P], k.ident_b[:, :])
                last.then_inc(qaT_psum, 1)

            def up(t, p):
                pe.wait_ge(qaT_ready, t + 1)
                if not known(t) or t:
                    pe.wait_ge(hb_ready, t * 4)
                for f in range(DC):
                    for c in range(DC):
                        last = pe.matmul(psH[f][:, :], qaT[p][:, c, :], k.w1T[:, c * FF + f * 512:c * FF + (f + 1) * 512],
                                         start=(c == 0), stop=(c == DC - 1))
                last.then_inc(h_psum, 1)

            def transpose_qb(t, p):
                pe.wait_ge(qb_ready, t + 1)
                for g in range(2):
                    if not known(t) or t:
                        pe.wait_ge(qbT_ready, t * 2 + (g - 1))
                    for c in range(8):
                        last = pe.transpose(psQ[g][:, c, :], qb[p][:, (8 * g + c) * P:(8 * g + c + 1) * P], k.ident_b[:, :])
                    last.then_inc(qbT_psum, 1)

            def down(t, p):
                pe.wait_ge(qbT_ready, t * 2 + 2)
                if not known(t) or t:
                    pe.wait_ge(y_added, t)
                for c in range(FC):
                    last = pe.matmul(psY[:, :], qbT[p][:, c, :], k.w2T[:, c * D:(c + 1) * D],
                                     start=(c == 0), stop=(c == FC - 1))
                last.then_inc(y_psum, 1)

            def step(n, p):
                if runs(n, 1):
                    transpose_qa(n + 1, 1 - p)
                    up(n + 1, 1 - p)
                if runs(n, -1):
                    transpose_qb(n - 1, 1 - p)
                    down(n - 1, 1 - p)

            transpose_qa(0, 0)
            up(0, 0)
            step(0, 0)
            step(1, 1)
            with pe.Fori(0, (NT - 4) // 2) as i:
                for p in range(2):
                    step(i * 2 + (p + 2), p)
            for n in range(NT - 2, NT + 1):
                step(n, n % 2)


RMS_EPS = 1e-6
HEADS, HD = 16, 32
HC = P // HD
UNITS = HEADS // 2
VC = HD + 1
ROWS = {"bq": 0, "gq": 4, "bk": 8, "gk": 12, "sgb": 16, "sb1": 20}
SCORE_SCALE = float(HD) ** -0.5


def broadcast_rows(src, n):
    return bass.AP(tensor=src.tensor, offset=0, ap=[[0, P], [1, n]])


def known(n):
    return isinstance(n, int)


def three_products(pe, out, stationary, moving, first=True, last=True):
    for n, (a, b) in enumerate(((0, 0), (0, 1), (1, 0))):
        instruction = pe.matmul(out, stationary[a], moving[b], start=first and n == 0, stop=last and n == 2)
    return instruction


def stage_attention_weights(k, split, vectors, vbias, x_mean, x_rstd, sel):
    nc = k.nc
    names = ("L1_xattn_Wk_img", "L1_xattn_Wv_img", "L1_xattn_Wq", "L1_xattn_Wo")
    with ExitStack() as ctx:
        sb = lambda name, shape, dt: ctx.enter_context(nc.sbuf_tensor(name, shape, dt))
        raw = [sb(f"aw_raw{i}", [P, DC, D], F32) for i in range(2)]
        rows = sb("aw_rows", [P, P], F32)
        stats = sb("aw_stats", [P, NT, 6], F32)
        var, tmp = (sb(f"aw_{n}", [P, NT], F32) for n in ("var", "tmp"))
        ps = ctx.enter_context(nc.psum_tensor("ps_aw", [P, P], F32))
        sem = lambda name: k.semaphore(("w2_" + name))
        loaded = [sem("load0"), sem("load1")]
        high_ready, low_ready, rows_zeroed, rows_loaded, rows_turned, dve_step, b_loaded = (
            sem(n) for n in ("high", "low", "rz", "rl", "rt", "dve", "bl"))
        stat_done, var_ready, sel_set = (sem(n) for n in ("stat", "var", "sel"))
        block = ctx.enter_context(nc.Block())

        @block.sync
        def _(sp):
            for n, name in enumerate(names):
                if n >= 2:
                    sp.wait_ge(low_ready, n - 1)
                sp.dma_start(raw[n % 2][:, :, :], k.ins[name].rearrange("(c p) n -> p c n", p=P)).then_inc(loaded[n % 2], 16)
            sp.dma_start(vbias[:, :], broadcast_rows(k.ins["L1_xattn_bv_img"], D)).then_inc(b_loaded, 16)
            sp.wait_ge(rows_zeroed, 1)
            for at, name in (("bq", "L1_xattn_bq"), ("gq", "L1_xattn_gq"), ("bk", "L1_xattn_bk_img"), ("gk", "L1_xattn_gk_img")):
                sp.dma_start(rows[ROWS[at]:ROWS[at] + DC, :], k.ins[name].rearrange("(c p) -> c p", p=P)).then_inc(rows_loaded, 16)
            for at, name in (("sgb", "L1_ffn_sgb"), ("sb1", "L1_ffn_sb1")):
                for e in range(2):
                    at_e = ROWS[at] + 2 * e
                    sp.dma_start(rows[at_e:at_e + 2, :], k.ins[name][e, :].rearrange("(c p) -> c p", p=P)).then_inc(rows_loaded, 16)
            sp.wait_ge(b_loaded, 16)

        @block.gpsimd
        def _(pool):
            pool.memset(rows[:, :], 0.0).then_inc(rows_zeroed, 1)
            pool.memset(sel[:, :, :], 1.0).then_inc(sel_set, 1)
            for j in range(2):
                pool.wait_ge(sel_set, 1 + 2 * j)
                pool.affine_select(out=sel[:, j, :], in_=sel[:, j, :], compare_op=ALU.is_ge, fill=0.0,
                                   base=-2 * j, pattern=[[0, P]], channel_multiplier=1).then_inc(sel_set, 1)
                pool.wait_ge(sel_set, 2 + 2 * j)
                pool.affine_select(out=sel[:, j, :], in_=sel[:, j, :], compare_op=ALU.is_ge, fill=0.0,
                                   base=2 * j + 1, pattern=[[0, P]], channel_multiplier=-1).then_inc(sel_set, 1)
            pool.wait_ge(var_ready, 1)
            pool.tensor_tensor(x_rstd[:, :], var[:, :], k.pow_half[:, :], ALU.pow)

        @block.scalar
        def _(act):
            for n in range(4):
                act.wait_ge(loaded[n % 2], 16 * (n // 2 + 1))
                act.activation(split[n][:, 0, :, :], raw[n % 2][:, :, :], ACT.Copy).then_inc(high_ready, 1)

        @block.tensor
        def _(pe):
            pe.wait_ge(rows_loaded, 16 * 8)
            pe.transpose(ps[:, :], rows[:, :], k.ident[:, :]).then_inc(rows_turned, 1)

        @block.vector
        def _(dve):
            link = Link(dve, dve_step)
            for t in range(NT):
                dve.bn_stats(stats[:, t, :], k.x[:, t, :]).then_inc(stat_done, 1)
            dve.wait_ge(stat_done, NT)
            mean_var(link, dve, stats, x_mean[:, :], var[:, :], tmp[:, :], LN_EPS)
            dve.sem_inc(var_ready, 1)
            for n in range(4):
                dve.wait_ge(high_ready, n + 1)
                dve.tensor_tensor(split[n][:, 1, :, :], raw[n % 2][:, :, :], split[n][:, 0, :, :], ALU.subtract).then_inc(low_ready, 1)
            dve.wait_ge(rows_turned, 1)
            dve.tensor_copy(vectors[:, :], ps[:, 0:vectors.shape[1]])


def refine_rms(dve, link, r, v, t):
    link(dve.scalar_tensor_tensor(t[:, :], r[:, :], -0.5, r[:, :], ALU.mult, ALU.mult))
    link(dve.tensor_tensor(t[:, :], t[:, :], v[:, :], ALU.mult))
    link(dve.scalar_tensor_tensor(r[:, :], t[:, :], 1.5, r[:, :], ALU.add, ALU.mult))


def stack_heads(sp, dst, high, low, order, done):
    for j, part in enumerate(order):
        src = (high, low)[part]
        for hm in range(HC):
            sp.dma_start(dst(slice(j * HD, (j + 1) * HD), hm), src[hm * HD:(hm + 1) * HD, :, :]).then_inc(done, 16)


STACK_INCS = 16 * HC * 4


def stage_keys_values(k, ctxT, kw, vw, vectors, vbias, ks, v_hi, v_lo):
    nc = k.nc
    with ExitStack() as ctx:
        sb = lambda name, shape, dt: ctx.enter_context(nc.sbuf_tensor(name, shape, dt))
        c_hi = [sb(f"kv_chi{i}", [P, DC, S], BF16) for i in range(2)]
        c_lo = [sb(f"kv_clo{i}", [P, DC, S], BF16) for i in range(2)]
        u = sb("kv_u", [P, DC, S], F32)
        sq = sb("kv_sq", [P, DC, S], F32)
        ln, r, v, tmp = (sb(f"kv_{n}", [P, S], F32) for n in ("ln", "r", "v", "t"))
        kn = sb("kv_kn", [P, DC, S], F32)
        k_hi = [sb(f"kv_khi{i}", [P, DC, S], BF16) for i in range(2)]
        k_lo = [sb(f"kv_klo{i}", [P, DC, S], BF16) for i in range(2)]
        vf = [sb(f"kv_vf{i}", [P, D], F32) for i in range(2)]
        psK = [ctx.enter_context(nc.psum_tensor(f"ps_k{i}", [P, 2, S], F32)) for i in range(2)]
        psV = [ctx.enter_context(nc.psum_tensor(f"ps_v{i}", [P, D], F32)) for i in range(2)]
        psR = ctx.enter_context(nc.psum_tensor("ps_r", [P, S], F32))
        sem = lambda name: k.semaphore(("k_" + name))
        ones_set, c_high, c_low, k_psum, v_psum, squared, r_psum, act_step, r_rough = (
            sem(n) for n in ("ones", "ch", "cl", "kp", "vp", "sq", "rp", "act", "rough"))
        normed, k_high, k_low, v_full, v_high, v_low, dve_step = (
            sem(n) for n in ("norm", "kh", "kl", "vf", "vh", "vl", "dve"))
        stacked = [sem("st0"), sem("st1")]
        block = ctx.enter_context(nc.Block())
        at = lambda b: bass.ds(b * S, S)
        heads = lambda a: a.rearrange("p (o h d) -> p o h d", o=1, d=HD)
        vtile = lambda a, b, t: a[:, bass.ds(b * 2 + t, 1), :, 0:HD]

        def stack_count(b, p):
            return b * (STACK_INCS // 2) - p * (STACK_INCS // 2)

        def batches(engine, step, link=None, per=0):
            for b in range(2):
                step(b, b)
            with (link.loop((B - 4) // 2, per) if link else engine.Fori(0, (B - 4) // 2)) as i:
                for p in range(2):
                    step(i * 2 + (p + 2), p)
            for b in range(B - 2, B):
                step(b, b % 2)

        @block.gpsimd
        def _(pool):
            pool.memset(v_hi[:, :, :, HD:], 1.0)
            pool.memset(v_lo[:, :, :, HD:], 0.0)

        @block.sync
        def _(sp):
            def step(b, p):
                sp.wait_ge(k_low, b + 1)
                stack_heads(sp, lambda rows, hm: ks[bass.ds(b, 1), rows, hm, :, :].rearrange("o p c s -> (o p) c s"), k_hi[p], k_lo[p], (0, 1, 0, 1), stacked[p])

            batches(sp, step)
            for p in range(2):
                sp.wait_ge(stacked[p], B // 2 * STACK_INCS)

        @block.scalar
        def _(act):
            link = Link(act, act_step)

            def split_context(b, p):
                act.activation(c_hi[p][:, :, :], ctxT[:, :, at(b)], ACT.Copy).then_inc(c_high, 1)

            def step(b, p):
                act.wait_ge(k_psum, b + 1)
                if not known(b) or b:
                    act.wait_ge(normed, b * DC)
                for c in range(DC):
                    bias = vectors[:, ROWS["bk"] + c:ROWS["bk"] + c + 1]
                    act.activation(u[:, c, :], psK[c // 2][:, c % 2, :], ACT.Identity, bias=bias).then_inc(squared, 1)
                    act.activation(sq[:, c, :], psK[c // 2][:, c % 2, :], ACT.Square, bias=bias).then_inc(squared, 1)
                for t in range(2):
                    act.wait_ge(v_full, b * 2 + (t + 1))
                    act.activation(vtile(v_hi, b, t), heads(vf[t][:, :]), ACT.Copy).then_inc(v_high, 1)
                if not known(b) or b + 2 < B:
                    act.wait_ge(v_psum, b * 2 + 2)
                    split_context(b + 2, p)
                act.wait_ge(r_psum, b + 1)
                act.activation(v[:, :], psR[:, :], ACT.Identity, scale=1.0 / D, bias=k.small[:, 3:4]).then_inc(r_rough, 1)
                link(act.activation(ln[:, :], psR[:, :], ACT.Ln, scale=1.0 / D, bias=k.small[:, 3:4]))
                act.activation(r[:, :], ln[:, :], ACT.Exp, scale=-0.5).then_inc(r_rough, 1)
                act.wait_ge(normed, b * DC + DC)
                if not known(b) or b >= 2:
                    act.wait_ge(stacked[p], stack_count(b, p))
                act.activation(k_hi[p][:, :, :], kn[:, :, :], ACT.Copy).then_inc(k_high, 1)

            split_context(0, 0)
            split_context(1, 1)
            batches(act, step, link, 2)

        @block.vector
        def _(dve):
            link = Link(dve, dve_step)

            def split_context(b, p):
                dve.wait_ge(c_high, b + 1)
                dve.tensor_tensor(c_lo[p][:, :, :], ctxT[:, :, at(b)], c_hi[p][:, :, :], ALU.subtract).then_inc(c_low, 1)

            def step(b, p):
                for t in range(2):
                    dve.wait_ge(v_psum, b * 2 + (t + 1))
                    if not known(b) or b:
                        dve.wait_ge(v_high, b * 2 + (t - 1))
                    dve.tensor_tensor(vf[t][:, :], psV[t][:, :], vbias[:, :], ALU.add).then_inc(v_full, 1)
                for t in range(2):
                    dve.wait_ge(v_high, b * 2 + (t + 1))
                    dve.tensor_tensor(vtile(v_lo, b, t), heads(vf[t][:, :]), vtile(v_hi, b, t), ALU.subtract)
                if not known(b) or b + 2 < B:
                    split_context(b + 2, p)
                dve.wait_ge(r_rough, b * 2 + 2)
                refine_rms(dve, link, r, v, tmp)
                if not known(b) or b:
                    dve.wait_ge(k_high, b)
                for c in range(DC):
                    dve.scalar_tensor_tensor(kn[:, c, :], u[:, c, :], vectors[:, ROWS["gk"] + c:ROWS["gk"] + c + 1],
                                             r[:, :], ALU.mult, ALU.mult).then_inc(normed, 1)
                dve.wait_ge(k_high, b + 1)
                dve.tensor_tensor(k_lo[p][:, :, :], kn[:, :, :], k_hi[p][:, :, :], ALU.subtract).then_inc(k_low, 1)

            split_context(0, 0)
            split_context(1, 1)
            batches(dve, step, link, 6)

        @block.tensor
        def _(pe):
            def step(b, p):
                pe.wait_ge(c_low, b + 1)
                if not known(b) or b:
                    pe.wait_ge(squared, b * (2 * DC))
                for f in range(DC):
                    for c in range(DC):
                        last = three_products(pe, psK[f // 2][:, f % 2, :],
                                              [kw[:, s, c, f * P:(f + 1) * P] for s in range(2)],
                                              [c_hi[p][:, c, :], c_lo[p][:, c, :]], c == 0, c == DC - 1)
                last.then_inc(k_psum, 1)
                for t in range(2):
                    if not known(b) or b:
                        pe.wait_ge(v_full, b * 2 + (t - 1))
                    for c in range(DC):
                        last = three_products(pe, psV[t][:, :], [a[p][:, c, t * P:(t + 1) * P] for a in (c_hi, c_lo)],
                                              [vw[:, s, c, :] for s in range(2)], c == 0, c == DC - 1)
                    last.then_inc(v_psum, 1)
                pe.wait_ge(squared, b * (2 * DC) + 2 * DC)
                for c in range(DC):
                    last = pe.matmul(psR[:, :], k.ones[:, :], sq[:, c, :], start=(c == 0), stop=(c == DC - 1))
                last.then_inc(r_psum, 1)

            batches(pe, step)


def stage_attention(k, ks, v_hi, v_lo, qw, ow, vectors, x_mean, x_rstd, sel):
    nc = k.nc
    with ExitStack() as ctx:
        sb = lambda name, shape, dt: ctx.enter_context(nc.sbuf_tensor(name, shape, dt))
        two = lambda name, shape, dt: [sb(f"{name}{i}", shape, dt) for i in range(2)]
        bo = sb("at_bo", [P, D], F32)
        xn = two("at_xn", [P, D], F32)
        x_hi, x_lo = sb("at_xhi", [P, DC, S], BF16), sb("at_xlo", [P, DC, S], BF16)
        u, sq = sb("at_u", [P, DC, S], F32), sb("at_sq", [P, DC, S], F32)
        ln, r, v, tt = (sb(f"at_{n}", [P, S], F32) for n in ("ln", "r", "v", "t"))
        q_hi, q_lo = sb("at_qhi", [P, DC, S], BF16), sb("at_qlo", [P, DC, S], BF16)
        qs = two("at_qs", [P, HC, DC, S], BF16)
        kb = two("at_kb", [P, HC, DC, S], BF16)
        negmax = two("at_negmax", [P, 4], F32)
        maxes = sb("at_maxes", [P, 2, P], BF16)
        maxT = sb("at_maxT", [P, 2, P], BF16)
        pf = two("at_pf", [P, 2, 2, S], F32)
        ph, pl = two("at_ph", [P, 2, 2, S], BF16), two("at_pl", [P, 2, 2, S], BF16)
        rden = sb("at_rden", [P, 4], F32)
        o = two("at_o", [P, 2, D], F32)
        o_hi, o_lo = sb("at_ohi", [P, DC, S], BF16), sb("at_olo", [P, DC, S], BF16)
        psS = ctx.enter_context(nc.psum_tensor("ps_s", [P, 2, 2, S], F32))
        psT = ctx.enter_context(nc.psum_tensor("ps_st", [P, 2, 2, S], F32))
        psM = ctx.enter_context(nc.psum_tensor("ps_m", [P, 2, P], BF16))
        psO = ctx.enter_context(nc.psum_tensor("ps_o", [P, 4, VC], F32))
        psP = [ctx.enter_context(nc.psum_tensor(f"ps_p{i}", [P, D], F32)) for i in range(2)]
        sem = lambda name: k.semaphore(("at_" + name))
        b_loaded, dve_step, act_step, maxes_zeroed = (sem(n) for n in ("bl", "dve", "act", "mz"))
        s_psum, max_read, maxes_ready, m_psum, maxT_ready, st_psum, exped, p_high, p_low, o_psum, o_read = (
            sem(n) for n in ("sp", "mr", "mx", "mp", "mt", "stp", "ex", "ph", "pl", "op", "od"))
        xn_ready, biased, xt_psum, x_high, x_low, q_psum, squared, r_psum, r_rough, normed, q_high, q_low = (
            sem(n) for n in ("xn", "bi", "xtp", "xh", "xl", "qp", "sq", "rp", "rr", "no", "qh", "ql"))
        ot_psum, ot_high, ot_low, y_psum, y_added = (sem(n) for n in ("otp", "oth", "otl", "yp", "ya"))
        stacked = [sem("st0"), sem("st1")]
        k_loaded = [sem("kl0"), sem("kl1")]
        block = ctx.enter_context(nc.Block())
        xtile = lambda t: k.x[:, bass.ds(t, 1), :]
        one = lambda a, t: a[:, bass.ds(t, 1)]
        in_q = lambda b, ahead: not known(b) or 0 <= b + ahead < B
        in_g = lambda b, u, off: not known(b) or 0 <= b * UNITS + u + off < B * UNITS
        G = UNITS

        uu = u

        def stack_count(b, p):
            return b * (STACK_INCS // 2) + (2 - p) * (STACK_INCS // 2)

        def steps(engine, step, link=None, per=0):
            for b in range(-2, 2):
                for u in range(UNITS):
                    step(b, b % 2, u)
            with (link.loop((B - 4) // 2, per) if link else engine.Fori(0, (B - 4) // 2)) as i:
                for p in range(2):
                    for u in range(UNITS):
                        step(i * 2 + (p + 2), p, u)
            for b in range(B - 2, B + 1):
                for u in range(UNITS):
                    step(b, b % 2, u)

        @block.sync
        def _(sp):
            sp.dma_start(bo[:, :], broadcast_rows(k.ins["L1_xattn_bo"], D)).then_inc(b_loaded, 16)

            def step(b, p, u):
                if u == 2 and in_q(b, 1):
                    if not known(b) or b >= 1:
                        sp.wait_ge(st_psum, b * G)
                    sp.dma_start(kb[1 - p][:, :, :, :], ks[bass.ds(b + 1, 1), :, :, :, :].rearrange("o p h c s -> (o p) h c s"))\
                      .then_inc(k_loaded[1 - p], 16)
                if u == 3 and in_q(b, 1):
                    sp.wait_ge(q_low, b + 2)
                    if not known(b) or b >= 1:
                        sp.wait_ge(st_psum, b * G)
                    stack_heads(sp, lambda rows, hm: qs[1 - p][rows, hm, :, :], q_hi, q_lo, (0, 0, 1, 1), stacked[1 - p])

            steps(sp, step)

        @block.gpsimd
        def _(pool):
            pool.memset(maxes[:, :, :], 0.0).then_inc(maxes_zeroed, 1)
            pool.wait_ge(b_loaded, 16)

            def step(b, p, u):
                if u == 5 and in_q(b, 2):
                    for t in range(2):
                        pool.wait_ge(xn_ready, b * 2 + (4 + t + 1))
                        pool.tensor_tensor(xtile(b * 2 + (4 + t)), xtile(b * 2 + (4 + t)), bo[:, :].unsqueeze(1), ALU.add)\
                            .then_inc(biased, 1)
                if in_g(b, u, 0):
                    g = b * G + u
                    pool.wait_ge(p_high, g + 1)
                    pool.tensor_tensor(pl[u % 2][:, :, :, :], pf[u % 2][:, :, :, :], ph[u % 2][:, :, :, :], ALU.subtract)\
                        .then_inc(p_low, 1)

            steps(pool, step)

        @block.scalar
        def _(act):
            link = Link(act, act_step)

            def biased_and_squared(q, c):
                act.wait_ge(q_psum, q * DC + (c + 1))
                if c == 0 and (not known(q) or q):
                    act.wait_ge(normed, q * DC)
                bias = vectors[:, ROWS["bq"] + c:ROWS["bq"] + c + 1]
                act.activation(u_[:, c, :], psP[1 - c % 2][:, 0:S], ACT.Identity, bias=bias).then_inc(squared, 1)
                act.activation(sq[:, c, :], psP[1 - c % 2][:, 0:S], ACT.Square, bias=bias).then_inc(squared, 1)

            def step(b, p, u):
                if u == 0 and in_q(b, 1):
                    biased_and_squared(b + 1, 2)
                    biased_and_squared(b + 1, 3)
                if in_g(b, u, 0):
                    g = b * G + u
                    act.wait_ge(st_psum, g + 1)
                    if not known(b) or g >= 2:
                        act.wait_ge(p_low, g - 1)
                    act.activation(pf[u % 2][:, :, :, :], psT[:, :, :, :], ACT.Exp, scale=SCORE_SCALE).then_inc(exped, 1)
                    act.wait_ge(exped, g + 1)
                    act.activation(ph[u % 2][:, :, :, :], pf[u % 2][:, :, :, :], ACT.Copy).then_inc(p_high, 1)
                if u == 1 and in_q(b, 1):
                    act.wait_ge(r_psum, b + 2)
                    act.activation(v[:, :], psP[0][:, 0:S], ACT.Identity, scale=1.0 / D, bias=k.small[:, 3:4]).then_inc(r_rough, 1)
                    link(act.activation(ln[:, :], psP[0][:, 0:S], ACT.Ln, scale=1.0 / D, bias=k.small[:, 3:4]))
                    act.activation(r[:, :], ln[:, :], ACT.Exp, scale=-0.5).then_inc(r_rough, 1)
                if u == 2 and in_q(b, 1):
                    act.wait_ge(normed, b * DC + 2 * DC)
                    if not known(b) or b + 1 >= 1:
                        act.wait_ge(stacked[p], stack_count(b, p))
                    act.activation(q_hi[:, :, :], u_[:, :, :], ACT.Copy).then_inc(q_high, 1)
                if u == 3 and in_q(b, -1):
                    for t in range(2):
                        act.wait_ge(ot_psum, b * 2 + (t - 1))
                        act.activation(o_hi[:, :, t * P:(t + 1) * P], psP[1 - t][:, :].rearrange("p (c t) -> p c t", c=DC),
                                       ACT.Copy).then_inc(ot_high, 1)
                if u == 6 and in_q(b, 2):
                    for t in range(2):
                        act.wait_ge(xt_psum, b * 2 + (4 + t + 1))
                        act.activation(x_hi[:, :, t * P:(t + 1) * P], psP[1 - t][:, :].rearrange("p (c t) -> p c t", c=DC),
                                       ACT.Copy).then_inc(x_high, 1)
                if u == 7 and in_q(b, 2):
                    biased_and_squared(b + 2, 0)
                    biased_and_squared(b + 2, 1)

            u_ = uu
            steps(act, step, link, 2)

        @block.vector
        def _(dve):
            link = Link(dve, dve_step)
            u_ = uu
            dve.wait_ge(maxes_zeroed, 1)

            def step(b, p, u):
                g = b * G + u
                if in_g(b, u, 0):
                    dve.wait_ge(m_psum, g + 1)
                    dve.tensor_copy(maxT[:, :, :], psM[:, :, :]).then_inc(maxT_ready, 1)
                if in_g(b, u, 1):
                    n = (u + 1) % 2
                    dve.wait_ge(s_psum, g + 2)
                    dve.tensor_reduce(negmax[n][:, :].rearrange("p (j q) -> p j q", j=2), psS[:, :, :, :], AX.X, ALU.max,
                                      negate=True).then_inc(max_read, 1)
                    dve.wait_ge(max_read, g + 2)
                    m = negmax[n][:, :].rearrange("p (j q) -> p q j", j=2)
                    link(dve.tensor_copy(maxes[:, :, 0:4:2], m))
                    dve.tensor_tensor(maxes[:, :, 1:4:2], m, maxes[:, :, 0:4:2], ALU.subtract).then_inc(maxes_ready, 1)
                if in_g(b, u, -2):
                    dve.wait_ge(o_psum, g - 1)
                    uo = (u - 2) % UNITS
                    po = p if u >= 2 else 1 - p
                    link(dve.reciprocal(rden[:, :], psO[:, :, HD]))
                    dst = o[po][:, :, uo * 2 * HD:(uo + 1) * 2 * HD].rearrange("p q (j d) -> p j q d", j=2)
                    dve.tensor_tensor(dst, psO[:, :, 0:HD].rearrange("p (j q) d -> p j q d", j=2),
                                      rden[:, :].rearrange("p (j q) -> p j q", j=2).unsqueeze(3).broadcast_to([P, 2, 2, HD]),
                                      ALU.mult).then_inc(o_read, 1)
                if u == 1 and in_q(b, 1):
                    dve.wait_ge(r_rough, b * 2 + 4)
                    refine_rms(dve, link, r, v, tt)
                    for c in range(DC):
                        dve.scalar_tensor_tensor(u_[:, c, :], u_[:, c, :], vectors[:, ROWS["gq"] + c:ROWS["gq"] + c + 1],
                                                 r[:, :], ALU.mult, ALU.mult).then_inc(normed, 1)
                if u == 2 and in_q(b, 1):
                    dve.wait_ge(q_high, b + 2)
                    dve.tensor_tensor(q_lo[:, :, :], u_[:, :, :], q_hi[:, :, :], ALU.subtract).then_inc(q_low, 1)
                if u == 3 and in_q(b, -1):
                    for t in range(2):
                        dve.wait_ge(ot_high, b * 2 + (t - 1))
                        half = slice(t * P, (t + 1) * P)
                        dve.tensor_tensor(o_lo[:, :, half], psP[1 - t][:, :].rearrange("p (c t) -> p c t", c=DC),
                                          o_hi[:, :, half], ALU.subtract).then_inc(ot_low, 1)
                for t in range(2):
                    if u == 4 + t and in_q(b, -1):
                        tile = b * 2 + (t - 2)
                        dve.wait_ge(y_psum, b * 2 + (t - 1))
                        dve.wait_ge(biased, b * 2 + (t - 1))
                        dve.tensor_tensor(xtile(tile), xtile(tile), psP[1 - t][:, :].unsqueeze(1), ALU.add).then_inc(y_added, 1)
                if u == 4 and in_q(b, 2):
                    for t in range(2):
                        tile = b * 2 + (4 + t)
                        if not known(b) or b + 2 >= 1:
                            dve.wait_ge(xt_psum, tile - 1)
                        dve.tensor_scalar(xn[t][:, :], xtile(tile), one(x_mean, tile), one(x_rstd, tile),
                                          ALU.subtract, ALU.mult).then_inc(xn_ready, 1)
                if u == 6 and in_q(b, 2):
                    for t in range(2):
                        dve.wait_ge(x_high, b * 2 + (4 + t + 1))
                        half = slice(t * P, (t + 1) * P)
                        dve.tensor_tensor(x_lo[:, :, half], psP[1 - t][:, :].rearrange("p (c t) -> p c t", c=DC),
                                          x_hi[:, :, half], ALU.subtract).then_inc(x_low, 1)

            steps(dve, step, link, 2 * (8 * 2 + 3))

        @block.tensor
        def _(pe):
            def scores(b, p, u, g):
                if u == 0:
                    pe.wait_ge(stacked[p], stack_count(b, p))
                    pe.wait_ge(k_loaded[p], b * 8 + 8 * (2 - p))
                if not known(g) or g:
                    pe.wait_ge(max_read, g)
                c, h0 = u // 2, 2 * (u % 2)
                for j in range(2):
                    for q in range(2):
                        last = pe.matmul(psS[:, j, q, :], qs[p][:, h0 + j, c, q * P:(q + 1) * P], kb[p][:, h0 + j, c, :],
                                         start=True, stop=True)
                last.then_inc(s_psum, 1)

            def turn_maxes(g):
                pe.wait_ge(maxes_ready, g + 1)
                if not known(g) or g:
                    pe.wait_ge(maxT_ready, g)
                for q in range(2):
                    last = pe.transpose(psM[:, q, :], maxes[:, q, :], k.ident_b[:, :])
                last.then_inc(m_psum, 1)

            def values(b, u, g):
                pe.wait_ge(p_low, g + 1)
                if not known(g) or g:
                    pe.wait_ge(o_read, g)
                for j in range(2):
                    for q in range(2):
                        cols = slice(q * P, (q + 1) * P)
                        for n, (pr, vv) in enumerate(((ph, v_hi), (ph, v_lo), (pl, v_hi))):
                            for kc in range(2):
                                last = pe.matmul(psO[:, 2 * j + q, :], pr[u % 2][:, j, kc, cols],
                                                 vv[:, bass.ds(b * 2 + kc, 1), 2 * u + j, :].rearrange("p o d -> p (o d)"),
                                                 start=(n == 0 and kc == 0), stop=(n == 2 and kc == 1))
                last.then_inc(o_psum, 1)

            def transposed_scores(b, p, u, g):
                pe.wait_ge(maxT_ready, g + 1)
                if not known(g) or g:
                    pe.wait_ge(exped, g)
                c, h0 = u // 2, 2 * (u % 2)
                for j in range(2):
                    for kc in range(2):
                        pe.matmul(psT[:, j, kc, :], kb[p][:, h0 + j, c, kc * P:(kc + 1) * P], qs[p][:, h0 + j, c, :],
                                  start=True, stop=False)
                        last = pe.matmul(psT[:, j, kc, :], sel[:, j, :], maxT[:, :, :].rearrange("p q t -> p (q t)"),
                                         start=False, stop=True)
                last.then_inc(st_psum, 1)

            def queries(q, c):
                if c == 0:
                    pe.wait_ge(x_low, q * 2 + 2)
                if c >= 2:
                    pe.wait_ge(squared, q * (2 * DC) + 2 * (c - 1))
                for kc in range(DC):
                    last = three_products(pe, psP[1 - c % 2][:, 0:S], [qw[:, s, kc, c * P:(c + 1) * P] for s in range(2)],
                                          [x_hi[:, kc, :], x_lo[:, kc, :]], kc == 0, kc == DC - 1)
                last.then_inc(q_psum, 1)

            def step(b, p, u):
                g = b * G + u
                if in_g(b, u, 1):
                    nb, np_, nu = (b, p, u + 1) if u + 1 < UNITS else (b + 1, 1 - p, 0)
                    scores(nb, np_, nu, g + 1)
                if in_g(b, u, 0):
                    turn_maxes(g)
                if in_g(b, u, -2):
                    ob, ou = (b, u - 2) if u >= 2 else (b - 1, u + UNITS - 2)
                    values(ob, ou, g - 2)
                if in_g(b, u, 0):
                    transposed_scores(b, p, u, g)
                if u == 0 and in_q(b, 1):
                    pe.wait_ge(squared, b * (2 * DC) + 4 * DC)
                    for c in range(DC):
                        last = pe.matmul(psP[0][:, 0:S], k.ones[:, :], sq[:, c, :], start=(c == 0), stop=(c == DC - 1))
                    last.then_inc(r_psum, 1)
                if u == 2 and in_q(b, -1):
                    pe.wait_ge(o_read, b * G)
                    if in_q(b, 1):
                        pe.wait_ge(r_rough, b * 2 + 4)
                    for t in range(2):
                        for c in range(DC):
                            last = pe.transpose(psP[1 - t][:, c * P:(c + 1) * P], o[1 - p][:, t, c * P:(c + 1) * P], k.ident[:, :])
                        last.then_inc(ot_psum, 1)
                for t in range(2):
                    if u == 3 + t and in_q(b, -1):
                        pe.wait_ge(ot_low, b * 2)
                        for c in range(DC):
                            last = three_products(pe, psP[1 - t][:, :], [a[:, c, t * P:(t + 1) * P] for a in (o_hi, o_lo)],
                                                  [ow[:, s, c, :] for s in range(2)], c == 0, c == DC - 1)
                        last.then_inc(y_psum, 1)
                if u == 5 and in_q(b, 2):
                    for t in range(2):
                        pe.wait_ge(xn_ready, b * 2 + (4 + t + 1))
                        if not known(b) or b >= 1:
                            pe.wait_ge(y_added, b * 2 + (t - 1))
                        for c in range(DC):
                            last = pe.transpose(psP[1 - t][:, c * P:(c + 1) * P], xn[t][:, c * P:(c + 1) * P], k.ident[:, :])
                        last.then_inc(xt_psum, 1)
                if u == 6 and in_q(b, 2):
                    queries(b + 2, 0)
                    queries(b + 2, 1)
                if u == 7 and in_q(b, 2):
                    queries(b + 2, 2)
                    queries(b + 2, 3)

            steps(pe, step)


E_N = 16
SH_N = 2
FE = 256
F2 = FE // P
BLK = 256
ST = BLK // P
NBLK = (2 * TOK + E_N * (BLK - 1)) // BLK
FLOOR = 0.498


def stage_router(k, xf, xT_hi, xT_lo, xaff):
    nc = k.nc
    with ExitStack() as ctx:
        sb = lambda name, shape, dt: ctx.enter_context(nc.sbuf_tensor(name, shape, dt))
        two = lambda name, shape, dt: [sb(f"{name}{i}", shape, dt) for i in range(2)]
        wa = sb("r_wa", [P, DC, E_N], F32)
        stats = sb("r_stats", [P, NT, 6], F32)
        mean, var, tmp, rstd = (sb(f"r_{n}", [P, NT], F32) for n in ("mean", "var", "tmp", "rstd"))
        xn, xT = two("r_xn", [P, D], F32), two("r_xT", [P, DC, P], F32)
        ex = sb("r_exp", [P, NT, E_N], F32)
        psX = [ctx.enter_context(nc.psum_tensor(f"ps_rx{i}", [P, D], F32)) for i in range(2)]
        psL = ctx.enter_context(nc.psum_tensor("ps_rl", [P, NT * E_N], F32))
        sem = lambda name: k.semaphore(("r_" + name))
        wa_loaded, stat_done, dve_step, var_ready, rstd_ready, xn_ready, added, x_psum, xT_ready, x_high, x_low, logits, exped = (
            sem(n) for n in ("wa", "stat", "dve", "var", "rstd", "xn", "add", "xp", "xT", "xh", "xl", "log", "ex"))
        block = ctx.enter_context(nc.Block())
        row = lambda a, t: a[:, bass.ds(t, 1), :]
        cols = lambda a, t: a[:, :, bass.ds(t * P, P)]
        chunks = lambda a: a.rearrange("p (c t) -> p c t", c=DC)

        @block.sync
        def _(sp):
            sp.dma_start(wa[:, :, :], k.ins["L1_ffn_wa"].rearrange("(c p) e -> p c e", p=P)).then_inc(wa_loaded, 16)

        @block.gpsimd
        def _(pool):
            pool.wait_ge(var_ready, 1)
            pool.tensor_tensor(rstd[:, :], var[:, :], k.pow_half[:, :], ALU.pow).then_inc(rstd_ready, 1)
            with pool.Fori(0, NT // 2) as i:
                for p in range(2):
                    t = i * 2 + p
                    pool.wait_ge(xn_ready, i * 2 + (p + 1))
                    pool.tensor_tensor(row(k.x, t), row(k.x, t), xn[p][:, :].unsqueeze(1), ALU.add).then_inc(added, 1)

        @block.vector
        def _(dve):
            link = Link(dve, dve_step)
            for t in range(NT):
                dve.bn_stats(stats[:, t, :], k.x[:, t, :]).then_inc(stat_done, 1)
            dve.wait_ge(stat_done, NT)
            mean_var(link, dve, stats, mean[:, :], var[:, :], tmp[:, :], LN_EPS)
            dve.sem_inc(var_ready, 1)
            dve.wait_ge(rstd_ready, 1)
            dve.sem_inc(added, 2)

            def split(t, p):
                dve.wait_ge(x_high, t + 1)
                dve.tensor_tensor(cols(xT_lo, t), xT[p][:, :, :], cols(xT_hi, t), ALU.subtract).then_inc(x_low, 1)

            with dve.Fori(0, NT // 2) as i:
                for p in range(2):
                    t = i * 2 + p
                    dve.wait_ge(added, i * 2 + (p + 1))
                    dve.wait_ge(x_psum, i * 2 + (p + 1))
                    dve.tensor_scalar(xn[p][:, :], row(k.x, t), mean[:, bass.ds(t, 1)], rstd[:, bass.ds(t, 1)],
                                      ALU.subtract, ALU.mult)
                    dve.tensor_scalar(row(xf, t), row(k.x, t), mean[:, bass.ds(t, 1)], rstd[:, bass.ds(t, 1)],
                                      ALU.subtract, ALU.mult).then_inc(xn_ready, 1)
                    split(t, p)
            dve.wait_ge(exped, 1)
            link(dve.tensor_scalar(ex[:, :, :], ex[:, :, :], 1.0, None, ALU.add))
            dve.reciprocal(xaff[:, :, :], ex[:, :, :])

        @block.tensor
        def _(pe):
            pe.sem_inc(x_psum, 2)
            pe.wait_ge(wa_loaded, 16)
            with pe.Fori(0, NT // 2) as i:
                for p in range(2):
                    t = i * 2 + p
                    pe.wait_ge(xn_ready, i * 2 + (p + 1))
                    pe.wait_ge(xT_ready, i * 2 + (p + 1))
                    for c in range(DC):
                        last = pe.transpose(psX[p][:, c * P:(c + 1) * P], xn[p][:, c * P:(c + 1) * P], k.ident[:, :])
                    last.then_inc(x_psum, 1)
                    pe.wait_ge(xT_ready, i * 2 + (p + 3))
                    for c in range(DC):
                        last = pe.matmul(psL[:, bass.ds(t * E_N, E_N)], xT[p][:, c, :], wa[:, c, :],
                                         start=(c == 0), stop=(c == DC - 1))
                    last.then_inc(logits, 1)

        @block.scalar
        def _(act):
            act.sem_inc(xT_ready, 2)
            act.sem_inc(logits, 2)
            act.sem_inc(x_low, 2)
            with act.Fori(0, NT // 2) as i:
                for p in range(2):
                    t = i * 2 + p
                    act.wait_ge(x_psum, i * 2 + (p + 3))
                    act.wait_ge(logits, i * 2 + (p + 1))
                    act.wait_ge(x_low, i * 2 + (p + 1))
                    act.activation(xT[p][:, :, :], chunks(psX[p][:, :]), ACT.Copy).then_inc(xT_ready, 1)
                    act.wait_ge(xT_ready, i * 2 + (p + 3))
                    act.activation(cols(xT_hi, t), xT[p][:, :, :], ACT.Copy).then_inc(x_high, 1)
            act.wait_ge(logits, NT + 2)
            act.activation(ex[:, :, :].rearrange("p t e -> p (t e)"), psL[:, :], ACT.Exp, scale=-1.0).then_inc(exped, 1)


def stage_shared_weights(k, sgu, sd, sbias):
    nc = k.nc
    with ExitStack() as ctx:
        sb = lambda name, shape, dt: ctx.enter_context(nc.sbuf_tensor(name, shape, dt))
        raw = [sb(f"sw_raw{i}", [P, 1024], F32) for i in range(6)]
        sem = lambda name: k.semaphore(("sw_" + name))
        loaded, b_loaded, high = [sem(f"l{i}") for i in range(6)], sem("bl"), sem("hi")
        block = ctx.enter_context(nc.Block())
        dst = [(sgu, e, m) for e in range(SH_N) for m in range(2)] + [(sd, e, 0) for e in range(SH_N)]
        place = lambda n, s: (dst[n][0][:, s, dst[n][1], dst[n][2], :] if n < 4 else dst[n][0][:, s, dst[n][1], :])

        @block.sync
        def _(sp):
            for n in range(6):
                e = dst[n][1]
                src = k.ins[("L1_ffn_sg", "L1_ffn_sw1")[dst[n][2]] if n < 4 else "L1_ffn_sw2"][e, :, :]
                c = D // P if n < 4 else F2
                sp.dma_start(raw[n][:, :].rearrange("p (c n) -> p c n", c=c),
                             src.rearrange("(c p) n -> p c n", p=P)).then_inc(loaded[n], 16)
            for e in range(SH_N):
                src = k.ins["L1_ffn_sb2"]
                sp.dma_start(sbias[:, e, :], bass.AP(tensor=src.tensor, offset=e * D, ap=[[0, P], [1, D]])).then_inc(b_loaded, 16)

        @block.scalar
        def _(act):
            for n in range(6):
                act.wait_ge(loaded[n], 16)
                act.activation(place(n, 0), raw[n][:, :], ACT.Copy).then_inc(high, 1)

        @block.vector
        def _(dve):
            for n in range(6):
                dve.wait_ge(high, n + 1)
                dve.tensor_tensor(place(n, 1), raw[n][:, :], place(n, 0), ALU.subtract)

        @block.gpsimd
        def _(pool):
            added = sem("ad")
            pool.wait_ge(b_loaded, 32)
            pool.tensor_tensor(sbias[:, 0, :], sbias[:, 0, :], sbias[:, 1, :], ALU.add).then_inc(added, 1)
            pool.wait_ge(added, 1)
            with pool.Fori(0, NT) as t:
                pool.tensor_tensor(k.x[:, bass.ds(t, 1), :], k.x[:, bass.ds(t, 1), :], sbias[:, 0:1, :], ALU.add)


def stage_route_and_shared(k, xf, xT_hi, xT_lo, xaff, sgu, sd, slots, share, combine, wrow):
    nc = k.nc
    with ExitStack() as ctx:
        sb = lambda name, shape, dt: ctx.enter_context(nc.sbuf_tensor(name, shape, dt))
        two = lambda name, shape, dt: [sb(f"{name}{i}", shape, dt) for i in range(2)]
        best = sb("s_best", [P, NT, 8], F32)
        index = sb("s_index", [P, NT, 8], U32)
        indexf = sb("s_indexf", [P, NT, 8], F32)
        iota_e = sb("s_iota_e", [P, E_N], F32)
        iota_j = sb("s_iota_j", [P, NBLK], F32)
        iota_p = sb("s_iota_p", [P, 1], F32)
        hot = [sb(f"s_hot{i}", [P, NT, E_N], F32) for i in range(2)]
        both = sb("s_both", [P, NT, E_N], F32)
        before = sb("s_before", [P, P], F32)
        pos = sb("s_pos", [P, NT, E_N], F32)
        run = [sb(f"s_run{i}", [P, NT + 1, E_N], F32) for i in range(2)]
        blocks = [sb(f"s_blocks{i}", [P, E_N], F32) for i in range(2)]
        start = sb("s_start", [P, E_N], F32)
        slotf = sb("s_slotf", [P, 2, NT], F32)
        le = sb("s_le", [P, NBLK, E_N], F32)
        wf = sb("s_wf", [P, NBLK], F32)
        total = sb("s_total", [P, NT], F32)
        gf, yf = two("s_gf", [P, F2, BLK], F32), two("s_yf", [P, F2, BLK], F32)
        y_hi, y_lo = two("s_yhi", [P, SH_N, F2, BLK], BF16), two("s_ylo", [P, SH_N, F2, BLK], BF16)
        psR = ctx.enter_context(nc.psum_tensor("ps_sr", [P, 2, NT * E_N], F32))
        psG = [ctx.enter_context(nc.psum_tensor(f"ps_sg{i}", [P, F2, BLK], F32)) for i in range(2)]
        psU = [ctx.enter_context(nc.psum_tensor(f"ps_su{i}", [P, F2, BLK], F32)) for i in range(2)]
        psD = [ctx.enter_context(nc.psum_tensor(f"ps_sd{i}", [P, D], F32)) for i in range(ST)]
        sem = lambda name: k.semaphore(("s_" + name))
        consts, both_ready, counted, dve_step, slots_ready, scattered = (sem(n) for n in ("co", "bo", "ct", "dve", "sl", "sc"))
        gu_psum, gelu_done, u_read, y_full, y_high, y_low, d_psum, d_added = (
            sem(n) for n in ("gu", "ge", "ur", "yf", "yh", "yl", "dp", "da"))
        block = ctx.enter_context(nc.Block())
        CH = TOK // BLK

        @block.gpsimd
        def _(pool):
            pool.iota(iota_e[:, :], [[1, E_N]], base=0, channel_multiplier=0, allow_small_or_imprecise_dtypes=True).then_inc(consts, 1)
            pool.iota(iota_j[:, :], [[1, NBLK]], base=0, channel_multiplier=0, allow_small_or_imprecise_dtypes=True).then_inc(consts, 1)
            pool.iota(iota_p[:, :], [[0, 1]], base=0, channel_multiplier=1, allow_small_or_imprecise_dtypes=True).then_inc(consts, 1)
            pool.affine_select(out=before[:, :], in_=k.ones[:, :], compare_op=ALU.is_gt, fill=0.0, base=0,
                               pattern=[[1, P]], channel_multiplier=-1).then_inc(consts, 1)
            pool.wait_ge(slots_ready, 1)
            for s in range(2):
                for t in range(NT):
                    pool.indirect_dma_start(out=k.scratch["rows"], out_offset=bass.IndirectOffsetOnAxis(ap=slots[:, s, t:t + 1], axis=0),
                                            in_=xf[:, t, :], in_offset=None).then_inc(scattered, 16)
            pool.wait_ge(scattered, 16 * 2 * NT)

        @block.vector
        def _(dve):
            link = Link(dve, dve_step)
            for t in range(NT):
                link(dve.max(best[:, t, :], xaff[:, t, :]), wait=False)
            dve.wait_ge(dve_step, NT)
            for t in range(NT):
                link(dve.max_index(index[:, t, :], best[:, t, :], xaff[:, t, :]), wait=False)
            dve.wait_ge(dve_step, 2 * NT)
            link(dve.tensor_copy(indexf[:, :, :], index[:, :, :]))
            dve.wait_ge(consts, 4)
            for s in range(2):
                link(dve.tensor_tensor(hot[s][:, :, :], iota_e[:, :].unsqueeze(1).broadcast_to([P, NT, E_N]),
                                       indexf[:, :, s:s + 1].broadcast_to([P, NT, E_N]), ALU.is_equal))
            dve.tensor_tensor(both[:, :, :], hot[0][:, :, :], hot[1][:, :, :], ALU.add).then_inc(both_ready, 1)
            link(dve.tensor_tensor(total[:, :], best[:, :, 0], best[:, :, 1], ALU.add))
            link(dve.reciprocal(total[:, :], total[:, :]))
            for s in range(2):
                link(dve.tensor_tensor(share[:, s, :], best[:, :, s], total[:, :], ALU.mult))
                link(dve.tensor_tensor(le[:, 0:NT, :] if s else combine[:, :, :], hot[s][:, :, :],
                                       share[:, s, :].unsqueeze(2).broadcast_to([P, NT, E_N]), ALU.mult))
            link(dve.tensor_tensor(combine[:, :, :], combine[:, :, :], le[:, 0:NT, :], ALU.add))
            dve.wait_ge(counted, 1)
            link(dve.memset(run[0][:, 0:1, :], 0.0))
            link(dve.tensor_copy(run[0][:, 1:, :], psR[:, 1, :].rearrange("p (t e) -> p t e", e=E_N)))
            a, step = 0, 1
            while step <= NT:
                link(dve.tensor_tensor(run[1 - a][:, step:, :], run[a][:, step:, :], run[a][:, 0:NT + 1 - step, :], ALU.add))
                link(dve.tensor_copy(run[1 - a][:, 0:step, :], run[a][:, 0:step, :]))
                a, step = 1 - a, 2 * step
            link(dve.tensor_scalar(blocks[0][:, :], run[a][:, NT, :], 1.0 / BLK, (BLK - 1.0) / BLK - FLOOR, ALU.mult, ALU.add))
            link(dve.tensor_scalar(blocks[0][:, :], blocks[0][:, :], ROUND, ROUND, ALU.add, ALU.subtract))
            link(dve.tensor_copy(start[:, :], blocks[0][:, :]))
            b, step = 0, 1
            while step < E_N:
                link(dve.tensor_tensor(blocks[1 - b][:, step:], blocks[b][:, step:], blocks[b][:, 0:E_N - step], ALU.add))
                link(dve.tensor_copy(blocks[1 - b][:, 0:step], blocks[b][:, 0:step]))
                b, step = 1 - b, 2 * step
            link(dve.tensor_tensor(start[:, :], blocks[b][:, :], start[:, :], ALU.subtract))
            link(dve.tensor_tensor(pos[:, :, :], psR[:, 0, :].rearrange("p (t e) -> p t e", e=E_N), run[a][:, 0:NT, :], ALU.add))
            link(dve.tensor_scalar(blocks[b][:, :], start[:, :], float(BLK), None, ALU.mult))
            link(dve.tensor_tensor(pos[:, :, :], pos[:, :, :], blocks[b][:, :].unsqueeze(1).broadcast_to([P, NT, E_N]), ALU.add))
            for s in range(2):
                link(dve.tensor_tensor(both[:, :, :], pos[:, :, :], hot[s][:, :, :], ALU.mult))
                link(dve.tensor_reduce(slotf[:, s, :], both[:, :, :], AX.X, ALU.add))
            dve.tensor_copy(slots[:, :, :], slotf[:, :, :]).then_inc(slots_ready, 1)
            link(dve.tensor_tensor(le[:, :, :], start[:, :].unsqueeze(1).broadcast_to([P, NBLK, E_N]),
                                   iota_j[:, :].unsqueeze(2).broadcast_to([P, NBLK, E_N]), ALU.is_le))
            link(dve.tensor_reduce(wf[:, :], le[:, :, :], AX.X, ALU.add))
            link(dve.tensor_scalar(wf[:, :], wf[:, :], float(P), -float(P), ALU.mult, ALU.add))
            link(dve.tensor_scalar(wf[:, :], wf[:, :], iota_p[:, :], None, ALU.add))
            link(dve.tensor_copy(wrow[:, :], wf[:, :]))

            dve.sem_inc(d_added, ST)
            with dve.Fori(0, CH) as i:
                for e in range(SH_N):
                    dve.wait_ge(gelu_done, i * SH_N + (e + 1))
                    for f in range(F2):
                        last = dve.scalar_tensor_tensor(yf[e][:, f, :], psU[e][:, f, :],
                                                        k.vectors[:, ROWS["sb1"] + 2 * e + f:ROWS["sb1"] + 2 * e + f + 1],
                                                        gf[e][:, f, :], ALU.add, ALU.mult)
                    last.then_inc(y_full, 1)
                    dve.wait_ge(y_high, i * SH_N + (e + 1))
                    dve.tensor_tensor(y_lo[0][:, e, :, :], yf[e][:, :, :], y_hi[0][:, e, :, :], ALU.subtract).then_inc(y_low, 1)
                for s in range(ST):
                    dve.wait_ge(d_psum, i * ST + (s + 2))
                    x = k.x[:, bass.ds(i * ST + s, 1), :]
                    dve.tensor_tensor(x, x, psD[s][:, :].unsqueeze(1), ALU.add).then_inc(d_added, 1)

        @block.scalar
        def _(act):
            act.sem_inc(y_low, SH_N)
            with act.Fori(0, CH) as i:
                for e in range(SH_N):
                    act.wait_ge(gu_psum, i * SH_N + (e + 1 + SH_N))
                    act.wait_ge(y_low, i * SH_N + (e + 1))
                    for f in range(F2):
                        last = act.activation(gf[e][:, f, :], psG[e][:, f, :], ACT.Gelu,
                                              bias=k.vectors[:, ROWS["sgb"] + 2 * e + f:ROWS["sgb"] + 2 * e + f + 1])
                    last.then_inc(gelu_done, 1)
                    act.wait_ge(y_full, i * SH_N + (e + 1))
                    act.wait_ge(d_psum, i * ST + 1)
                    act.activation(y_hi[0][:, e, :, :], yf[e][:, :, :], ACT.Copy).then_inc(y_high, 1)

        @block.tensor
        def _(pe):
            pe.sem_inc(gu_psum, SH_N)
            pe.sem_inc(d_psum, 1)
            pe.wait_ge(both_ready, 1)
            pe.wait_ge(consts, 4)
            flat = both[:, :, :].rearrange("p t e -> p (t e)")
            pe.matmul(psR[:, 0, :], before[:, :], flat, start=True, stop=True)
            pe.matmul(psR[:, 1, :], k.ones[:, :], flat, start=True, stop=True).then_inc(counted, 1)

            def up(i, e):
                for ps, m in ((psG, 0), (psU, 1)):
                    for f in range(F2):
                        for c in range(DC):
                            col = c * FE + f * P
                            last = three_products(pe, ps[e][:, f, :], [sgu[:, s, e, m, col:col + P] for s in range(2)],
                                                  [a[:, c, bass.ds(i * BLK, BLK)] for a in (xT_hi, xT_lo)], c == 0, c == DC - 1)
                last.then_inc(gu_psum, 1)

            def down(i):
                for e in range(SH_N):
                    pe.wait_ge(y_low, i * SH_N + (e + 1 + SH_N))
                for s in range(ST):
                    pe.wait_ge(d_added, i * ST + (s + 1))
                    for e in range(SH_N):
                        for f in range(F2):
                            last = three_products(pe, psD[s][:, :], [a[0][:, e, f, s * P:(s + 1) * P] for a in (y_hi, y_lo)],
                                                  [sd[:, h, e, f * D:(f + 1) * D] for h in range(2)],
                                                  e == 0 and f == 0, e == SH_N - 1 and f == F2 - 1)
                    last.then_inc(d_psum, 1)

            for e in range(SH_N):
                up(0, e)
            with pe.Fori(0, CH - 1) as i:
                for e in range(SH_N):
                    pe.wait_ge(y_full, i * SH_N + (e + 1))
                    up(i + 1, e)
                down(i)
            down(CH - 1)


def stage_experts(k, wrow):
    nc = k.nc
    with ExitStack() as ctx:
        sb = lambda name, shape, dt: ctx.enter_context(nc.sbuf_tensor(name, shape, dt))
        two = lambda name, shape, dt: [sb(f"{name}{i}", shape, dt) for i in range(2)]
        raw = [two(f"e_raw{m}", [P, DC * FE], F32) for m in range(3)]
        wb = [two(f"e_wb{m}", [P, F2], F32) for m in range(2)]
        hi, lo = ([two(f"e_{n}{m}", [P, DC * FE], BF16) for m in range(3)] for n in ("hi", "lo"))
        rows = two("e_rows", [P, ST, D], F32)
        x_hi, x_lo = two("e_xhi", [P, DC, BLK], BF16), two("e_xlo", [P, DC, BLK], BF16)
        gf, yf = two("e_gf", [P, F2, BLK], F32), two("e_yf", [P, F2, BLK], F32)
        y_hi, y_lo = two("e_yhi", [P, F2, BLK], BF16), two("e_ylo", [P, F2, BLK], BF16)
        yo = two("e_yo", [P, ST, D], F32)
        psX = [ctx.enter_context(nc.psum_tensor(f"ps_ex{i}", [P, D], F32)) for i in range(ST)]
        psG = [ctx.enter_context(nc.psum_tensor(f"ps_eg{i}", [P, F2, BLK], F32)) for i in range(2)]
        psU = [ctx.enter_context(nc.psum_tensor(f"ps_eu{i}", [P, F2, BLK], F32)) for i in range(2)]
        psD = [ctx.enter_context(nc.psum_tensor(f"ps_ed{i}", [P, D], F32)) for i in range(ST)]
        sem = lambda name: k.semaphore(("e_" + name))
        w_loaded, rows_loaded = [sem("wl0"), sem("wl1")], [sem("rl0"), sem("rl1")]
        w_high, w_low, x_psum, x_high, x_low, gu_psum, gelu_done, y_full, y_high, y_low, d_psum, out_ready = (
            sem(n) for n in ("wh", "wlo", "xp", "xh", "xl", "gu", "ge", "yf", "yh", "yl", "dp", "or"))
        stored, row_ready = [sem("st0"), sem("st1")], sem("rr")
        wrow_p, turn = two("e_wrow", [P, 1], U32), sem("turn")
        block = ctx.enter_context(nc.Block())
        tables = (k.ins["L1_ffn_rg"].rearrange("e (p c) f -> (e p) (c f)", c=DC),
                  k.ins["L1_ffn_rw1"].rearrange("e (p c) f -> (e p) (c f)", c=DC),
                  k.ins["L1_ffn_rw2"].rearrange("e (p c) f -> (e p) (c f)", c=F2))
        bias_tables = (k.ins["L1_ffn_rgb"].rearrange("e (p c) -> (e p) c", c=F2),
                       k.ins["L1_ffn_rb1"].rearrange("e (p c) -> (e p) c", c=F2))
        rows_dram = k.scratch["rows"].rearrange("(j s p) d -> j p s d", s=ST, p=P)
        out_dram = k.scratch["results"].rearrange("(j s p) d -> j p s d", s=ST, p=P)
        GATHERS = 5

        def blocks_of(engine, step):
            step(0, 0)
            step(1, 1)
            with engine.Fori(0, (NBLK - 3) // 2) as i:
                for p in range(2):
                    step(i * 2 + (p + 2), p)
            for j in range(2 + (NBLK - 3) // 2 * 2, NBLK):
                step(j, j % 2)

        first = lambda j: known(j) and j < 2
        half = lambda j, p, n: j * (n // 2) - p * (n // 2)

        @block.gpsimd
        def _(pool):
            def step(j, p):
                if not first(j):
                    pool.wait_ge(w_low, j * 3 - 3)
                    pool.wait_ge(y_full, j - 1)
                pool.sem_inc(turn, 1)
                idx = bass.IndirectOffsetOnAxis(ap=wrow_p[p][:, :], axis=0)
                for dst, src in [(raw[m][p], tables[m]) for m in range(3)] + [(wb[m][p], bias_tables[m]) for m in range(2)]:
                    pool.indirect_dma_start(out=dst[:, :], out_offset=None, in_=src, in_offset=idx).then_inc(w_loaded[p], 16)

            def with_row(j, p):
                if not first(j):
                    pool.wait_ge(w_loaded[p], half(j, p, 16 * GATHERS))
                pool.tensor_copy(wrow_p[p][:, :], wrow[:, bass.ds(j, 1)]).then_inc(row_ready, 1)
                pool.wait_ge(row_ready, j + 1)
                step(j, p)

            blocks_of(pool, with_row)

        @block.sync
        def _(sp):
            def load(j, p):
                if not first(j):
                    sp.wait_ge(x_psum, j * ST - ST)
                sp.dma_start(rows[p][:, :, :], rows_dram[bass.ds(j, 1), :, :, :].rearrange("o p s d -> (o p) s d"))\
                  .then_inc(rows_loaded[p], 16)

            blocks_of(sp, load)

        @block.scalar
        def _(act):
            def split_weights(j, p):
                act.wait_ge(w_loaded[p], half(j, p, 16 * GATHERS) + 16 * GATHERS)
                for m in range(3):
                    if not first(j):
                        act.wait_ge(d_psum, j * ST - ST)
                    if m < 2:
                        src = raw[m][p][:, :].rearrange("p (c q f) -> p c f q", c=DC, f=F2)
                        dst = hi[m][p][:, :].rearrange("p (c f q) -> p c f q", c=DC, f=F2)
                    else:
                        src, dst = raw[m][p][:, :], hi[m][p][:, :]
                    act.activation(dst, src, ACT.Copy).then_inc(w_high, 1)

            def step(j, p):
                for s in range(ST):
                    act.wait_ge(x_psum, j * ST + (s + 1))
                    if s == 0 and not first(j):
                        act.wait_ge(gu_psum, j - 1)
                    act.activation(x_hi[p][:, :, s * P:(s + 1) * P], psX[s][:, :].rearrange("p (c t) -> p c t", c=DC),
                                   ACT.Copy).then_inc(x_high, 1)
                split_weights(j, p)
                act.wait_ge(gu_psum, j + 1)
                if not first(j):
                    act.wait_ge(y_full, j - 1)
                for f in range(F2):
                    last = act.activation(gf[p][:, f, :], psG[p][:, f, :], ACT.Gelu, bias=wb[0][p][:, f:f + 1])
                last.then_inc(gelu_done, 1)
                act.wait_ge(y_full, j + 1)
                act.activation(y_hi[p][:, :, :], yf[p][:, :, :], ACT.Copy).then_inc(y_high, 1)
                act.wait_ge(out_ready, j + 1)
                act.dma_start(out_dram[bass.ds(j, 1), :, :, :].rearrange("o p s d -> (o p) s d"), yo[p][:, :, :])\
                   .then_inc(stored[p], 16)

            blocks_of(act, step)
            for p in range(2):
                act.wait_ge(stored[p], 16 * ((NBLK + 1 - p) // 2))

        @block.vector
        def _(dve):
            def step(j, p):
                for s in range(ST):
                    dve.wait_ge(x_high, j * ST + (s + 1))
                    part = slice(s * P, (s + 1) * P)
                    dve.tensor_tensor(x_lo[p][:, :, part], psX[s][:, :].rearrange("p (c t) -> p c t", c=DC),
                                      x_hi[p][:, :, part], ALU.subtract).then_inc(x_low, 1)
                for m in range(3):
                    dve.wait_ge(w_high, j * 3 + (m + 1))
                    if m < 2:
                        src = raw[m][p][:, :].rearrange("p (c q f) -> p c f q", c=DC, f=F2)
                        h, l = (a[m][p][:, :].rearrange("p (c f q) -> p c f q", c=DC, f=F2) for a in (hi, lo))
                    else:
                        src, h, l = raw[m][p][:, :], hi[m][p][:, :], lo[m][p][:, :]
                    dve.tensor_tensor(l, src, h, ALU.subtract).then_inc(w_low, 1)
                dve.wait_ge(gelu_done, j + 1)
                for f in range(F2):
                    last = dve.scalar_tensor_tensor(yf[p][:, f, :], psU[p][:, f, :], wb[1][p][:, f:f + 1],
                                                    gf[p][:, f, :], ALU.add, ALU.mult)
                last.then_inc(y_full, 1)
                dve.wait_ge(y_high, j + 1)
                dve.tensor_tensor(y_lo[p][:, :, :], yf[p][:, :, :], y_hi[p][:, :, :], ALU.subtract).then_inc(y_low, 1)
                if not first(j):
                    dve.wait_ge(stored[p], half(j, p, 16))
                for s in range(ST):
                    dve.wait_ge(d_psum, j * ST + (s + 1))
                    last = dve.tensor_copy(yo[p][:, s, :], psD[s][:, :])
                last.then_inc(out_ready, 1)

            blocks_of(dve, step)

        @block.tensor
        def _(pe):
            def turn(j, p):
                pe.wait_ge(rows_loaded[p], half(j, p, 16) + 16)
                if not known(j) or j:
                    pe.wait_ge(x_low, j * ST)
                for s in range(ST):
                    for c in range(DC):
                        last = pe.transpose(psX[s][:, c * P:(c + 1) * P], rows[p][:, s, c::DC], k.ident[:, :])
                    last.then_inc(x_psum, 1)

            def up(j, p):
                pe.wait_ge(x_low, j * ST + ST)
                if not first(j):
                    pe.wait_ge(y_full, j - 1)
                for m, ps in ((0, psG), (1, psU)):
                    pe.wait_ge(w_low, j * 3 + (m + 1))
                    for f in range(F2):
                        for c in range(DC):
                            col = (c * F2 + f) * P
                            last = three_products(pe, ps[p][:, f, :], [a[m][p][:, col:col + P] for a in (hi, lo)],
                                                  [a[p][:, c, :] for a in (x_hi, x_lo)], c == 0, c == DC - 1)
                last.then_inc(gu_psum, 1)

            def down(j, p):
                pe.wait_ge(y_low, j + 1)
                pe.wait_ge(w_low, j * 3 + 3)
                if not known(j) or j:
                    pe.wait_ge(out_ready, j)
                for s in range(ST):
                    for f in range(F2):
                        last = three_products(pe, psD[s][:, :], [a[p][:, f, s * P:(s + 1) * P] for a in (y_hi, y_lo)],
                                              [a[2][p][:, f * D:(f + 1) * D] for a in (hi, lo)], f == 0, f == F2 - 1)
                    last.then_inc(d_psum, 1)

            def step(j, p):
                turn(j, p)
                up(j, p)
                down(j, p)

            blocks_of(pe, step)


def stage_combine(k, slots, share, combine, out):
    nc = k.nc
    with ExitStack() as ctx:
        sb = lambda name, shape, dt: ctx.enter_context(nc.sbuf_tensor(name, shape, dt))
        b2 = sb("m_b2", [E_N, D], F32)
        b2_hi, b2_lo = sb("m_b2hi", [E_N, D], BF16), sb("m_b2lo", [E_N, D], BF16)
        mixT_hi, mixT_lo = (sb(f"m_mix{n}", [E_N, NT, P], BF16) for n in ("h", "l"))
        got = [sb(f"m_got{i}", [P, 2, D], F32) for i in range(4)]
        psC = [ctx.enter_context(nc.psum_tensor(f"ps_mc{i}", [E_N, 4, P], F32)) for i in range(4)]
        psB = [ctx.enter_context(nc.psum_tensor(f"ps_mb{i}", [P, D], F32)) for i in range(2)]
        sem = lambda name: k.semaphore(("m_" + name))
        b_loaded, b_high, b_low, turned, mix_high, mix_low, b_psum, b_added, first_added, done = (
            sem(n) for n in ("bl", "bh", "blo", "tu", "mh", "ml", "bp", "ba", "fa", "do"))
        gathered = [sem(f"g{i}") for i in range(4)]
        stored = sem("st")
        block = ctx.enter_context(nc.Block())
        out_dram = out.rearrange("b s d -> (b s) d")

        @block.gpsimd
        def _(pool):
            for t in range(NT):
                if t >= 4:
                    pool.wait_ge(done, t - 3)
                for s in range(2):
                    pool.indirect_dma_start(out=got[t % 4][:, s, :], out_offset=None, in_=k.scratch["results"],
                                            in_offset=bass.IndirectOffsetOnAxis(ap=slots[:, s, t:t + 1], axis=0))\
                        .then_inc(gathered[t % 4], 16)

        @block.sync
        def _(sp):
            sp.dma_start(b2[:, :], k.ins["L1_ffn_rb2"]).then_inc(b_loaded, 16)
            for t in range(NT):
                sp.wait_ge(done, t + 1)
                sp.dma_start(out_dram[t * P:(t + 1) * P, :], k.x[:, t, :]).then_inc(stored, 16)
            sp.wait_ge(stored, 16 * NT)

        @block.scalar
        def _(act):
            act.wait_ge(b_loaded, 16)
            act.activation(b2_hi[:, :], b2[:, :], ACT.Copy).then_inc(b_high, 1)
            for i in range(4):
                act.wait_ge(turned, i + 1)
                act.activation(mixT_hi[:, 4 * i:4 * i + 4, :], psC[i][:, :, :], ACT.Copy).then_inc(mix_high, 1)

        @block.tensor
        def _(pe):
            for i in range(4):
                for j in range(4):
                    last = pe.transpose(psC[i][:, j, :], combine[:, 4 * i + j, :], k.ident[:, :])
                last.then_inc(turned, 1)
            pe.wait_ge(b_low, 1)
            for t in range(NT):
                pe.wait_ge(mix_low, t // 4 + 1)
                if t >= 2:
                    pe.wait_ge(b_added, t - 1)
                three_products(pe, psB[t % 2][:, :], [a[:, t, :] for a in (mixT_hi, mixT_lo)], [b2_hi[:, :], b2_lo[:, :]])\
                    .then_inc(b_psum, 1)

        @block.vector
        def _(dve):
            dve.wait_ge(b_high, 1)
            dve.tensor_tensor(b2_lo[:, :], b2[:, :], b2_hi[:, :], ALU.subtract).then_inc(b_low, 1)
            for i in range(4):
                dve.wait_ge(mix_high, i + 1)
                dve.tensor_tensor(mixT_lo[:, 4 * i:4 * i + 4, :], psC[i][:, :, :], mixT_hi[:, 4 * i:4 * i + 4, :],
                                  ALU.subtract).then_inc(mix_low, 1)
            for t in range(NT):
                x = k.x[:, t, :]
                dve.wait_ge(b_psum, t + 1)
                dve.tensor_tensor(x, x, psB[t % 2][:, :], ALU.add).then_inc(b_added, 1)
                dve.wait_ge(gathered[t % 4], 32 * (t // 4 + 1))
                dve.wait_ge(b_added, t + 1)
                dve.scalar_tensor_tensor(x, got[t % 4][:, 0, :], share[:, 0, t:t + 1], x, ALU.mult, ALU.add).then_inc(first_added, 1)
                dve.wait_ge(first_added, t + 1)
                dve.scalar_tensor_tensor(x, got[t % 4][:, 1, :], share[:, 1, t:t + 1], x, ALU.mult, ALU.add).then_inc(done, 1)


def build(nc, ins, out, scratch):
    with ExitStack() as ctx:
        k = Kernel(nc, ins, out, scratch, ctx)
        left = lambda stack, name, shape, dt: stack.enter_context(nc.sbuf_tensor(name, shape, dt))
        stage_constants(k)
        with ExitStack() as attention:
            with ExitStack() as context:
                ctxT = context.enter_context(nc.sbuf_tensor("ctxT", [P, DC, TOK], F32, side="right"))
                with ExitStack() as low:
                    k.w1T = left(low, "w1T", [P, DC * FF], BF16)
                    k.w2T = left(low, "w2T", [P, FC * D], BF16)
                    stage_ternary_weights(k)
                    mean, quant, dequant = (left(low, n, [P, NT], F32) for n in ("ffn_mean", "ffn_quant", "ffn_dequant"))
                    with ExitStack() as conv:
                        outT = left(conv, "outT", [P, DC, TOK], F32)
                        with ExitStack() as lower:
                            qT = left(lower, "qT", [P, DC, TOK], F32)
                            stage_transposes(k, ctxT, qT)
                            stage_long_conv(k, ctxT, qT, outT)
                        stage_ffn_entry(k, outT, mean, quant, dequant)
                    stage_ffn(k, mean, quant, dequant)
                k.clear_semaphores()
                ks = scratch["keys"]
                v_hi = left(attention, "v_hi", [P, NT, HEADS, VC], BF16)
                v_lo = left(attention, "v_lo", [P, NT, HEADS, VC], BF16)
                qw, ow = (left(attention, n, [P, 2, DC, D], BF16) for n in ("qw", "ow"))
                x_mean, x_rstd = (left(attention, n, [P, NT], F32) for n in ("x_mean", "x_rstd"))
                sel = left(attention, "sel", [P, 2, P], BF16)
                with ExitStack() as kv:
                    kw, vw = (left(kv, n, [P, 2, DC, D], BF16) for n in ("kw", "vw"))
                    vbias = left(kv, "vbias", [P, D], F32)
                    stage_attention_weights(k, (kw, vw, qw, ow), k.vectors, vbias, x_mean, x_rstd, sel)
                    stage_keys_values(k, ctxT, kw, vw, k.vectors, vbias, ks, v_hi, v_lo)
            stage_attention(k, ks, v_hi, v_lo, qw, ow, k.vectors, x_mean, x_rstd, sel)
        slots = left(ctx, "slots", [P, 2, NT], U32)
        share = left(ctx, "share", [P, 2, NT], F32)
        combine = left(ctx, "combine", [P, NT, E_N], F32)
        wrow = left(ctx, "wrow", [P, NBLK], U32)
        with ExitStack() as moe:
            xf = left(moe, "xf", [P, NT, D], F32)
            xT_hi, xT_lo = (left(moe, n, [P, DC, TOK], BF16) for n in ("xT_hi", "xT_lo"))
            xaff = left(moe, "xaff", [P, NT, E_N], F32)
            sgu = left(moe, "sgu", [P, 2, SH_N, 2, DC * FE], BF16)
            sd = left(moe, "sd", [P, 2, SH_N, F2 * D], BF16)
            sbias = left(moe, "sbias", [P, SH_N, D], F32)
            stage_router(k, xf, xT_hi, xT_lo, xaff)
            stage_shared_weights(k, sgu, sd, sbias)
            stage_route_and_shared(k, xf, xT_hi, xT_lo, xaff, sgu, sd, slots, share, combine, wrow)
        stage_experts(k, wrow)
        stage_combine(k, slots, share, combine, out)
        k.open_semaphores.close()


def program(nc, ins, out):
    scratch = {"taps": nc.dram_tensor("taps_padded", [H0, PAD + D], F32, kind="Internal").ap(),
               "keys": nc.dram_tensor("keys_stacked", [B, P, HC, DC, S], BF16, kind="Internal").ap(),
               "rows": nc.dram_tensor("expert_rows", [NBLK * BLK, D], F32, kind="Internal").ap(),
               "results": nc.dram_tensor("expert_results", [NBLK * BLK, D], F32, kind="Internal").ap()}
    build(nc, ins, out, scratch)


INPUTS = ["x", "ctx_2048", "L0_xattn_ssm_kernel", "L0_xattn_D", "L0_ffn_w1", "L0_ffn_b1", "L0_ffn_w2", "L0_ffn_b2",
          "L1_xattn_Wq", "L1_xattn_bq", "L1_xattn_gq", "L1_xattn_Wk_img", "L1_xattn_bk_img", "L1_xattn_gk_img",
          "L1_xattn_Wv_img", "L1_xattn_bv_img", "L1_xattn_Wo", "L1_xattn_bo", "L1_ffn_wa", "L1_ffn_rg", "L1_ffn_rgb",
          "L1_ffn_rw1", "L1_ffn_rb1", "L1_ffn_rw2", "L1_ffn_rb2", "L1_ffn_sg", "L1_ffn_sgb", "L1_ffn_sw1",
          "L1_ffn_sb1", "L1_ffn_sw2", "L1_ffn_sb2"]


def kernel(**inputs):
    import concourse.bacc as _bacc
    from concourse.bass_utils import run_bass_kernel_spmd as _run

    nc = _bacc.Bacc("TRN2", target_bir_lowering=False, num_devices=1)
    arrays, ins = {}, {}
    for name in INPUTS:
        a = np.ascontiguousarray(inputs[name])
        arrays[f"in_{name}"] = a
        ins[name] = nc.dram_tensor(f"in_{name}", a.shape, mybir.dt.from_np(a.dtype), kind="ExternalInput").ap()
    out = nc.dram_tensor("out", (B, S, D), F32, kind="ExternalOutput").ap()
    program(nc, ins, out)
    return _run(nc, [arrays], core_ids=[0]).results[0]["out"]
```

```python
from contextlib import ExitStack, contextmanager

import numpy as np

import concourse.bass as bass
from concourse import mybir
from concourse.alu_op_type import AluOpType as ALU

ACT = mybir.ActivationFunctionType
AX = mybir.AxisListType
F32 = mybir.dt.float32
BF16 = mybir.dt.bfloat16
I32 = mybir.dt.int32
U32 = mybir.dt.uint32

P = 128
B, S, D = 8, 256, 512
TOK = B * S
NT = TOK // P
DC = D // P
TPB = S // P
FF = 2048
FC = FF // P
HD0 = 8
H0 = S // HD0
PAIRS = HD0 * (HD0 + 1) // 2
PAD = 128
LN_EPS = 1e-5
ACT_EPS = 1e-5
W_EPS = 1e-8
ROUND = 12582912.0


class Link:

    def __init__(self, engine, sem):
        self.engine, self.sem, self.start, self.n, self.i, self.per = engine, sem, 0, 0, None, 0

    def at(self):
        return self.start + self.n if self.i is None else self.i * self.per + (self.start + self.n)

    def __call__(self, instruction, wait=True):
        instruction.then_inc(self.sem, 1)
        self.n += 1
        if wait:
            self.engine.wait_ge(self.sem, self.at())

    @contextmanager
    def loop(self, count, per):
        self.start, self.n, self.per = self.start + self.n, 0, per
        with self.engine.Fori(0, count) as i:
            self.i = i
            yield i
        assert self.n == per, f"{self.n} steps in the loop's body"
        self.start, self.n, self.i = self.start + count * per, 0, None


def pair_at(i):
    return i * HD0 - i * (i - 1) // 2


class Kernel:

    def __init__(self, nc, ins, out, scratch, ctx):
        self.nc, self.ins, self.out, self.scratch = nc, ins, out, scratch
        sb = lambda name, shape, dt: ctx.enter_context(nc.sbuf_tensor(name, shape, dt))
        self.x = sb("x_res", [P, NT, D], F32)
        self.ident = sb("ident", [P, P], F32)
        self.ident_b = sb("ident_b", [P, P], BF16)
        self.reverse = sb("reverse", [P, P], F32)
        self.ones = sb("ones", [P, P], F32)
        self.small = sb("small", [P, 8], F32)
        self.pow_half = sb("pow_half", [P, NT], F32)
        self.vectors = sb("vectors", [P, 24], F32)
        self.w1T = self.w2T = None
        self.open_semaphores, self.semaphores = ExitStack(), []

    def semaphore(self, name):
        self.semaphores.append(self.open_semaphores.enter_context(self.nc.semaphore(name)))
        return self.semaphores[-1]

    def clear_semaphores(self):
        used, self.semaphores = self.semaphores, []
        with self.nc.Block() as block:
            @block.gpsimd
            def _(pool):
                for s in used:
                    pool.sem_clear(s)
        self.open_semaphores.close()


def stage_constants(k):
    nc = k.nc
    with ExitStack() as ctx:
        taps = ctx.enter_context(nc.sbuf_tensor("taps", [H0, PAD + D], F32))
        forwards = ctx.enter_context(nc.sbuf_tensor("taps_forwards", [H0, D], F32))
        skip = ctx.enter_context(nc.sbuf_tensor("skip", [H0, 1], F32))
        sem = k.semaphore
        zeroed, selected = sem("c_zeroed"), sem("c_selected")
        taps_zeroed, taps_loaded, taps_ready, taps_stored = sem("c_tz"), sem("c_tl"), sem("c_tr"), sem("c_ts")
        block = ctx.enter_context(nc.Block())

        @block.gpsimd
        def _(pool):
            pool.memset(k.ident[:, :], 0.0).then_inc(zeroed, 1)
            pool.memset(k.ident_b[:, :], 0.0).then_inc(zeroed, 1)
            pool.memset(k.reverse[:, :], 0.0).then_inc(zeroed, 1)
            pool.memset(k.ones[:, :], 1.0)
            pool.memset(k.small[:, 0:3], ROUND)
            pool.memset(k.small[:, 3:4], RMS_EPS)
            pool.memset(k.pow_half[:, :], -0.5)
            pool.wait_ge(zeroed, 3)
            for m, base, step in ((k.ident, 0, -1), (k.ident_b, 0, -1), (k.reverse, 1 - P, 1)):
                pool.affine_select(out=m[:, :], in_=m[:, :], compare_op=ALU.not_equal, fill=1.0, base=base,
                                   pattern=[[step, P]], channel_multiplier=1).then_inc(selected, 1)

        @block.vector
        def _(dve):
            dve.memset(taps[:, D:], 0.0).then_inc(taps_zeroed, 1)
            dve.wait_ge(taps_loaded, 32)
            dve.tensor_copy(taps[:, D - 2::-1], forwards[:, 1:]).then_inc(taps_ready, 1)
            dve.tensor_tensor(taps[:, D - 1:D], forwards[:, 0:1], skip[:, :], ALU.add).then_inc(taps_ready, 1)

        @block.sync
        def _(sp):
            sp.dma_start(forwards[:, :], k.ins["L0_xattn_ssm_kernel"]).then_inc(taps_loaded, 16)
            sp.dma_start(skip[:, :], k.ins["L0_xattn_D"].rearrange("(h o) -> h o", o=1)).then_inc(taps_loaded, 16)
            sp.wait_ge(taps_zeroed, 1)
            sp.wait_ge(taps_ready, 2)
            sp.dma_start(k.scratch["taps"], taps[:, :]).then_inc(taps_stored, 16)
            sp.wait_ge(taps_stored, 16)


def stage_ternary_weights(k):
    nc = k.nc
    W = FF * D // P
    HALF = 1024
    with ExitStack() as ctx:
        sb = lambda name, shape, dt: ctx.enter_context(nc.sbuf_tensor(name, shape, dt))
        raw = [sb(f"w_raw{i}", [P, W], F32) for i in range(2)]
        tern = [sb(f"w_tern{i}", [P, W], BF16) for i in range(2)]
        total = sb("w_total", [P, 2], F32)
        inv = sb("w_inv", [P, 2], F32)
        ps_sum = ctx.enter_context(nc.psum_tensor("ps_sum", [P, 2], F32))
        ps_t = [ctx.enter_context(nc.psum_tensor(f"ps_wt{i}", [P, HALF], BF16)) for i in range(4)]
        sem = k.semaphore
        loaded = [sem("w_loaded0"), sem("w_loaded1")]
        abs_summed, sum_ready, inv_ready = sem("w_abs"), sem("w_sum"), sem("w_invr")
        scaled, rounded, transposed, copied = sem("w_scaled"), sem("w_rounded"), sem("w_transposed"), sem("w_copied")
        copied_even, dve_step = sem("w_copied_even"), sem("w_dve")
        block = ctx.enter_context(nc.Block())
        GROUPS = W // HALF

        def group(wi, g):
            for j in range(HALF // P):
                col = g * HALF + j * P
                if wi == 0:
                    c, a = col // FF, col % FF // P
                    yield j, a * D + c * P
                else:
                    c, a = col // D, col % D // P
                    yield j, a * FF + c * P

        @block.sync
        def _(sp):
            sp.dma_start(raw[0][:, :].rearrange("p (a n) -> p a n", n=D),
                         k.ins["L0_ffn_w1"].rearrange("(a p) n -> p a n", p=P)).then_inc(loaded[0], 16)
            sp.dma_start(raw[1][:, :].rearrange("p (a n) -> p a n", n=FF),
                         k.ins["L0_ffn_w2"].rearrange("(a p) n -> p a n", p=P)).then_inc(loaded[1], 16)

        @block.scalar
        def _(act):
            for wi in range(2):
                act.wait_ge(loaded[wi], 16)
                act.activation(tern[wi][:, :], raw[wi][:, :], ACT.Abs,
                               accum_out=total[:, wi:wi + 1]).then_inc(abs_summed, 1)
                act.wait_ge(inv_ready, wi + 1)
                act.activation(raw[wi][:, :], raw[wi][:, :], ACT.Identity, bias=k.small[:, 2:3],
                               scale=inv[:, wi:wi + 1]).then_inc(scaled, 1)
            for n in range(1, 2 * GROUPS, 2):
                act.wait_ge(transposed, n + 1)
                dst = (k.w1T, k.w2T)[n // GROUPS]
                act.activation(dst[:, n % GROUPS * HALF:(n % GROUPS + 1) * HALF], ps_t[n % 4][:, :],
                               ACT.Copy).then_inc(copied, 1)

        @block.tensor
        def _(pe):
            for wi in range(2):
                pe.wait_ge(abs_summed, wi + 1)
                pe.matmul(ps_sum[:, wi:wi + 1], k.ones[:, :], total[:, wi:wi + 1], start=True, stop=True)\
                  .then_inc(sum_ready, 1)
            for wi in range(2):
                pe.wait_ge(rounded, wi + 1)
                for g in range(GROUPS):
                    n = wi * GROUPS + g
                    if n >= 4:
                        pe.wait_ge(copied if n % 2 else copied_even, (n - 4) // 2 + 1)
                    for j, at in group(wi, g):
                        last = pe.transpose(ps_t[n % 4][:, j * P:(j + 1) * P], tern[wi][:, at:at + P],
                                            k.ident_b[:, :])
                    last.then_inc(transposed, 1)

        @block.vector
        def _(dve):
            link = Link(dve, dve_step)
            for wi in range(2):
                dve.wait_ge(sum_ready, wi + 1)
                link(dve.tensor_scalar(k.small[:, wi:wi + 1], ps_sum[:, wi:wi + 1], 1.0 / (FF * D), W_EPS,
                                       ALU.mult, ALU.max))
                dve.reciprocal(inv[:, wi:wi + 1], k.small[:, wi:wi + 1]).then_inc(inv_ready, 1)
            for wi in range(2):
                dve.wait_ge(scaled, wi + 1)
                link(dve.tensor_scalar(raw[wi][:, :], raw[wi][:, :], ROUND - 1.0, ROUND + 1.0, ALU.max, ALU.min))
                dve.tensor_scalar(tern[wi][:, :], raw[wi][:, :], ROUND, None, ALU.subtract).then_inc(rounded, 1)
                for n in range(wi * GROUPS, (wi + 1) * GROUPS, 2):
                    dve.wait_ge(transposed, n + 1)
                    dst = (k.w1T, k.w2T)[wi]
                    dve.tensor_copy(dst[:, n % GROUPS * HALF:(n % GROUPS + 1) * HALF], ps_t[n % 4][:, :])\
                       .then_inc(copied_even, 1)


def stage_transposes(k, ctxT, qT):
    nc = k.nc
    with ExitStack() as ctx:
        sb = lambda name, shape, dt: ctx.enter_context(nc.sbuf_tensor(name, shape, dt))
        c_in = [sb(f"c_in{i}", [P, D], F32) for i in range(4)]
        xn = [sb(f"xn{i}", [P, D], F32) for i in range(4)]
        stats = sb("t_stats", [P, NT, 6], F32)
        mean = sb("t_mean", [P, NT], F32)
        var = sb("t_var", [P, NT], F32)
        diff = sb("t_diff", [P, NT], F32)
        rstd = sb("t_rstd", [P, NT], F32)
        ps = [ctx.enter_context(nc.psum_tensor(f"ps_tr{i}", [P, D], F32)) for i in range(4)]
        sem = k.semaphore
        x_loaded = [sem(f"t_x{i}") for i in range(4)]
        c_loaded = [sem(f"t_c{i}") for i in range(4)]
        c_used, transposed, evacuated = sem("t_cused"), sem("t_transposed"), sem("t_evac")
        var_ready, rstd_ready, xn_ready, xn_used, dve_step = sem("t_var"), sem("t_rstd"), sem("t_xn"), sem("t_xnused"), sem("t_dve")
        block = ctx.enter_context(nc.Block())
        c_dram = k.ins["ctx_2048"].rearrange("b s d -> (b s) d")
        x_dram = k.ins["x"].rearrange("b s d -> (b s) d").rearrange("(t p) d -> p t d", p=P)

        @block.sync
        def _(sp):
            for i in range(4):
                sp.dma_start(k.x[:, 4 * i:4 * i + 4, :], x_dram[:, 4 * i:4 * i + 4, :]).then_inc(x_loaded[i], 16)
            with sp.Fori(0, NT // 4) as i:
                for j in range(4):
                    sp.wait_ge(c_used, i * 4 + (j + 1))
                    sp.dma_start(c_in[j][:, :], c_dram[bass.ds(i * (4 * P) + j * P, P), :]).then_inc(c_loaded[j], 16)

        @block.tensor
        def _(pe):
            pe.sem_inc(c_used, 4)
            pe.sem_inc(xn_used, 4)
            with pe.Fori(0, NT // 4) as i:
                for j in range(4):
                    pe.wait_ge(c_loaded[j], i * 16 + 16)
                    pe.wait_ge(evacuated, i * 4 + (j + 1))
                    for c in range(DC):
                        last = pe.transpose(ps[j][:, c * P:(c + 1) * P], c_in[j][:, c * P:(c + 1) * P], k.ident[:, :])
                    last.then_inc(transposed, 1)
                    pe.wait_ge(transposed, i * 4 + (j + 1))
                    pe.sem_inc(c_used, 1)
            with pe.Fori(0, NT // 4) as i:
                for j in range(4):
                    pe.wait_ge(xn_ready, i * 4 + (j + 1))
                    pe.wait_ge(evacuated, i * 4 + (NT + j + 1))
                    for c in range(DC):
                        last = pe.transpose(ps[j][:, c * P:(c + 1) * P], xn[j][:, (DC - 1 - c) * P:(DC - c) * P], k.ident[:, :])
                    last.then_inc(transposed, 1)

        @block.scalar
        def _(act):
            act.sem_inc(evacuated, 4)
            for n, dst in enumerate((ctxT, qT)):
                with act.Fori(0, NT // 4) as i:
                    for j in range(4):
                        act.wait_ge(transposed, i * 4 + (NT * n + j + 1))
                        act.activation(dst[:, :, bass.ds(i * (4 * P) + j * P, P)],
                                       ps[j][:, :].rearrange("p (c t) -> p c t", c=DC), ACT.Copy).then_inc(evacuated, 1)

        @block.vector
        def _(dve):
            link = Link(dve, dve_step)
            for i in range(4):
                dve.wait_ge(x_loaded[i], 16)
                for t in range(4 * i, 4 * i + 4):
                    link(dve.bn_stats(stats[:, t, :], k.x[:, t, :]), wait=False)
            dve.wait_ge(dve_step, NT)
            link(dve.tensor_tensor(mean[:, :], stats[:, :, 1], stats[:, :, 4], ALU.add))
            link(dve.tensor_scalar(mean[:, :], mean[:, :], 0.5, None, ALU.mult))
            link(dve.tensor_tensor(diff[:, :], stats[:, :, 1], stats[:, :, 4], ALU.subtract))
            link(dve.tensor_tensor(diff[:, :], diff[:, :], diff[:, :], ALU.mult))
            link(dve.tensor_tensor(var[:, :], stats[:, :, 2], stats[:, :, 5], ALU.add))
            link(dve.tensor_scalar(var[:, :], var[:, :], 1.0 / D, LN_EPS, ALU.mult, ALU.add))
            link(dve.scalar_tensor_tensor(var[:, :], diff[:, :], 0.25, var[:, :], ALU.mult, ALU.add))
            dve.sem_inc(var_ready, 1)
            dve.wait_ge(rstd_ready, 1)
            with dve.Fori(0, NT // 4) as i:
                for j in range(4):
                    dve.wait_ge(transposed, i * 4 + (NT + j - 3))
                    t = bass.ds(i * 4 + j, 1)
                    dve.tensor_scalar(xn[j][:, ::-1], k.x[:, t, :], mean[:, t], rstd[:, t], ALU.subtract, ALU.mult)\
                       .then_inc(xn_ready, 1)

        @block.gpsimd
        def _(pool):
            pool.wait_ge(var_ready, 1)
            pool.tensor_tensor(rstd[:, :], var[:, :], k.pow_half[:, :], ALU.pow).then_inc(rstd_ready, 1)


def stage_long_conv(k, ctxT, qT, outT):
    nc = k.nc
    BP = B * PAIRS
    with ExitStack() as ctx:
        sb = lambda name, shape, dt: ctx.enter_context(nc.sbuf_tensor(name, shape, dt))
        toep = [sb(f"toep{i}", [P, D], F32) for i in range(2)]
        kv = [sb(f"kv{i}", [P, DC, B, PAIRS], F32) for i in range(2)]
        prod = [sb(f"prod{i}", [P, DC, B, HD0, HD0], F32) for i in range(2)]
        Y = [ctx.enter_context(nc.psum_tensor(f"ps_y{i}", [P, DC, 512], F32)) for i in range(2)]
        sem = k.semaphore
        toep_loaded = [sem("a_toep0"), sem("a_toep1")]
        kv_ready, conv_done, y_read, prod_ready, reduced = (sem(f"a_{n}") for n in ("kv", "conv", "yread", "prod", "red"))
        block = ctx.enter_context(nc.Block())
        taps = k.scratch["taps"]
        ctx4 = ctxT[:, :, :].rearrange("p c (b s) -> p c b s", b=B)
        q4 = qT[:, :, :].rearrange("p c (b s) -> p c b s", b=B)
        o4 = outT[:, :, :].rearrange("p c (b s) -> p c b s", b=B)

        @block.sync
        def _(sp):
            with sp.Fori(0, H0 // 2) as i:
                for p in range(2):
                    sp.wait_ge(conv_done, i * 2 + (p + 1))
                    row = taps[bass.ds(i * 2 + p, 1), 0:D]
                    src = bass.AP(tensor=row.tensor, offset=row.offset, ap=[[1, P], [1, D]])
                    sp.dma_start(toep[p][:, :], src).then_inc(toep_loaded[p], 16)

        @block.gpsimd
        def _(pool):
            with pool.Fori(0, H0 // 2) as i:
                for p in range(2):
                    pool.wait_ge(conv_done, i * 2 + (p + 1))
                    for c in range(HD0):
                        n = HD0 - c
                        at = i * (2 * HD0) + (p * HD0 + c)
                        last = pool.tensor_tensor(kv[p][:, :, :, pair_at(c):pair_at(c) + n],
                                                  ctx4[:, :, :, bass.ds(at, 1)].broadcast_to([P, DC, B, n]),
                                                  ctx4[:, :, :, bass.ds(at, n)], ALU.mult)
                    last.then_inc(kv_ready, 1)

        @block.tensor
        def _(pe):
            pe.sem_inc(conv_done, 2)
            with pe.Fori(0, H0 // 2) as i:
                for p in range(2):
                    pe.wait_ge(toep_loaded[p], i * 16 + 16)
                    pe.wait_ge(kv_ready, i * 2 + (p + 1))
                    pe.wait_ge(y_read, i * 2 + (p + 1))
                    for l in range(DC):
                        for m in range(l + 1):
                            last = pe.matmul(Y[p][:, l, 0:BP], toep[p][:, (DC - 1 - l + m) * P:(DC - l + m) * P],
                                             kv[p][:, m, :, :].rearrange("p b n -> p (b n)"),
                                             start=(m == 0), stop=(m == l))
                    last.then_inc(conv_done, 1)

        @block.vector
        def _(dve):
            dve.sem_inc(y_read, 2)
            with dve.Fori(0, H0 // 2) as i:
                for p in range(2):
                    dve.wait_ge(conv_done, i * 2 + (p + 3))
                    y = Y[p][:, :, 0:BP].rearrange("p c (b n) -> p c b n", b=B)
                    for c in range(HD0):
                        n = HD0 - c
                        at = i * (2 * HD0) + (p * HD0 + c)
                        dve.tensor_tensor(prod[p][:, :, :, c:, c], y[:, :, :, pair_at(c):pair_at(c) + n],
                                          q4[:, :, :, bass.ds(at, 1)].broadcast_to([P, DC, B, n]), ALU.mult)\
                           .then_inc(prod_ready, 1)
                        if n > 1:
                            last = dve.tensor_tensor(prod[p][:, :, :, c, c + 1:],
                                                     y[:, :, :, pair_at(c) + 1:pair_at(c) + n],
                                                     q4[:, :, :, bass.ds(at + 1, n - 1)], ALU.mult)
                            last.then_inc(prod_ready, 1)
                    per = 2 * HD0 - 1
                    dve.wait_ge(prod_ready, i * (2 * per) + (p + 1) * per)
                    dve.sem_inc(y_read, 1)
                    dve.tensor_reduce(o4[:, :, :, bass.ds(i * (2 * HD0) + p * HD0, HD0)], prod[p][:, :, :, :, :],
                                      AX.X, ALU.add).then_inc(reduced, 1)


def mean_var(link, dve, stats, mean, var, tmp, eps):
    link(dve.tensor_tensor(mean, stats[:, :, 1], stats[:, :, 4], ALU.add))
    link(dve.tensor_scalar(mean, mean, 0.5, None, ALU.mult))
    link(dve.tensor_tensor(tmp, stats[:, :, 1], stats[:, :, 4], ALU.subtract))
    link(dve.tensor_tensor(tmp, tmp, tmp, ALU.mult))
    link(dve.tensor_tensor(var, stats[:, :, 2], stats[:, :, 5], ALU.add))
    link(dve.tensor_scalar(var, var, 1.0 / D, eps, ALU.mult, ALU.add))
    link(dve.scalar_tensor_tensor(var, tmp, 0.25, var, ALU.mult, ALU.add))


def stage_ffn_entry(k, outT, mean, quant, dequant):
    nc = k.nc
    with ExitStack() as ctx:
        sb = lambda name, shape, dt: ctx.enter_context(nc.sbuf_tensor(name, shape, dt))
        part = [sb(f"e_part{i}", [P, DC, P], F32) for i in range(4)]
        stats = sb("e_stats", [P, NT, 6], F32)
        hi, lo, var, tmp, r1, r2 = (sb(f"e_{n}", [P, NT], F32) for n in ("hi", "lo", "var", "tmp", "r1", "r2"))
        ps = [ctx.enter_context(nc.psum_tensor(f"ps_e{i}", [P, D], F32)) for i in range(4)]
        sem = k.semaphore
        staged, transposed, added, seen, dve_step, var_ready, r_ready = (
            sem(f"e_{n}") for n in ("staged", "transposed", "added", "seen", "dve", "varr", "rr"))
        block = ctx.enter_context(nc.Block())

        @block.gpsimd
        def _(pool):
            with pool.Fori(0, NT // 4) as i:
                for j in range(4):
                    pool.wait_ge(transposed, i * 4 + (j + 1))
                    pool.tensor_copy(part[j][:, :, :], outT[:, :, bass.ds(i * (4 * P) + j * P, P)]).then_inc(staged, 1)
            for n, r in enumerate((r1, r2)):
                pool.wait_ge(var_ready, n + 1)
                pool.tensor_tensor(r[:, :], var[:, :], k.pow_half[:, :], ALU.pow).then_inc(r_ready, 1)

        @block.tensor
        def _(pe):
            pe.sem_inc(transposed, 4)
            with pe.Fori(0, NT // 4) as i:
                for j in range(4):
                    pe.wait_ge(staged, i * 4 + (j + 1))
                    pe.wait_ge(added, i * 4 + (j + 1))
                    for c in range(DC):
                        last = pe.matmul(ps[j][:, c * P:(c + 1) * P], part[j][:, c, :], k.reverse[:, :], start=True, stop=True)
                    last.then_inc(transposed, 1)

        @block.vector
        def _(dve):
            link = Link(dve, dve_step)
            dve.sem_inc(added, 4)
            with dve.Fori(0, NT // 4) as i:
                for j in range(4):
                    t = bass.ds(i * 4 + j, 1)
                    dve.wait_ge(transposed, i * 4 + (j + 5))
                    dve.tensor_tensor(k.x[:, t, :], k.x[:, t, :], ps[j][:, :].unsqueeze(1), ALU.add).then_inc(added, 1)
                    dve.wait_ge(added, i * 4 + (j + 5))
                    dve.bn_stats(stats[:, t, :], k.x[:, t, :]).then_inc(seen, 1)
                    dve.tensor_reduce(hi[:, t], k.x[:, t, :], AX.X, ALU.max).then_inc(seen, 1)
                    dve.tensor_reduce(lo[:, t], k.x[:, t, :], AX.X, ALU.min).then_inc(seen, 1)
            dve.wait_ge(seen, 3 * NT)
            mean_var(link, dve, stats, mean[:, :], var[:, :], tmp[:, :], LN_EPS)
            dve.sem_inc(var_ready, 1)
            link(dve.tensor_tensor(hi[:, :], hi[:, :], mean[:, :], ALU.subtract))
            link(dve.tensor_tensor(lo[:, :], mean[:, :], lo[:, :], ALU.subtract))
            link(dve.tensor_tensor(hi[:, :], hi[:, :], lo[:, :], ALU.max))
            dve.wait_ge(r_ready, 1)
            link(dve.tensor_scalar(tmp[:, :], var[:, :], LN_EPS, None, ALU.subtract))
            link(dve.tensor_tensor(tmp[:, :], tmp[:, :], r1[:, :], ALU.mult))
            link(dve.tensor_tensor(tmp[:, :], tmp[:, :], r1[:, :], ALU.mult))
            link(dve.tensor_scalar(var[:, :], tmp[:, :], LN_EPS, None, ALU.add))
            dve.sem_inc(var_ready, 1)
            dve.wait_ge(r_ready, 2)
            link(dve.tensor_tensor(r1[:, :], r1[:, :], r2[:, :], ALU.mult))
            link(dve.tensor_tensor(hi[:, :], hi[:, :], r1[:, :], ALU.mult))
            link(dve.tensor_scalar(hi[:, :], hi[:, :], ACT_EPS, None, ALU.max))
            link(dve.reciprocal(tmp[:, :], hi[:, :]))
            link(dve.tensor_tensor(tmp[:, :], tmp[:, :], r1[:, :], ALU.mult))
            link(dve.tensor_scalar(quant[:, :], tmp[:, :], 127.0, None, ALU.mult))
            link(dve.tensor_scalar(dequant[:, :], hi[:, :], 1.0 / 127.0, k.small[:, 0:1], ALU.mult, ALU.mult))


def stage_ffn(k, mean, quant, dequant):
    nc = k.nc
    with ExitStack() as ctx:
        sb = lambda name, shape, dt: ctx.enter_context(nc.sbuf_tensor(name, shape, dt))
        b1 = sb("f_b1", [P, FF], F32)
        b2 = sb("f_b2", [P, D], F32)
        scaled = [sb(f"f_scaled{i}", [P, D], F32) for i in range(2)]
        qa = [sb(f"f_qa{i}", [P, D], BF16) for i in range(2)]
        qaT = [sb(f"f_qaT{i}", [P, DC, P], BF16) for i in range(2)]
        h = [sb(f"f_h{i}", [P, FF], F32) for i in range(2)]
        qb = [sb(f"f_qb{i}", [P, FF], BF16) for i in range(2)]
        qbT = [sb(f"f_qbT{i}", [P, FC, P], BF16) for i in range(2)]
        stats = [sb(f"f_stats{i}", [P, DC, 6], F32) for i in range(2)]
        mv = [sb(f"f_mv{i}", [P, 2], F32) for i in range(2)]
        NEG_MEAN, VAR, RSTD, AMAX, INV, QUANT, DEQUANT = range(7)
        sc = [sb(f"f_sc{i}", [P, 7], F32) for i in range(2)]
        col = lambda p, c: sc[p][:, c:c + 1]
        psT = ctx.enter_context(nc.psum_tensor("ps_fT", [P, DC, P], BF16))
        psH = [ctx.enter_context(nc.psum_tensor(f"ps_fH{i}", [P, 512], F32)) for i in range(DC)]
        psQ = [ctx.enter_context(nc.psum_tensor(f"ps_fQ{i}", [P, 8, P], BF16)) for i in range(2)]
        psY = ctx.enter_context(nc.psum_tensor("ps_fY", [P, D], F32))
        sem = lambda name: k.semaphore(("f_" + name))
        b_loaded, dve_step, aggregate_turn, zeros_set, zeroed = (sem(n) for n in ("bload", "dve", "aggr", "zs", "zd"))
        zeros = sb("f_zeros", [P, 2 * D], F32)
        qa_ready, qaT_psum, qaT_ready, h_psum, hb_ready, gelu_done = (
            sem(n) for n in ("qa", "qaTp", "qaT", "hp", "hb", "gelu"))
        stat_ready, rstd_ready, centred, quant_ready, h_scaled, qb_ready = (
            sem(n) for n in ("stat", "rstd", "cent", "quant", "hsc", "qb"))
        qbT_psum, qbT_ready, y_psum, y_added, biased = (sem(n) for n in ("qbTp", "qbT", "yp", "ya", "biased"))
        block = ctx.enter_context(nc.Block())
        tile = lambda t: k.x[:, bass.ds(t, 1), :]
        one = lambda a, t: a[:, bass.ds(t, 1)]

        known = lambda n: isinstance(n, int)
        runs = lambda n, ahead: not known(n) or 0 <= n + ahead < NT

        @block.sync
        def _(sp):
            for dst, name, n in ((b1, "L0_ffn_b1", FF), (b2, "L0_ffn_b2", D)):
                src = k.ins[name]
                sp.dma_start(dst[:, :], bass.AP(tensor=src.tensor, offset=0, ap=[[0, P], [1, n]])).then_inc(b_loaded, 16)
            sp.wait_ge(zeros_set, 1)
            rows = k.scratch["rows"].rearrange("(j p) d -> j p d", p=2 * P)
            with sp.Fori(0, NBLK * BLK // (2 * P)) as i:
                sp.dma_start(rows[bass.ds(i, 1), :, :].rearrange("o (p s) d -> (o p) (s d)", s=2), zeros[:, :]).then_inc(zeroed, 16)
            sp.wait_ge(zeroed, 16 * (NBLK * BLK // (2 * P)))

        @block.vector
        def _(dve):
            link = Link(dve, dve_step)
            dve.wait_ge(b_loaded, 32)

            def quantise_x(t, p):
                if not known(t) or t >= 2:
                    dve.wait_ge(qaT_psum, t - 1)
                link(dve.tensor_scalar(scaled[p][:, :], tile(t), one(mean, t), one(quant, t), ALU.subtract, ALU.mult))
                dve.tensor_scalar(qa[p][:, :], scaled[p][:, :], ROUND, ROUND, ALU.add, ALU.subtract).then_inc(qa_ready, 1)

            def add_bias1(t, p):
                dve.wait_ge(h_psum, t + 1)
                if not known(t) or t >= 2:
                    dve.wait_ge(qb_ready, t - 1)
                for c in range(DC):
                    dve.scalar_tensor_tensor(h[p][:, c * 512:(c + 1) * 512], psH[c][:, :], one(dequant, t),
                                             b1[:, c * 512:(c + 1) * 512], ALU.mult, ALU.add).then_inc(hb_ready, 1)

            def statistics(t, p):
                dve.wait_ge(gelu_done, t + 1)
                for c in range(DC):
                    link(dve.bn_stats(stats[p][:, c, :], h[p][:, c * 512:(c + 1) * 512]), wait=c == DC - 1)
                dve.sem_inc(aggregate_turn, 1)
                link(dve.bn_aggr(mv[p][:, :], stats[p][:, :, :]))
                dve.tensor_scalar(col(p, NEG_MEAN), mv[p][:, 0:1], -1.0, None, ALU.mult).then_inc(stat_ready, 1)
                dve.tensor_scalar(col(p, VAR), mv[p][:, 1:2], LN_EPS, None, ALU.add).then_inc(stat_ready, 1)

            def scale_of(t, p):
                dve.wait_ge(centred, t + 1)
                link(dve.tensor_reduce(col(p, AMAX), h[p][:, :], AX.X, ALU.max, apply_absolute_value=True))
                dve.wait_ge(rstd_ready, t + 1)
                link(dve.tensor_scalar(col(p, AMAX), col(p, AMAX), col(p, RSTD), ACT_EPS, ALU.mult, ALU.max))
                link(dve.reciprocal(col(p, INV), col(p, AMAX)))
                dve.tensor_scalar(col(p, QUANT), col(p, INV), 127.0, col(p, RSTD), ALU.mult, ALU.mult).then_inc(quant_ready, 1)
                link(dve.tensor_scalar(col(p, DEQUANT), col(p, AMAX), 1.0 / 127.0, k.small[:, 1:2], ALU.mult, ALU.mult), wait=False)

            def round_h(t, p):
                dve.wait_ge(h_scaled, t + 1)
                dve.tensor_scalar(qb[p][:, :], h[p][:, :], ROUND, None, ALU.subtract).then_inc(qb_ready, 1)

            def add_y(t, p):
                dve.wait_ge(y_psum, t + 1)
                dve.wait_ge(biased, t + 1)
                dve.scalar_tensor_tensor(tile(t), psY[:, :].unsqueeze(1), col(p, DEQUANT), tile(t), ALU.mult, ALU.add)\
                   .then_inc(y_added, 1)

            def step(n, p):
                if runs(n, 0):
                    add_bias1(n, p)
                if runs(n, -1):
                    scale_of(n - 1, 1 - p)
                if runs(n, 0):
                    statistics(n, p)
                if runs(n, 2):
                    quantise_x(n + 2, p)
                if runs(n, -2):
                    add_y(n - 2, p)
                if runs(n, -1):
                    round_h(n - 1, 1 - p)

            quantise_x(0, 0)
            quantise_x(1, 1)
            step(0, 0)
            step(1, 1)
            with link.loop((NT - 4) // 2, 20) as i:
                for p in range(2):
                    step(i * 2 + (p + 2), p)
            for n in range(NT - 2, NT + 2):
                step(n, n % 2)

        @block.scalar
        def _(act):
            def copy_qaT(t, p):
                act.wait_ge(qaT_psum, t + 1)
                act.activation(qaT[p][:, :, :], psT[:, :, :], ACT.Copy).then_inc(qaT_ready, 1)

            def gelu(t, p):
                act.wait_ge(hb_ready, t * 4 + 4)
                act.activation(h[p][:, :], h[p][:, :], ACT.Gelu).then_inc(gelu_done, 1)

            def centre(t, p):
                act.wait_ge(stat_ready, t * 2 + 2)
                act.activation(h[p][:, :], h[p][:, :], ACT.Identity, bias=col(p, NEG_MEAN)).then_inc(centred, 1)

            def scale(t, p):
                act.wait_ge(quant_ready, t + 1)
                act.activation(h[p][:, :], h[p][:, :], ACT.Identity, bias=k.small[:, 2:3],
                               scale=col(p, QUANT)).then_inc(h_scaled, 1)

            def copy_qbT(t, p):
                for g in range(2):
                    act.wait_ge(qbT_psum, t * 2 + (g + 1))
                    act.activation(qbT[p][:, 8 * g:8 * g + 8, :], psQ[g][:, :, :], ACT.Copy).then_inc(qbT_ready, 1)

            def step(n, p):
                if runs(n, 0):
                    gelu(n, p)
                if runs(n, -1):
                    scale(n - 1, 1 - p)
                if runs(n, 0):
                    centre(n, p)
                if runs(n, 2):
                    copy_qaT(n + 2, p)
                if runs(n, -1):
                    copy_qbT(n - 1, 1 - p)

            copy_qaT(0, 0)
            copy_qaT(1, 1)
            step(0, 0)
            step(1, 1)
            with act.Fori(0, (NT - 4) // 2) as i:
                for p in range(2):
                    step(i * 2 + (p + 2), p)
            for n in range(NT - 2, NT + 1):
                step(n, n % 2)

        @block.gpsimd
        def _(pool):
            pool.memset(zeros[:, :], 0.0).then_inc(zeros_set, 1)
            pool.wait_ge(b_loaded, 32)

            def add_bias2(t, p):
                pool.wait_ge(qa_ready, t + 1)
                pool.tensor_tensor(tile(t), tile(t), b2[:, :].unsqueeze(1), ALU.add).then_inc(biased, 1)

            def step(n, p):
                pool.wait_ge(stat_ready, n * 2 + 2)
                pool.tensor_tensor(col(p, RSTD), col(p, VAR), k.pow_half[:, 0:1], ALU.pow).then_inc(rstd_ready, 1)
                if runs(n, 2):
                    add_bias2(n + 2, p)

            add_bias2(0, 0)
            add_bias2(1, 1)
            with pool.Fori(0, NT // 2 - 1) as i:
                for p in range(2):
                    step(i * 2 + p, p)
            for n in range(NT - 2, NT):
                step(n, n % 2)

        @block.tensor
        def _(pe):
            def transpose_qa(t, p):
                pe.wait_ge(qa_ready, t + 1)
                if not known(t) or t:
                    pe.wait_ge(qaT_ready, t)
                for c in range(DC):
                    last = pe.transpose(psT[:, c, :], qa[p][:, c * P:(c + 1) * P], k.ident_b[:, :])
                last.then_inc(qaT_psum, 1)

            def up(t, p):
                pe.wait_ge(qaT_ready, t + 1)
                if not known(t) or t:
                    pe.wait_ge(hb_ready, t * 4)
                for f in range(DC):
                    for c in range(DC):
                        last = pe.matmul(psH[f][:, :], qaT[p][:, c, :], k.w1T[:, c * FF + f * 512:c * FF + (f + 1) * 512],
                                         start=(c == 0), stop=(c == DC - 1))
                last.then_inc(h_psum, 1)

            def transpose_qb(t, p):
                pe.wait_ge(qb_ready, t + 1)
                for g in range(2):
                    if not known(t) or t:
                        pe.wait_ge(qbT_ready, t * 2 + (g - 1))
                    for c in range(8):
                        last = pe.transpose(psQ[g][:, c, :], qb[p][:, (8 * g + c) * P:(8 * g + c + 1) * P], k.ident_b[:, :])
                    last.then_inc(qbT_psum, 1)

            def down(t, p):
                pe.wait_ge(qbT_ready, t * 2 + 2)
                if not known(t) or t:
                    pe.wait_ge(y_added, t)
                for c in range(FC):
                    last = pe.matmul(psY[:, :], qbT[p][:, c, :], k.w2T[:, c * D:(c + 1) * D],
                                     start=(c == 0), stop=(c == FC - 1))
                last.then_inc(y_psum, 1)

            def step(n, p):
                if runs(n, 1):
                    up(n + 1, 1 - p)
                if runs(n, 2):
                    transpose_qa(n + 2, p)
                if runs(n, -1):
                    transpose_qb(n - 1, 1 - p)
                    down(n - 1, 1 - p)

            transpose_qa(0, 0)
            transpose_qa(1, 1)
            up(0, 0)
            step(0, 0)
            step(1, 1)
            with pe.Fori(0, (NT - 4) // 2) as i:
                for p in range(2):
                    step(i * 2 + (p + 2), p)
            for n in range(NT - 2, NT + 1):
                step(n, n % 2)


RMS_EPS = 1e-6
HEADS, HD = 16, 32
HC = P // HD
UNITS = HEADS // 2
VC = HD + 1
ROWS = {"bq": 0, "gq": 4, "bk": 8, "gk": 12, "sgb": 16, "sb1": 20}
SCORE_SCALE = float(HD) ** -0.5


def broadcast_rows(src, n):
    return bass.AP(tensor=src.tensor, offset=0, ap=[[0, P], [1, n]])


def known(n):
    return isinstance(n, int)


def three_products(pe, out, stationary, moving, first=True, last=True):
    for n, (a, b) in enumerate(((0, 0), (0, 1), (1, 0))):
        instruction = pe.matmul(out, stationary[a], moving[b], start=first and n == 0, stop=last and n == 2)
    return instruction


def stage_attention_weights(k, split, vectors, vbias, x_mean, x_rstd, sel):
    nc = k.nc
    names = ("L1_xattn_Wk_img", "L1_xattn_Wv_img", "L1_xattn_Wq", "L1_xattn_Wo")
    with ExitStack() as ctx:
        sb = lambda name, shape, dt: ctx.enter_context(nc.sbuf_tensor(name, shape, dt))
        raw = [sb(f"aw_raw{i}", [P, DC, D], F32) for i in range(2)]
        rows = sb("aw_rows", [P, P], F32)
        stats = sb("aw_stats", [P, NT, 6], F32)
        var, tmp = (sb(f"aw_{n}", [P, NT], F32) for n in ("var", "tmp"))
        ps = ctx.enter_context(nc.psum_tensor("ps_aw", [P, P], F32))
        sem = lambda name: k.semaphore(("w2_" + name))
        loaded = [sem("load0"), sem("load1")]
        high_ready, low_ready, rows_zeroed, rows_loaded, rows_turned, dve_step, b_loaded = (
            sem(n) for n in ("high", "low", "rz", "rl", "rt", "dve", "bl"))
        stat_done, var_ready, sel_set = (sem(n) for n in ("stat", "var", "sel"))
        block = ctx.enter_context(nc.Block())

        @block.sync
        def _(sp):
            for n, name in enumerate(names):
                if n >= 2:
                    sp.wait_ge(low_ready, n - 1)
                sp.dma_start(raw[n % 2][:, :, :], k.ins[name].rearrange("(c p) n -> p c n", p=P)).then_inc(loaded[n % 2], 16)
            sp.dma_start(vbias[:, :], broadcast_rows(k.ins["L1_xattn_bv_img"], D)).then_inc(b_loaded, 16)
            sp.wait_ge(rows_zeroed, 1)
            for at, name in (("bq", "L1_xattn_bq"), ("gq", "L1_xattn_gq"), ("bk", "L1_xattn_bk_img"), ("gk", "L1_xattn_gk_img")):
                sp.dma_start(rows[ROWS[at]:ROWS[at] + DC, :], k.ins[name].rearrange("(c p) -> c p", p=P)).then_inc(rows_loaded, 16)
            for at, name in (("sgb", "L1_ffn_sgb"), ("sb1", "L1_ffn_sb1")):
                for e in range(2):
                    at_e = ROWS[at] + 2 * e
                    sp.dma_start(rows[at_e:at_e + 2, :], k.ins[name][e, :].rearrange("(c p) -> c p", p=P)).then_inc(rows_loaded, 16)
            sp.wait_ge(b_loaded, 16)

        @block.gpsimd
        def _(pool):
            pool.memset(rows[:, :], 0.0).then_inc(rows_zeroed, 1)
            pool.memset(sel[:, :, :], 1.0).then_inc(sel_set, 1)
            for j in range(2):
                pool.wait_ge(sel_set, 1 + 2 * j)
                pool.affine_select(out=sel[:, j, :], in_=sel[:, j, :], compare_op=ALU.is_ge, fill=0.0,
                                   base=-2 * j, pattern=[[0, P]], channel_multiplier=1).then_inc(sel_set, 1)
                pool.wait_ge(sel_set, 2 + 2 * j)
                pool.affine_select(out=sel[:, j, :], in_=sel[:, j, :], compare_op=ALU.is_ge, fill=0.0,
                                   base=2 * j + 1, pattern=[[0, P]], channel_multiplier=-1).then_inc(sel_set, 1)
            pool.wait_ge(var_ready, 1)
            pool.tensor_tensor(x_rstd[:, :], var[:, :], k.pow_half[:, :], ALU.pow)

        @block.scalar
        def _(act):
            for n in range(4):
                act.wait_ge(loaded[n % 2], 16 * (n // 2 + 1))
                act.activation(split[n][:, 0, :, :], raw[n % 2][:, :, :], ACT.Copy).then_inc(high_ready, 1)

        @block.tensor
        def _(pe):
            pe.wait_ge(rows_loaded, 16 * 8)
            pe.transpose(ps[:, :], rows[:, :], k.ident[:, :]).then_inc(rows_turned, 1)

        @block.vector
        def _(dve):
            link = Link(dve, dve_step)
            for t in range(NT):
                dve.bn_stats(stats[:, t, :], k.x[:, t, :]).then_inc(stat_done, 1)
            dve.wait_ge(stat_done, NT)
            mean_var(link, dve, stats, x_mean[:, :], var[:, :], tmp[:, :], LN_EPS)
            dve.sem_inc(var_ready, 1)
            for n in range(4):
                dve.wait_ge(high_ready, n + 1)
                dve.tensor_tensor(split[n][:, 1, :, :], raw[n % 2][:, :, :], split[n][:, 0, :, :], ALU.subtract).then_inc(low_ready, 1)
            dve.wait_ge(rows_turned, 1)
            dve.tensor_copy(vectors[:, :], ps[:, 0:vectors.shape[1]])


def square_sums(pe, k, out, sq):
    for t in range(TPB):
        for c in range(DC):
            last = pe.matmul(out[:, t:t + 1], sq[:, c, t * P:(t + 1) * P], k.ones[:, 0:1], start=(c == 0), stop=(c == DC - 1))
    return last


def spread_on_diagonals(dve, k, diag, r):
    for t in range(TPB):
        last = dve.tensor_scalar(diag[:, t, :], k.ident[:, :], r[:, t:t + 1], None, ALU.mult)
    return last


KEY_INCS = 16 * 4
STACK_INCS = 16 * HC * 4


def stage_keys_values(k, ctxT, kw, vw, vectors, vbias, ks, v_hi, v_lo):
    nc = k.nc
    with ExitStack() as ctx:
        sb = lambda name, shape, dt: ctx.enter_context(nc.sbuf_tensor(name, shape, dt))
        c_hi = [sb(f"kv_chi{i}", [P, DC, S], BF16) for i in range(2)]
        c_lo = [sb(f"kv_clo{i}", [P, DC, S], BF16) for i in range(2)]
        u = [sb(f"kv_u{i}", [P, DC, S], F32) for i in range(2)]
        sq = sb("kv_sq", [P, DC, S], F32)
        v, r = (sb(f"kv_{n}", [P, TPB], F32) for n in ("v", "r"))
        diag = sb("kv_diag", [P, TPB, P], F32)
        kn = sb("kv_kn", [P, DC, S], F32)
        k_hi = [sb(f"kv_khi{i}", [P, DC, S], BF16) for i in range(2)]
        k_lo = [sb(f"kv_klo{i}", [P, DC, S], BF16) for i in range(2)]
        vf = [sb(f"kv_vf{i}", [P, D], F32) for i in range(2)]
        psK = [ctx.enter_context(nc.psum_tensor(f"ps_k{i}", [P, 2, S], F32)) for i in range(2)]
        psV = [ctx.enter_context(nc.psum_tensor(f"ps_v{i}", [P, D], F32)) for i in range(2)]
        psR = ctx.enter_context(nc.psum_tensor("ps_r", [P, 2, S], F32))
        sem = lambda name: k.semaphore(("k_" + name))
        c_high, c_low, k_psum, v_psum, squared, sum_psum, var_ready, r_ready, diag_ready, r_psum = (
            sem(n) for n in ("ch", "cl", "kp", "vp", "sq", "sp", "vr", "rr", "di", "rp"))
        normed, k_high, k_low, v_full, v_high = (sem(n) for n in ("norm", "kh", "kl", "vf", "vh"))
        stacked = [sem("st0"), sem("st1")]
        block = ctx.enter_context(nc.Block())
        at = lambda b: bass.ds(b * S, S)
        heads = lambda a: a.rearrange("p (o h d) -> p o h d", o=1, d=HD)
        vtile = lambda a, b, t: a[:, bass.ds(b * 2 + t, 1), :, 0:HD]

        def stack_count(b, p):
            return b * (KEY_INCS // 2) + (2 - p) * (KEY_INCS // 2)

        def batches(engine, step, last=B - 1):
            for b in range(2):
                step(b, b % 2)
            with engine.Fori(0, (B - 4) // 2) as i:
                for p in range(2):
                    step(i * 2 + (p + 2), p)
            for b in range(B - 2, last + 1):
                step(b, b % 2)

        first = lambda b: known(b) and b == 0
        exists = lambda b: not known(b) or 0 <= b < B

        @block.gpsimd
        def _(pool):
            pool.memset(v_hi[:, :, :, HD:], 1.0)
            pool.memset(v_lo[:, :, :, HD:], 0.0)

            def step(b, p):
                pool.wait_ge(var_ready, b + 1)
                pool.tensor_tensor(r[:, :], v[:, :], k.pow_half[:, 0:TPB], ALU.pow).then_inc(r_ready, 1)

            batches(pool, step)

        @block.sync
        def _(sp):
            def step(b, p):
                sp.wait_ge(k_low, b + 1)
                for j, part in enumerate((k_hi[p], k_lo[p]) * 2):
                    rows = ks[bass.ds(b, 1), j * HD:(j + 1) * HD, :, :, :].rearrange("o d h c s -> (o h) d (c s)")
                    sp.dma_start(rows, part[:, :, :].rearrange("p c s -> p (c s)")).then_inc(stacked[p], 16)

            for p in range(2):
                sp.sem_inc(stacked[p], KEY_INCS)
            batches(sp, step)
            for p in range(2):
                sp.wait_ge(stacked[p], (B // 2 + 1) * KEY_INCS)

        @block.scalar
        def _(act):
            def split_context(b, p):
                act.activation(c_hi[p][:, :, :], ctxT[:, :, at(b)], ACT.Copy).then_inc(c_high, 1)

            def step(b, p):
                if exists(b):
                    squares(b, p)
                if exists(b - 1):
                    high(b - 1, 1 - p)
                if exists(b):
                    products(b, p)

            def squares(b, p):
                act.wait_ge(k_psum, b + 1)
                if not known(b) or b >= 2:
                    act.wait_ge(normed, b * DC - DC)
                if not first(b):
                    act.wait_ge(sum_psum, b)
                for c in range(DC):
                    bias = vectors[:, ROWS["bk"] + c:ROWS["bk"] + c + 1]
                    act.activation(u[p][:, c, :], psK[c // 2][:, c % 2, :], ACT.Identity, bias=bias).then_inc(squared, 1)
                    act.activation(sq[:, c, :], psK[c // 2][:, c % 2, :], ACT.Square, bias=bias).then_inc(squared, 1)

            def products(b, p):
                for t in range(2):
                    act.wait_ge(v_full, b * 2 + (t + 1))
                    act.activation(vtile(v_hi, b, t), heads(vf[t][:, :]), ACT.Copy).then_inc(v_high, 1)
                if not known(b) or b + 2 < B:
                    act.wait_ge(v_psum, b * 2 + 2)
                    split_context(b + 2, p)

            def high(b, p):
                act.wait_ge(normed, b * DC + DC)
                act.wait_ge(stacked[p], stack_count(b, p))
                act.activation(k_hi[p][:, :, :], kn[:, :, :], ACT.Copy).then_inc(k_high, 1)

            split_context(0, 0)
            split_context(1, 1)
            batches(act, step, B)

        @block.vector
        def _(dve):
            def split_context(b, p):
                dve.wait_ge(c_high, b + 1)
                dve.tensor_tensor(c_lo[p][:, :, :], ctxT[:, :, at(b)], c_hi[p][:, :, :], ALU.subtract).then_inc(c_low, 1)

            def step(b, p):
                if exists(b - 1):
                    normalise(b - 1, 1 - p)
                if exists(b):
                    products(b, p)

            def products(b, p):
                for t in range(2):
                    dve.wait_ge(v_psum, b * 2 + (t + 1))
                    if not known(b) or b:
                        dve.wait_ge(v_high, b * 2 + (t - 1))
                    dve.tensor_tensor(vf[t][:, :], psV[t][:, :], vbias[:, :], ALU.add).then_inc(v_full, 1)
                for t in range(2):
                    dve.wait_ge(v_high, b * 2 + (t + 1))
                    dve.tensor_tensor(vtile(v_lo, b, t), heads(vf[t][:, :]), vtile(v_hi, b, t), ALU.subtract)
                if not known(b) or b + 2 < B:
                    split_context(b + 2, p)
                dve.wait_ge(sum_psum, b + 1)
                dve.tensor_scalar(v[:, :], psR[:, 0, 0:TPB], 1.0 / D, RMS_EPS, ALU.mult, ALU.add).then_inc(var_ready, 1)
                dve.wait_ge(r_ready, b + 1)
                spread_on_diagonals(dve, k, diag, r).then_inc(diag_ready, 1)

            def normalise(b, p):
                if not known(b) or b:
                    dve.wait_ge(k_high, b)
                dve.wait_ge(r_psum, b + 1)
                for c in range(DC):
                    dve.scalar_tensor_tensor(kn[:, c, :], u[p][:, c, :], vectors[:, ROWS["gk"] + c:ROWS["gk"] + c + 1],
                                             psR[:, 1, :], ALU.mult, ALU.mult).then_inc(normed, 1)
                dve.wait_ge(k_high, b + 1)
                dve.tensor_tensor(k_lo[p][:, :, :], kn[:, :, :], k_hi[p][:, :, :], ALU.subtract).then_inc(k_low, 1)

            split_context(0, 0)
            split_context(1, 1)
            batches(dve, step, B)

        @block.tensor
        def _(pe):
            def keys(b, p):
                pe.wait_ge(c_low, b + 1)
                if not first(b):
                    pe.wait_ge(squared, b * (2 * DC))
                for f in range(DC):
                    for c in range(DC):
                        last = three_products(pe, psK[f // 2][:, f % 2, :],
                                              [kw[:, s, c, f * P:(f + 1) * P] for s in range(2)],
                                              [c_hi[p][:, c, :], c_lo[p][:, c, :]], c == 0, c == DC - 1)
                last.then_inc(k_psum, 1)

            def spread(b):
                pe.wait_ge(diag_ready, b + 1)
                pe.matmul(psR[:, 1, :], k.ones[:, :], diag[:, :, :].rearrange("p t q -> p (t q)"), start=True, stop=True)\
                  .then_inc(r_psum, 1)

            def values(b, p, t):
                if not first(b):
                    pe.wait_ge(v_full, b * 2 + (t - 1))
                for c in range(DC):
                    last = three_products(pe, psV[t][:, :], [a[p][:, c, t * P:(t + 1) * P] for a in (c_hi, c_lo)],
                                          [vw[:, s, c, :] for s in range(2)], c == 0, c == DC - 1)
                last.then_inc(v_psum, 1)

            def sums(b):
                pe.wait_ge(squared, b * (2 * DC) + 2 * DC)
                if not first(b):
                    pe.wait_ge(normed, b * DC)
                square_sums(pe, k, psR[:, 0, :], sq).then_inc(sum_psum, 1)

            def step(b, p):
                if exists(b):
                    keys(b, p)
                if exists(b - 1):
                    spread(b - 1)
                if exists(b):
                    values(b, p, 0)
                    values(b, p, 1)
                    sums(b)

            batches(pe, step, B)


def stage_attention(k, ks, v_hi, v_lo, qw, ow, vectors, x_mean, x_rstd, sel):
    nc = k.nc
    with ExitStack() as ctx:
        sb = lambda name, shape, dt: ctx.enter_context(nc.sbuf_tensor(name, shape, dt))
        two = lambda name, shape, dt: [sb(f"{name}{i}", shape, dt) for i in range(2)]
        bo = sb("at_bo", [P, D], F32)
        xn = two("at_xn", [P, D], F32)
        x_hi, x_lo = sb("at_xhi", [P, DC, S], BF16), sb("at_xlo", [P, DC, S], BF16)
        qn, sq = sb("at_qn", [P, DC, S], F32), sb("at_sq", [P, DC, S], F32)
        v, r = (sb(f"at_{n}", [P, TPB], F32) for n in ("v", "r"))
        diag = sb("at_diag", [P, TPB, P], F32)
        q_hi, q_lo = sb("at_qhi", [P, DC, S], BF16), sb("at_qlo", [P, DC, S], BF16)
        qs = two("at_qs", [P, HC, DC, S], BF16)
        kb = two("at_kb", [P, HC, DC, S], BF16)
        negmax = two("at_negmax", [P, 4], F32)
        maxes = sb("at_maxes", [P, 2, P], BF16)
        maxT = sb("at_maxT", [P, 2, P], BF16)
        pf = two("at_pf", [P, 2, 2, S], F32)
        ph, pl = ([sb(f"at_{n}{i}", [P, 2, 2, S], BF16) for i in range(4)] for n in ("ph", "pl"))
        rden = sb("at_rden", [P, 4], F32)
        o = two("at_o", [P, 2, D], F32)
        o_hi, o_lo = sb("at_ohi", [P, DC, S], BF16), sb("at_olo", [P, DC, S], BF16)
        psS = ctx.enter_context(nc.psum_tensor("ps_s", [P, 2, 2, S], F32))
        psT = ctx.enter_context(nc.psum_tensor("ps_st", [P, 2, 2, S], F32))
        psM = ctx.enter_context(nc.psum_tensor("ps_m", [P, 2, P], BF16))
        psO = ctx.enter_context(nc.psum_tensor("ps_o", [P, 4, VC], F32))
        psP = [ctx.enter_context(nc.psum_tensor(f"ps_p{i}", [P, D], F32)) for i in range(2)]
        sem = lambda name: k.semaphore(("at_" + name))
        b_loaded, dve_step, maxes_zeroed = (sem(n) for n in ("bl", "dve", "mz"))
        s_psum, max_read, maxes_ready, m_psum, maxT_ready, st_psum, exped, p_high, p_low, o_psum, o_read = (
            sem(n) for n in ("sp", "mr", "mx", "mp", "mt", "stp", "ex", "ph", "pl", "op", "od"))
        xn_ready, biased, xt_psum, x_high, x_low, q_psum, squared, normed, q_high, q_low = (
            sem(n) for n in ("xn", "bi", "xtp", "xh", "xl", "qp", "sq", "no", "qh", "ql"))
        sum_psum, var_ready, r_ready, diag_ready, r_psum = (sem(n) for n in ("sup", "var", "rr", "di", "rp"))
        ot_psum, ot_high, ot_low, y_psum, y_added = (sem(n) for n in ("otp", "oth", "otl", "yp", "ya"))
        stacked = [sem("st0"), sem("st1")]
        k_loaded = [sem("kl0"), sem("kl1")]
        block = ctx.enter_context(nc.Block())
        xtile = lambda t: k.x[:, bass.ds(t, 1), :]
        one = lambda a, t: a[:, bass.ds(t, 1)]
        in_q = lambda b, ahead: not known(b) or 0 <= b + ahead < B
        in_g = lambda b, u, off: not known(b) or 0 <= b * UNITS + u + off < B * UNITS
        G = UNITS

        def stack_count(b, p):
            return b * (STACK_INCS // 2) + (2 - p) * (STACK_INCS // 2)

        def steps(engine, step, link=None, per=0):
            for b in range(-2, 2):
                for u in range(UNITS):
                    step(b, b % 2, u)
            with (link.loop((B - 4) // 2, per) if link else engine.Fori(0, (B - 4) // 2)) as i:
                for p in range(2):
                    for u in range(UNITS):
                        step(i * 2 + (p + 2), p, u)
            for b in range(B - 2, B + 1):
                for u in range(UNITS):
                    step(b, b % 2, u)

        @block.sync
        def _(sp):
            sp.dma_start(bo[:, :], broadcast_rows(k.ins["L1_xattn_bo"], D)).then_inc(b_loaded, 16)

            def step(b, p, u):
                if u == 2 and in_q(b, 1):
                    if not known(b) or b >= 1:
                        sp.wait_ge(st_psum, b * G)
                    sp.dma_start(kb[1 - p][:, :, :, :], ks[bass.ds(b + 1, 1), :, :, :, :].rearrange("o p h c s -> (o p) h c s"))\
                      .then_inc(k_loaded[1 - p], 16)
                if u == 3 and in_q(b, 1):
                    for j, part in enumerate((q_hi, q_hi, q_lo, q_lo)):
                        if j % 2 == 0:
                            sp.wait_ge((q_high, q_low)[j // 2], b + 2)
                        for h in range(HC):
                            sp.dma_start(qs[1 - p][j * HD:(j + 1) * HD, h, :, :], part[h * HD:(h + 1) * HD, :, :])\
                              .then_inc(stacked[1 - p], 16)

            steps(sp, step)

        @block.gpsimd
        def _(pool):
            pool.memset(maxes[:, :, :], 0.0).then_inc(maxes_zeroed, 1)
            pool.wait_ge(b_loaded, 16)

            def step(b, p, u):
                if u == 5 and in_q(b, 2):
                    for t in range(2):
                        pool.wait_ge(xn_ready, b * 2 + (4 + t + 1))
                        pool.tensor_tensor(xtile(b * 2 + (4 + t)), xtile(b * 2 + (4 + t)), bo[:, :].unsqueeze(1), ALU.add)\
                            .then_inc(biased, 1)
                if in_g(b, u, 0):
                    g = b * G + u
                    pool.wait_ge(p_high, g + 1)
                    pool.tensor_tensor(pl[u % 4][:, :, :, :], pf[u % 2][:, :, :, :], ph[u % 4][:, :, :, :], ALU.subtract)\
                        .then_inc(p_low, 1)
                if u == 0 and in_q(b, 1):
                    pool.wait_ge(var_ready, b + 2)
                    pool.tensor_tensor(r[:, :], v[:, :], k.pow_half[:, 0:TPB], ALU.pow).then_inc(r_ready, 1)

            steps(pool, step)

        @block.scalar
        def _(act):
            def biased_and_squared(q, c):
                act.wait_ge(q_psum, q * DC + (c + 1))
                if c == 0 and (not known(q) or q):
                    act.wait_ge(normed, q * DC)
                bias = vectors[:, ROWS["bq"] + c:ROWS["bq"] + c + 1]
                act.activation(qn[:, c, :], psP[1 - c % 2][:, 0:S], ACT.Identity, bias=bias).then_inc(squared, 1)
                act.activation(sq[:, c, :], psP[1 - c % 2][:, 0:S], ACT.Square, bias=bias).then_inc(squared, 1)

            def step(b, p, u):
                if u == 0 and in_q(b, 1):
                    biased_and_squared(b + 1, 2)
                    biased_and_squared(b + 1, 3)
                if u == 2 and in_q(b, 1):
                    act.wait_ge(normed, b * DC + 2 * DC)
                    if not known(b) or b + 1 >= 1:
                        act.wait_ge(stacked[p], stack_count(b, p))
                    act.activation(q_hi[:, :, :], qn[:, :, :], ACT.Copy).then_inc(q_high, 1)
                if u == 3 and in_q(b, -1):
                    for t in range(2):
                        act.wait_ge(ot_psum, b * 2 + (t - 1))
                        act.activation(o_hi[:, :, t * P:(t + 1) * P], psP[1 - t][:, :].rearrange("p (c t) -> p c t", c=DC),
                                       ACT.Copy).then_inc(ot_high, 1)
                if u == 6 and in_q(b, 2):
                    for t in range(2):
                        act.wait_ge(xt_psum, b * 2 + (4 + t + 1))
                        act.activation(x_hi[:, :, t * P:(t + 1) * P], psP[1 - t][:, :].rearrange("p (c t) -> p c t", c=DC),
                                       ACT.Copy).then_inc(x_high, 1)
                if u == 7 and in_q(b, 2):
                    biased_and_squared(b + 2, 0)
                    biased_and_squared(b + 2, 1)
                if in_g(b, u, 0):
                    g = b * G + u
                    act.wait_ge(st_psum, g + 1)
                    if not known(b) or g >= 2:
                        act.wait_ge(p_low, g - 1)
                    act.activation(pf[u % 2][:, :, :, :], psT[:, :, :, :], ACT.Exp, scale=SCORE_SCALE).then_inc(exped, 1)
                    act.wait_ge(exped, g + 1)
                    act.activation(ph[u % 4][:, :, :, :], pf[u % 2][:, :, :, :], ACT.Copy).then_inc(p_high, 1)

            steps(act, step)

        @block.vector
        def _(dve):
            link = Link(dve, dve_step)
            dve.wait_ge(maxes_zeroed, 1)

            def step(b, p, u):
                g = b * G + u
                if in_g(b, u, 1):
                    dve.wait_ge(m_psum, g + 2)
                    dve.tensor_copy(maxT[:, :, :], psM[:, :, :]).then_inc(maxT_ready, 1)
                if in_g(b, u, 2):
                    n = u % 2
                    dve.wait_ge(s_psum, g + 3)
                    dve.tensor_reduce(negmax[n][:, :].rearrange("p (j q) -> p j q", j=2), psS[:, :, :, :], AX.X, ALU.max,
                                      negate=True).then_inc(max_read, 1)
                    dve.wait_ge(max_read, g + 3)
                    m = negmax[n][:, :].rearrange("p (j q) -> p q j", j=2)
                    link(dve.tensor_copy(maxes[:, :, 0:4:2], m))
                    dve.tensor_tensor(maxes[:, :, 1:4:2], m, maxes[:, :, 0:4:2], ALU.subtract).then_inc(maxes_ready, 1)
                if u == 2 and in_q(b, 1):
                    dve.wait_ge(q_high, b + 2)
                    dve.tensor_tensor(q_lo[:, :, :], qn[:, :, :], q_hi[:, :, :], ALU.subtract).then_inc(q_low, 1)
                if u == 3 and in_q(b, -1):
                    for t in range(2):
                        dve.wait_ge(ot_high, b * 2 + (t - 1))
                        half = slice(t * P, (t + 1) * P)
                        dve.tensor_tensor(o_lo[:, :, half], psP[1 - t][:, :].rearrange("p (c t) -> p c t", c=DC),
                                          o_hi[:, :, half], ALU.subtract).then_inc(ot_low, 1)
                if u == 6 and in_q(b, 2):
                    for t in range(2):
                        dve.wait_ge(x_high, b * 2 + (4 + t + 1))
                        half = slice(t * P, (t + 1) * P)
                        dve.tensor_tensor(x_lo[:, :, half], psP[1 - t][:, :].rearrange("p (c t) -> p c t", c=DC),
                                          x_hi[:, :, half], ALU.subtract).then_inc(x_low, 1)
                if u == 1 and in_q(b, 1):
                    dve.wait_ge(r_ready, b + 2)
                    spread_on_diagonals(dve, k, diag, r).then_inc(diag_ready, 1)
                if in_g(b, u, -2):
                    dve.wait_ge(o_psum, g - 1)
                    uo = (u - 2) % UNITS
                    po = p if u >= 2 else 1 - p
                    link(dve.reciprocal(rden[:, :], psO[:, :, HD]))
                    dst = o[po][:, :, uo * 2 * HD:(uo + 1) * 2 * HD].rearrange("p q (j d) -> p j q d", j=2)
                    dve.tensor_tensor(dst, psO[:, :, 0:HD].rearrange("p (j q) d -> p j q d", j=2),
                                      rden[:, :].rearrange("p (j q) -> p j q", j=2).unsqueeze(3).broadcast_to([P, 2, 2, HD]),
                                      ALU.mult).then_inc(o_read, 1)
                if u == 0 and in_q(b, 1):
                    dve.wait_ge(sum_psum, b + 2)
                    dve.tensor_scalar(v[:, :], psP[0][:, 0:TPB], 1.0 / D, RMS_EPS, ALU.mult, ALU.add).then_inc(var_ready, 1)
                if u == 1 and in_q(b, 1):
                    dve.wait_ge(r_psum, b + 2)
                    for c in range(DC):
                        dve.scalar_tensor_tensor(qn[:, c, :], qn[:, c, :], vectors[:, ROWS["gq"] + c:ROWS["gq"] + c + 1],
                                                 psP[0][:, S:], ALU.mult, ALU.mult).then_inc(normed, 1)
                for t in range(2):
                    if u == 4 + t and in_q(b, -1):
                        tile = b * 2 + (t - 2)
                        dve.wait_ge(y_psum, b * 2 + (t - 1))
                        dve.wait_ge(biased, b * 2 + (t - 1))
                        dve.tensor_tensor(xtile(tile), xtile(tile), psP[1 - t][:, :].unsqueeze(1), ALU.add).then_inc(y_added, 1)
                if u == 4 and in_q(b, 2):
                    for t in range(2):
                        tile = b * 2 + (4 + t)
                        if not known(b) or b + 2 >= 1:
                            dve.wait_ge(xt_psum, tile - 1)
                        dve.tensor_scalar(xn[t][:, :], xtile(tile), one(x_mean, tile), one(x_rstd, tile),
                                          ALU.subtract, ALU.mult).then_inc(xn_ready, 1)

            steps(dve, step, link, 2 * (8 * 2))

        @block.tensor
        def _(pe):
            def scores(b, p, u, g):
                if u == 0:
                    pe.wait_ge(stacked[p], stack_count(b, p))
                    pe.wait_ge(k_loaded[p], b * 8 + 8 * (2 - p))
                if not known(g) or g:
                    pe.wait_ge(max_read, g)
                c, h0 = u // 2, 2 * (u % 2)
                for j in range(2):
                    for q in range(2):
                        last = pe.matmul(psS[:, j, q, :], qs[p][:, h0 + j, c, q * P:(q + 1) * P], kb[p][:, h0 + j, c, :],
                                         start=True, stop=True)
                last.then_inc(s_psum, 1)

            def turn_maxes(g):
                pe.wait_ge(maxes_ready, g + 1)
                if not known(g) or g:
                    pe.wait_ge(maxT_ready, g)
                for q in range(2):
                    last = pe.transpose(psM[:, q, :], maxes[:, q, :], k.ident_b[:, :])
                last.then_inc(m_psum, 1)

            def values(b, u, g):
                pe.wait_ge(p_low, g + 1)
                if not known(g) or g:
                    pe.wait_ge(o_read, g)
                for j in range(2):
                    for q in range(2):
                        cols = slice(q * P, (q + 1) * P)
                        for n, (pr, vv) in enumerate(((ph, v_hi), (ph, v_lo), (pl, v_hi))):
                            for kc in range(2):
                                last = pe.matmul(psO[:, 2 * j + q, :], pr[u % 4][:, j, kc, cols],
                                                 vv[:, bass.ds(b * 2 + kc, 1), 2 * u + j, :].rearrange("p o d -> p (o d)"),
                                                 start=(n == 0 and kc == 0), stop=(n == 2 and kc == 1))
                last.then_inc(o_psum, 1)

            def transposed_scores(b, p, u, g):
                pe.wait_ge(maxT_ready, g + 1)
                if not known(g) or g:
                    pe.wait_ge(exped, g)
                c, h0 = u // 2, 2 * (u % 2)
                for j in range(2):
                    for kc in range(2):
                        pe.matmul(psT[:, j, kc, :], kb[p][:, h0 + j, c, kc * P:(kc + 1) * P], qs[p][:, h0 + j, c, :],
                                  start=True, stop=False)
                        last = pe.matmul(psT[:, j, kc, :], sel[:, j, :], maxT[:, :, :].rearrange("p q t -> p (q t)"),
                                         start=False, stop=True)
                last.then_inc(st_psum, 1)

            def queries(q, c):
                if c == 0:
                    pe.wait_ge(x_low, q * 2 + 2)
                if c >= 2:
                    pe.wait_ge(squared, q * (2 * DC) + 2 * (c - 1))
                for kc in range(DC):
                    last = three_products(pe, psP[1 - c % 2][:, 0:S], [qw[:, s, kc, c * P:(c + 1) * P] for s in range(2)],
                                          [x_hi[:, kc, :], x_lo[:, kc, :]], kc == 0, kc == DC - 1)
                last.then_inc(q_psum, 1)

            def step(b, p, u):
                g = b * G + u
                if in_g(b, u, 0):
                    transposed_scores(b, p, u, g)
                if in_g(b, u, 2):
                    nb, np_, nu = (b, p, u + 2) if u + 2 < UNITS else (b + 1, 1 - p, u + 2 - UNITS)
                    scores(nb, np_, nu, g + 2)
                if in_g(b, u, 1):
                    turn_maxes(g + 1)
                if in_g(b, u, -2):
                    ob, ou = (b, u - 2) if u >= 2 else (b - 1, u + UNITS - 2)
                    values(ob, ou, g - 2)
                if u == 0 and in_q(b, 1):
                    pe.wait_ge(squared, b * (2 * DC) + 4 * DC)
                    square_sums(pe, k, psP[0], sq).then_inc(sum_psum, 1)
                if u == 1 and in_q(b, 1):
                    pe.wait_ge(diag_ready, b + 2)
                    pe.matmul(psP[0][:, S:], k.ones[:, :], diag[:, :, :].rearrange("p t q -> p (t q)"), start=True, stop=True)\
                      .then_inc(r_psum, 1)
                if u == 2 and in_q(b, -1):
                    pe.wait_ge(o_read, b * G)
                    if in_q(b, 1):
                        pe.wait_ge(normed, b * DC + 2 * DC)
                    for t in range(2):
                        for c in range(DC):
                            last = pe.transpose(psP[1 - t][:, c * P:(c + 1) * P], o[1 - p][:, t, c * P:(c + 1) * P], k.ident[:, :])
                        last.then_inc(ot_psum, 1)
                for t in range(2):
                    if u == 3 + t and in_q(b, -1):
                        pe.wait_ge(ot_low, b * 2)
                        for c in range(DC):
                            last = three_products(pe, psP[1 - t][:, :], [a[:, c, t * P:(t + 1) * P] for a in (o_hi, o_lo)],
                                                  [ow[:, s, c, :] for s in range(2)], c == 0, c == DC - 1)
                        last.then_inc(y_psum, 1)
                if u == 5 and in_q(b, 2):
                    for t in range(2):
                        pe.wait_ge(xn_ready, b * 2 + (4 + t + 1))
                        if not known(b) or b >= 1:
                            pe.wait_ge(y_added, b * 2 + (t - 1))
                        for c in range(DC):
                            last = pe.transpose(psP[1 - t][:, c * P:(c + 1) * P], xn[t][:, c * P:(c + 1) * P], k.ident[:, :])
                        last.then_inc(xt_psum, 1)
                if u == 6 and in_q(b, 2):
                    queries(b + 2, 0)
                    queries(b + 2, 1)
                if u == 7 and in_q(b, 2):
                    queries(b + 2, 2)
                    queries(b + 2, 3)

            steps(pe, step)


E_N = 16
SH_N = 2
FE = 256
F2 = FE // P
BLK = 256
ST = BLK // P
NBLK = (2 * TOK + E_N * (BLK - 1)) // BLK
FLOOR = 0.498


def stage_router(k, xf, xT_hi, xT_lo, xaff, sgu, sd):
    nc = k.nc
    with ExitStack() as ctx:
        sb = lambda name, shape, dt: ctx.enter_context(nc.sbuf_tensor(name, shape, dt))
        two = lambda name, shape, dt: [sb(f"{name}{i}", shape, dt) for i in range(2)]
        wa = sb("r_wa", [P, DC, E_N], F32)
        stats = sb("r_stats", [P, NT, 6], F32)
        mean, var, tmp, rstd = (sb(f"r_{n}", [P, NT], F32) for n in ("mean", "var", "tmp", "rstd"))
        xn, xT = two("r_xn", [P, D], F32), two("r_xT", [P, DC, P], F32)
        ex = sb("r_exp", [P, NT, E_N], F32)
        psX = [ctx.enter_context(nc.psum_tensor(f"ps_rx{i}", [P, D], F32)) for i in range(2)]
        psL = ctx.enter_context(nc.psum_tensor("ps_rl", [P, NT * E_N], F32))
        raw = [sb(f"r_raw{i}", [P, 1024], F32) for i in range(6)]
        w_loaded, w_high = [k.semaphore(f"r_w{i}") for i in range(6)], k.semaphore("r_whi")
        dst = [(sgu, e, m) for e in range(SH_N) for m in range(2)] + [(sd, e, 0) for e in range(SH_N)]
        place = lambda n, s: (dst[n][0][:, s, dst[n][1], dst[n][2], :] if n < 4 else dst[n][0][:, s, dst[n][1], :])
        sem = lambda name: k.semaphore(("r_" + name))
        wa_loaded, stat_done, dve_step, var_ready, rstd_ready, xn_ready, added, x_psum, xT_ready, x_high, x_low, logits, exped = (
            sem(n) for n in ("wa", "stat", "dve", "var", "rstd", "xn", "add", "xp", "xT", "xh", "xl", "log", "ex"))
        block = ctx.enter_context(nc.Block())
        row = lambda a, t: a[:, bass.ds(t, 1), :]
        cols = lambda a, t: a[:, :, bass.ds(t * P, P)]
        chunks = lambda a: a.rearrange("p (c t) -> p c t", c=DC)

        @block.sync
        def _(sp):
            sp.dma_start(wa[:, :, :], k.ins["L1_ffn_wa"].rearrange("(c p) e -> p c e", p=P)).then_inc(wa_loaded, 16)
            for n in range(6):
                src = k.ins[("L1_ffn_sg", "L1_ffn_sw1")[dst[n][2]] if n < 4 else "L1_ffn_sw2"][dst[n][1], :, :]
                sp.dma_start(raw[n][:, :].rearrange("p (c n) -> p c n", c=D // P if n < 4 else F2),
                             src.rearrange("(c p) n -> p c n", p=P)).then_inc(w_loaded[n], 16)

        @block.gpsimd
        def _(pool):
            pool.wait_ge(var_ready, 1)
            pool.tensor_tensor(rstd[:, :], var[:, :], k.pow_half[:, :], ALU.pow).then_inc(rstd_ready, 1)
            with pool.Fori(0, NT // 2) as i:
                for p in range(2):
                    t = i * 2 + p
                    pool.wait_ge(xn_ready, i * 4 + (2 * p + 2))
                    pool.tensor_tensor(row(k.x, t), row(k.x, t), xn[p][:, :].unsqueeze(1), ALU.add).then_inc(added, 1)

        @block.vector
        def _(dve):
            link = Link(dve, dve_step)
            for t in range(NT):
                dve.bn_stats(stats[:, t, :], k.x[:, t, :]).then_inc(stat_done, 1)
            dve.wait_ge(stat_done, NT)
            mean_var(link, dve, stats, mean[:, :], var[:, :], tmp[:, :], LN_EPS)
            dve.sem_inc(var_ready, 1)
            dve.wait_ge(rstd_ready, 1)

            def normalise(t, p):
                if not known(t) or t >= 2:
                    dve.wait_ge(added, t - 1)
                    dve.wait_ge(x_psum, t - 1)
                scale = (mean[:, bass.ds(t, 1)], rstd[:, bass.ds(t, 1)], ALU.subtract, ALU.mult)
                dve.tensor_scalar(xn[p][:, :], row(k.x, t), *scale).then_inc(xn_ready, 1)
                dve.tensor_scalar(row(xf, t), row(k.x, t), *scale).then_inc(xn_ready, 1)

            def split(t, p):
                dve.wait_ge(x_high, t + 1)
                dve.tensor_tensor(cols(xT_lo, t), xT[p][:, :, :], cols(xT_hi, t), ALU.subtract).then_inc(x_low, 1)

            normalise(0, 0)
            normalise(1, 1)
            with dve.Fori(0, NT // 2 - 1) as i:
                for p in range(2):
                    normalise(i * 2 + (p + 2), p)
                    split(i * 2 + p, p)
            for t in range(NT - 2, NT):
                split(t, t % 2)
            dve.wait_ge(exped, 1)
            link(dve.tensor_scalar(ex[:, :, :], ex[:, :, :], 1.0, None, ALU.add))
            dve.reciprocal(xaff[:, :, :], ex[:, :, :])
            for n in range(6):
                dve.wait_ge(w_high, n + 1)
                dve.tensor_tensor(place(n, 1), raw[n][:, :], place(n, 0), ALU.subtract)

        @block.tensor
        def _(pe):
            def turn(t, p):
                pe.wait_ge(xn_ready, t * 2 + 1)
                if not known(t) or t >= 2:
                    pe.wait_ge(xT_ready, t - 1)
                for c in range(DC):
                    last = pe.transpose(psX[p][:, c * P:(c + 1) * P], xn[p][:, c * P:(c + 1) * P], k.ident[:, :])
                last.then_inc(x_psum, 1)

            def score(t, p):
                pe.wait_ge(xT_ready, t + 1)
                for c in range(DC):
                    last = pe.matmul(psL[:, bass.ds(t * E_N, E_N)], xT[p][:, c, :], wa[:, c, :],
                                     start=(c == 0), stop=(c == DC - 1))
                last.then_inc(logits, 1)

            pe.wait_ge(wa_loaded, 16)
            turn(0, 0)
            turn(1, 1)
            with pe.Fori(0, NT // 2 - 1) as i:
                for p in range(2):
                    score(i * 2 + p, p)
                    turn(i * 2 + (p + 2), p)
            for t in range(NT - 2, NT):
                score(t, t % 2)

        @block.scalar
        def _(act):
            act.sem_inc(logits, 2)
            act.sem_inc(x_low, 2)
            with act.Fori(0, NT // 2) as i:
                for p in range(2):
                    t = i * 2 + p
                    act.wait_ge(x_psum, t + 1)
                    act.wait_ge(logits, i * 2 + (p + 1))
                    act.wait_ge(x_low, i * 2 + (p + 1))
                    act.activation(xT[p][:, :, :], chunks(psX[p][:, :]), ACT.Copy).then_inc(xT_ready, 1)
                    act.wait_ge(xT_ready, t + 1)
                    act.activation(cols(xT_hi, t), xT[p][:, :, :], ACT.Copy).then_inc(x_high, 1)
            act.wait_ge(logits, NT + 2)
            act.activation(ex[:, :, :].rearrange("p t e -> p (t e)"), psL[:, :], ACT.Exp, scale=-1.0).then_inc(exped, 1)
            for n in range(6):
                act.wait_ge(w_loaded[n], 16)
                act.activation(place(n, 0), raw[n][:, :], ACT.Copy).then_inc(w_high, 1)


def stage_route_and_shared(k, xf, xT_hi, xT_lo, xaff, sgu, sd, slots, share, combine, wrow):
    nc = k.nc
    with ExitStack() as ctx:
        sb = lambda name, shape, dt: ctx.enter_context(nc.sbuf_tensor(name, shape, dt))
        two = lambda name, shape, dt: [sb(f"{name}{i}", shape, dt) for i in range(2)]
        best = sb("s_best", [P, NT, 8], F32)
        index = sb("s_index", [P, NT, 8], U32)
        indexf = sb("s_indexf", [P, NT, 8], F32)
        iota_e = sb("s_iota_e", [P, E_N], F32)
        iota_j = sb("s_iota_j", [P, NBLK], F32)
        iota_p = sb("s_iota_p", [P, 1], F32)
        hot = [sb(f"s_hot{i}", [P, NT, E_N], F32) for i in range(2)]
        both = sb("s_both", [P, NT, E_N], F32)
        before = sb("s_before", [P, P], F32)
        pos = sb("s_pos", [P, NT, E_N], F32)
        run = [sb(f"s_run{i}", [P, NT + 1, E_N], F32) for i in range(2)]
        blocks = [sb(f"s_blocks{i}", [P, E_N], F32) for i in range(2)]
        start = sb("s_start", [P, E_N], F32)
        slotf = sb("s_slotf", [P, 2, NT], F32)
        le = sb("s_le", [P, NBLK, E_N], F32)
        wf = sb("s_wf", [P, NBLK], F32)
        total = sb("s_total", [P, NT], F32)
        gf, yf = two("s_gf", [P, F2, BLK], F32), two("s_yf", [P, F2, BLK], F32)
        y_hi, y_lo = two("s_yhi", [P, SH_N, F2, BLK], BF16), two("s_ylo", [P, SH_N, F2, BLK], BF16)
        psR = ctx.enter_context(nc.psum_tensor("ps_sr", [P, 2, NT * E_N], F32))
        psG = [ctx.enter_context(nc.psum_tensor(f"ps_sg{i}", [P, F2, BLK], F32)) for i in range(2)]
        psU = [ctx.enter_context(nc.psum_tensor(f"ps_su{i}", [P, F2, BLK], F32)) for i in range(2)]
        psD = [ctx.enter_context(nc.psum_tensor(f"ps_sd{i}", [P, D], F32)) for i in range(ST)]
        sem = lambda name: k.semaphore(("s_" + name))
        consts, both_ready, counted, dve_step, slots_ready, scattered = (sem(n) for n in ("co", "bo", "ct", "dve", "sl", "sc"))
        gu_psum, gelu_done, u_read, y_full, y_high, y_low, d_psum, d_added = (
            sem(n) for n in ("gu", "ge", "ur", "yf", "yh", "yl", "dp", "da"))
        block = ctx.enter_context(nc.Block())
        CH = TOK // BLK

        @block.gpsimd
        def _(pool):
            pool.iota(iota_e[:, :], [[1, E_N]], base=0, channel_multiplier=0, allow_small_or_imprecise_dtypes=True).then_inc(consts, 1)
            pool.iota(iota_j[:, :], [[1, NBLK]], base=0, channel_multiplier=0, allow_small_or_imprecise_dtypes=True).then_inc(consts, 1)
            pool.iota(iota_p[:, :], [[0, 1]], base=0, channel_multiplier=1, allow_small_or_imprecise_dtypes=True).then_inc(consts, 1)
            pool.affine_select(out=before[:, :], in_=k.ones[:, :], compare_op=ALU.is_gt, fill=0.0, base=0,
                               pattern=[[1, P]], channel_multiplier=-1).then_inc(consts, 1)
            pool.wait_ge(slots_ready, 1)
            for s in range(2):
                for t in range(NT):
                    pool.indirect_dma_start(out=k.scratch["rows"], out_offset=bass.IndirectOffsetOnAxis(ap=slots[:, s, t:t + 1], axis=0),
                                            in_=xf[:, t, :], in_offset=None).then_inc(scattered, 16)
            pool.wait_ge(scattered, 16 * 2 * NT)

        @block.vector
        def _(dve):
            link = Link(dve, dve_step)
            for t in range(NT):
                link(dve.max(best[:, t, :], xaff[:, t, :]), wait=False)
            dve.wait_ge(dve_step, NT)
            for t in range(NT):
                link(dve.max_index(index[:, t, :], best[:, t, :], xaff[:, t, :]), wait=False)
            dve.wait_ge(dve_step, 2 * NT)
            link(dve.tensor_copy(indexf[:, :, :], index[:, :, :]))
            dve.wait_ge(consts, 4)
            for s in range(2):
                link(dve.tensor_tensor(hot[s][:, :, :], iota_e[:, :].unsqueeze(1).broadcast_to([P, NT, E_N]),
                                       indexf[:, :, s:s + 1].broadcast_to([P, NT, E_N]), ALU.is_equal))
            dve.tensor_tensor(both[:, :, :], hot[0][:, :, :], hot[1][:, :, :], ALU.add).then_inc(both_ready, 1)
            link(dve.tensor_tensor(total[:, :], best[:, :, 0], best[:, :, 1], ALU.add))
            link(dve.reciprocal(total[:, :], total[:, :]))
            for s in range(2):
                link(dve.tensor_tensor(share[:, s, :], best[:, :, s], total[:, :], ALU.mult))
                link(dve.tensor_tensor(le[:, 0:NT, :] if s else combine[:, :, :], hot[s][:, :, :],
                                       share[:, s, :].unsqueeze(2).broadcast_to([P, NT, E_N]), ALU.mult))
            link(dve.tensor_tensor(combine[:, :, :], combine[:, :, :], le[:, 0:NT, :], ALU.add))
            dve.wait_ge(counted, 1)
            link(dve.memset(run[0][:, 0:1, :], 0.0))
            link(dve.tensor_copy(run[0][:, 1:, :], psR[:, 1, :].rearrange("p (t e) -> p t e", e=E_N)))
            a, step = 0, 1
            while step <= NT:
                link(dve.tensor_tensor(run[1 - a][:, step:, :], run[a][:, step:, :], run[a][:, 0:NT + 1 - step, :], ALU.add))
                link(dve.tensor_copy(run[1 - a][:, 0:step, :], run[a][:, 0:step, :]))
                a, step = 1 - a, 2 * step
            link(dve.tensor_scalar(blocks[0][:, :], run[a][:, NT, :], 1.0 / BLK, (BLK - 1.0) / BLK - FLOOR, ALU.mult, ALU.add))
            link(dve.tensor_scalar(blocks[0][:, :], blocks[0][:, :], ROUND, ROUND, ALU.add, ALU.subtract))
            link(dve.tensor_copy(start[:, :], blocks[0][:, :]))
            b, step = 0, 1
            while step < E_N:
                link(dve.tensor_tensor(blocks[1 - b][:, step:], blocks[b][:, step:], blocks[b][:, 0:E_N - step], ALU.add))
                link(dve.tensor_copy(blocks[1 - b][:, 0:step], blocks[b][:, 0:step]))
                b, step = 1 - b, 2 * step
            link(dve.tensor_tensor(start[:, :], blocks[b][:, :], start[:, :], ALU.subtract))
            link(dve.tensor_tensor(pos[:, :, :], psR[:, 0, :].rearrange("p (t e) -> p t e", e=E_N), run[a][:, 0:NT, :], ALU.add))
            link(dve.tensor_scalar(blocks[b][:, :], start[:, :], float(BLK), None, ALU.mult))
            link(dve.tensor_tensor(pos[:, :, :], pos[:, :, :], blocks[b][:, :].unsqueeze(1).broadcast_to([P, NT, E_N]), ALU.add))
            for s in range(2):
                link(dve.tensor_tensor(both[:, :, :], pos[:, :, :], hot[s][:, :, :], ALU.mult))
                link(dve.tensor_reduce(slotf[:, s, :], both[:, :, :], AX.X, ALU.add))
            dve.tensor_copy(slots[:, :, :], slotf[:, :, :]).then_inc(slots_ready, 1)
            link(dve.tensor_tensor(le[:, :, :], start[:, :].unsqueeze(1).broadcast_to([P, NBLK, E_N]),
                                   iota_j[:, :].unsqueeze(2).broadcast_to([P, NBLK, E_N]), ALU.is_le))
            link(dve.tensor_reduce(wf[:, :], le[:, :, :], AX.X, ALU.add))
            link(dve.tensor_scalar(wf[:, :], wf[:, :], float(P), -float(P), ALU.mult, ALU.add))
            link(dve.tensor_scalar(wf[:, :], wf[:, :], iota_p[:, :], None, ALU.add))
            link(dve.tensor_copy(wrow[:, :], wf[:, :]))

            dve.sem_inc(d_added, ST)
            with dve.Fori(0, CH) as i:
                for e in range(SH_N):
                    dve.wait_ge(gelu_done, i * SH_N + (e + 1))
                    for f in range(F2):
                        last = dve.scalar_tensor_tensor(yf[e][:, f, :], psU[e][:, f, :],
                                                        k.vectors[:, ROWS["sb1"] + 2 * e + f:ROWS["sb1"] + 2 * e + f + 1],
                                                        gf[e][:, f, :], ALU.add, ALU.mult)
                    last.then_inc(y_full, 1)
                    dve.wait_ge(y_high, i * SH_N + (e + 1))
                    dve.tensor_tensor(y_lo[0][:, e, :, :], yf[e][:, :, :], y_hi[0][:, e, :, :], ALU.subtract).then_inc(y_low, 1)
                for s in range(ST):
                    dve.wait_ge(d_psum, i * ST + (s + 2))
                    x = k.x[:, bass.ds(i * ST + s, 1), :]
                    dve.tensor_tensor(x, x, psD[s][:, :].unsqueeze(1), ALU.add).then_inc(d_added, 1)

        @block.scalar
        def _(act):
            act.sem_inc(y_low, SH_N)
            with act.Fori(0, CH) as i:
                for e in range(SH_N):
                    act.wait_ge(gu_psum, i * SH_N + (e + 1 + SH_N))
                    act.wait_ge(y_low, i * SH_N + (e + 1))
                    for f in range(F2):
                        last = act.activation(gf[e][:, f, :], psG[e][:, f, :], ACT.Gelu,
                                              bias=k.vectors[:, ROWS["sgb"] + 2 * e + f:ROWS["sgb"] + 2 * e + f + 1])
                    last.then_inc(gelu_done, 1)
                    act.wait_ge(y_full, i * SH_N + (e + 1))
                    act.wait_ge(d_psum, i * ST + 1)
                    act.activation(y_hi[0][:, e, :, :], yf[e][:, :, :], ACT.Copy).then_inc(y_high, 1)

        @block.tensor
        def _(pe):
            pe.sem_inc(gu_psum, SH_N)
            pe.sem_inc(d_psum, 1)
            pe.wait_ge(both_ready, 1)
            pe.wait_ge(consts, 4)
            flat = both[:, :, :].rearrange("p t e -> p (t e)")
            pe.matmul(psR[:, 0, :], before[:, :], flat, start=True, stop=True)
            pe.matmul(psR[:, 1, :], k.ones[:, :], flat, start=True, stop=True).then_inc(counted, 1)

            def up(i, e):
                for ps, m in ((psG, 0), (psU, 1)):
                    for f in range(F2):
                        for c in range(DC):
                            col = c * FE + f * P
                            last = three_products(pe, ps[e][:, f, :], [sgu[:, s, e, m, col:col + P] for s in range(2)],
                                                  [a[:, c, bass.ds(i * BLK, BLK)] for a in (xT_hi, xT_lo)], c == 0, c == DC - 1)
                last.then_inc(gu_psum, 1)

            def down(i):
                for e in range(SH_N):
                    pe.wait_ge(y_low, i * SH_N + (e + 1 + SH_N))
                for s in range(ST):
                    pe.wait_ge(d_added, i * ST + (s + 1))
                    for e in range(SH_N):
                        for f in range(F2):
                            last = three_products(pe, psD[s][:, :], [a[0][:, e, f, s * P:(s + 1) * P] for a in (y_hi, y_lo)],
                                                  [sd[:, h, e, f * D:(f + 1) * D] for h in range(2)],
                                                  e == 0 and f == 0, e == SH_N - 1 and f == F2 - 1)
                    last.then_inc(d_psum, 1)

            for e in range(SH_N):
                up(0, e)
            with pe.Fori(0, CH - 1) as i:
                for e in range(SH_N):
                    pe.wait_ge(y_full, i * SH_N + (e + 1))
                    up(i + 1, e)
                down(i)
            down(CH - 1)


def stage_experts(k, wrow):
    nc = k.nc
    with ExitStack() as ctx:
        sb = lambda name, shape, dt: ctx.enter_context(nc.sbuf_tensor(name, shape, dt))
        two = lambda name, shape, dt: [sb(f"{name}{i}", shape, dt) for i in range(2)]
        raw = [two(f"e_raw{m}", [P, DC * FE], F32) for m in range(3)]
        wb = [two(f"e_wb{m}", [P, F2], F32) for m in range(2)]
        hi, lo = ([two(f"e_{n}{m}", [P, DC * FE], BF16) for m in range(3)] for n in ("hi", "lo"))
        rows = two("e_rows", [P, ST, D], F32)
        x_hi, x_lo = two("e_xhi", [P, DC, BLK], BF16), two("e_xlo", [P, DC, BLK], BF16)
        gf, yf = two("e_gf", [P, F2, BLK], F32), two("e_yf", [P, F2, BLK], F32)
        y_hi, y_lo = two("e_yhi", [P, F2, BLK], BF16), two("e_ylo", [P, F2, BLK], BF16)
        yo = two("e_yo", [P, ST, D], F32)
        psX = [ctx.enter_context(nc.psum_tensor(f"ps_ex{i}", [P, D], F32)) for i in range(ST)]
        psG = [ctx.enter_context(nc.psum_tensor(f"ps_eg{i}", [P, F2, BLK], F32)) for i in range(2)]
        psU = [ctx.enter_context(nc.psum_tensor(f"ps_eu{i}", [P, F2, BLK], F32)) for i in range(2)]
        psD = [ctx.enter_context(nc.psum_tensor(f"ps_ed{i}", [P, D], F32)) for i in range(ST)]
        sem = lambda name: k.semaphore(("e_" + name))
        up_loaded, down_loaded, biases_loaded, rows_loaded, stored = (
            [sem(f"{n}{i}") for i in range(2)] for n in ("ul", "dl", "bl", "rl", "st"))
        up_high, up_low, down_high, down_low, x_psum, x_high, x_low, gu_psum, gelu_done, y_full, y_high, y_low = (
            sem(n) for n in ("uh", "ulo", "dh", "dlo", "xp", "xh", "xl", "gu", "ge", "yf", "yh", "yl"))
        d_psum, out_ready, row_ready, gather_turn = (sem(n) for n in ("dp", "or", "rr", "turn"))
        wrow_p = two("e_wrow", [P, 1], U32)
        block = ctx.enter_context(nc.Block())
        tables = (k.ins["L1_ffn_rg"].rearrange("e (p c) f -> (e p) (c f)", c=DC),
                  k.ins["L1_ffn_rw1"].rearrange("e (p c) f -> (e p) (c f)", c=DC),
                  k.ins["L1_ffn_rw2"].rearrange("e (p c) f -> (e p) (c f)", c=F2))
        bias_tables = (k.ins["L1_ffn_rgb"].rearrange("e (p c) -> (e p) c", c=F2),
                       k.ins["L1_ffn_rb1"].rearrange("e (p c) -> (e p) c", c=F2))
        rows_dram = k.scratch["rows"].rearrange("(j s p) d -> j p s d", s=ST, p=P)
        out_dram = k.scratch["results"].rearrange("(j s p) d -> j p s d", s=ST, p=P)

        def steps(engine, step):
            for n in range(-2, 4):
                step(n, n % 2)
            with engine.Fori(0, (NBLK - 6) // 2) as i:
                for p in range(2):
                    step(i * 2 + (p + 4), p)
            for n in range(4 + (NBLK - 6) // 2 * 2, NBLK + 2):
                step(n, n % 2)

        exists = lambda j: not known(j) or 0 <= j < NBLK
        first = lambda j: known(j) and j < 2
        half = lambda j, p, n: j * (n // 2) - p * (n // 2)

        @block.gpsimd
        def _(pool):
            def gather(p, dst, src, done):
                idx = bass.IndirectOffsetOnAxis(ap=wrow_p[p][:, :], axis=0)
                pool.indirect_dma_start(out=dst[:, :], out_offset=None, in_=src, in_offset=idx).then_inc(done, 16)

            def gathers(j, p):
                if not first(j):
                    pool.wait_ge(biases_loaded[p], half(j, p, 32))
                pool.tensor_copy(wrow_p[p][:, :], wrow[:, bass.ds(j, 1)]).then_inc(row_ready, 1)
                pool.wait_ge(row_ready, j + 1)
                if not first(j):
                    pool.wait_ge(up_low, j * 2 - 2)
                pool.sem_inc(gather_turn, 1)
                for m in range(2):
                    gather(p, raw[m][p], tables[m], up_loaded[p])
                if not first(j):
                    pool.wait_ge(down_low, j - 1)
                pool.sem_inc(gather_turn, 1)
                gather(p, raw[2][p], tables[2], down_loaded[p])
                if not first(j):
                    pool.wait_ge(y_full, j - 1)
                pool.sem_inc(gather_turn, 1)
                for m in range(2):
                    gather(p, wb[m][p], bias_tables[m], biases_loaded[p])

            def step(n, p):
                if exists(n + 2):
                    gathers(n + 2, p)

            steps(pool, step)

        @block.sync
        def _(sp):
            def load(j, p):
                if not first(j):
                    sp.wait_ge(x_psum, j * ST - ST)
                sp.dma_start(rows[p][:, :, :], rows_dram[bass.ds(j, 1), :, :, :].rearrange("o p s d -> (o p) s d"))\
                  .then_inc(rows_loaded[p], 16)

            def store(j, p):
                sp.wait_ge(out_ready, j + 1)
                sp.dma_start(out_dram[bass.ds(j, 1), :, :, :].rearrange("o p s d -> (o p) s d"), yo[p][:, :, :])\
                  .then_inc(stored[p], 16)

            def step(n, p):
                if exists(n + 2):
                    load(n + 2, p)
                if exists(n - 2):
                    store(n - 2, p)

            steps(sp, step)
            for p in range(2):
                sp.wait_ge(stored[p], 16 * ((NBLK + 1 - p) // 2))

        def up_weight(a):
            return a[:, :].rearrange("p (c q f) -> p c f q", c=DC, f=F2)

        def up_split(a):
            return a[:, :].rearrange("p (c f q) -> p c f q", c=DC, f=F2)

        @block.scalar
        def _(act):
            def gelu(j, p):
                act.wait_ge(gu_psum, j + 1)
                act.wait_ge(biases_loaded[p], half(j, p, 32) + 32)
                if not first(j):
                    act.wait_ge(y_full, j - 1)
                for f in range(F2):
                    last = act.activation(gf[p][:, f, :], psG[p][:, f, :], ACT.Gelu, bias=wb[0][p][:, f:f + 1])
                last.then_inc(gelu_done, 1)

            def x_split(j, p):
                for s in range(ST):
                    act.wait_ge(x_psum, j * ST + (s + 1))
                    if s == 0 and not first(j):
                        act.wait_ge(gu_psum, j - 1)
                    act.activation(x_hi[p][:, :, s * P:(s + 1) * P], psX[s][:, :].rearrange("p (c t) -> p c t", c=DC),
                                   ACT.Copy).then_inc(x_high, 1)

            def y_split(j, p):
                act.wait_ge(y_full, j + 1)
                if not first(j):
                    act.wait_ge(d_psum, j * ST - ST)
                act.activation(y_hi[p][:, :, :], yf[p][:, :, :], ACT.Copy).then_inc(y_high, 1)

            def up_weights(j, p):
                act.wait_ge(up_loaded[p], half(j, p, 32) + 32)
                if not first(j):
                    act.wait_ge(gu_psum, j - 1)
                for m in range(2):
                    act.activation(up_split(hi[m][p]), up_weight(raw[m][p]), ACT.Copy).then_inc(up_high, 1)

            def down_weights(j, p):
                act.wait_ge(down_loaded[p], half(j, p, 16) + 16)
                if not first(j):
                    act.wait_ge(d_psum, j * ST - ST)
                act.activation(hi[2][p][:, :], raw[2][p][:, :], ACT.Copy).then_inc(down_high, 1)

            def step(n, p):
                if exists(n - 1):
                    gelu(n - 1, 1 - p)
                if exists(n + 1):
                    x_split(n + 1, 1 - p)
                if exists(n - 1):
                    y_split(n - 1, 1 - p)
                if exists(n + 1):
                    up_weights(n + 1, 1 - p)
                if exists(n):
                    down_weights(n, p)

            steps(act, step)

        @block.vector
        def _(dve):
            def out_rows(j, p):
                if not first(j):
                    dve.wait_ge(stored[p], half(j, p, 16))
                for s in range(ST):
                    dve.wait_ge(d_psum, j * ST + (s + 1))
                    last = dve.tensor_copy(yo[p][:, s, :], psD[s][:, :])
                last.then_inc(out_ready, 1)

            def gate(j, p):
                dve.wait_ge(gelu_done, j + 1)
                if not first(j):
                    dve.wait_ge(y_high, j - 1)
                for f in range(F2):
                    last = dve.scalar_tensor_tensor(yf[p][:, f, :], psU[p][:, f, :], wb[1][p][:, f:f + 1],
                                                    gf[p][:, f, :], ALU.add, ALU.mult)
                last.then_inc(y_full, 1)

            def x_split(j, p):
                for s in range(ST):
                    dve.wait_ge(x_high, j * ST + (s + 1))
                    part = slice(s * P, (s + 1) * P)
                    dve.tensor_tensor(x_lo[p][:, :, part], psX[s][:, :].rearrange("p (c t) -> p c t", c=DC),
                                      x_hi[p][:, :, part], ALU.subtract).then_inc(x_low, 1)

            def y_split(j, p):
                dve.wait_ge(y_high, j + 1)
                dve.tensor_tensor(y_lo[p][:, :, :], yf[p][:, :, :], y_hi[p][:, :, :], ALU.subtract).then_inc(y_low, 1)

            def up_weights(j, p):
                for m in range(2):
                    dve.wait_ge(up_high, j * 2 + (m + 1))
                    dve.tensor_tensor(up_split(lo[m][p]), up_weight(raw[m][p]), up_split(hi[m][p]), ALU.subtract)\
                       .then_inc(up_low, 1)

            def down_weights(j, p):
                dve.wait_ge(down_high, j + 1)
                dve.tensor_tensor(lo[2][p][:, :], raw[2][p][:, :], hi[2][p][:, :], ALU.subtract).then_inc(down_low, 1)

            def step(n, p):
                if exists(n - 2):
                    out_rows(n - 2, p)
                if exists(n - 1):
                    gate(n - 1, 1 - p)
                if exists(n + 1):
                    x_split(n + 1, 1 - p)
                if exists(n - 1):
                    y_split(n - 1, 1 - p)
                if exists(n + 1):
                    up_weights(n + 1, 1 - p)
                if exists(n):
                    down_weights(n, p)

            steps(dve, step)

        @block.tensor
        def _(pe):
            def turn(j, p):
                pe.wait_ge(rows_loaded[p], half(j, p, 16) + 16)
                if not known(j) or j:
                    pe.wait_ge(x_low, j * ST)
                for s in range(ST):
                    for c in range(DC):
                        last = pe.transpose(psX[s][:, c * P:(c + 1) * P], rows[p][:, s, c::DC], k.ident[:, :])
                    last.then_inc(x_psum, 1)

            def up(j, p):
                pe.wait_ge(x_low, j * ST + ST)
                if not first(j):
                    pe.wait_ge(y_full, j - 1)
                for m, ps in ((0, psG), (1, psU)):
                    pe.wait_ge(up_low, j * 2 + (m + 1))
                    for f in range(F2):
                        for c in range(DC):
                            col = (c * F2 + f) * P
                            last = three_products(pe, ps[p][:, f, :], [a[m][p][:, col:col + P] for a in (hi, lo)],
                                                  [a[p][:, c, :] for a in (x_hi, x_lo)], c == 0, c == DC - 1)
                last.then_inc(gu_psum, 1)

            def down(j, p):
                pe.wait_ge(y_low, j + 1)
                pe.wait_ge(down_low, j + 1)
                if not known(j) or j:
                    pe.wait_ge(out_ready, j)
                for s in range(ST):
                    for f in range(F2):
                        last = three_products(pe, psD[s][:, :], [a[p][:, f, s * P:(s + 1) * P] for a in (y_hi, y_lo)],
                                              [a[2][p][:, f * D:(f + 1) * D] for a in (hi, lo)], f == 0, f == F2 - 1)
                    last.then_inc(d_psum, 1)

            def step(n, p):
                if exists(n + 1):
                    turn(n + 1, 1 - p)
                if exists(n):
                    up(n, p)
                if exists(n - 1):
                    down(n - 1, 1 - p)

            steps(pe, step)


def stage_combine(k, slots, share, combine, out):
    nc = k.nc
    with ExitStack() as ctx:
        sb = lambda name, shape, dt: ctx.enter_context(nc.sbuf_tensor(name, shape, dt))
        ALL_N = E_N + SH_N
        b2 = sb("m_b2", [ALL_N, D], F32)
        b2_hi, b2_lo = sb("m_b2hi", [ALL_N, D], BF16), sb("m_b2lo", [ALL_N, D], BF16)
        mixT_hi, mixT_lo = (sb(f"m_mix{n}", [ALL_N, NT, P], BF16) for n in ("h", "l"))
        mix_set = k.semaphore("m_ms")
        got = [sb(f"m_got{i}", [P, 2, D], F32) for i in range(4)]
        psC = [ctx.enter_context(nc.psum_tensor(f"ps_mc{i}", [E_N, 4, P], F32)) for i in range(4)]
        psB = [ctx.enter_context(nc.psum_tensor(f"ps_mb{i}", [P, D], F32)) for i in range(2)]
        sem = lambda name: k.semaphore(("m_" + name))
        b_loaded, b_high, b_low, turned, mix_high, mix_low, b_psum, b_added, first_added, done = (
            sem(n) for n in ("bl", "bh", "blo", "tu", "mh", "ml", "bp", "ba", "fa", "do"))
        gathered = [sem(f"g{i}") for i in range(4)]
        stored = sem("st")
        block = ctx.enter_context(nc.Block())
        out_dram = out.rearrange("b s d -> (b s) d")

        @block.gpsimd
        def _(pool):
            for t in range(NT):
                if t >= 4:
                    pool.wait_ge(done, t - 3)
                for s in range(2):
                    pool.indirect_dma_start(out=got[t % 4][:, s, :], out_offset=None, in_=k.scratch["results"],
                                            in_offset=bass.IndirectOffsetOnAxis(ap=slots[:, s, t:t + 1], axis=0))\
                        .then_inc(gathered[t % 4], 16)

        @block.sync
        def _(sp):
            sp.dma_start(b2[0:E_N, :], k.ins["L1_ffn_rb2"]).then_inc(b_loaded, 16)
            sp.dma_start(b2[E_N:, :], k.ins["L1_ffn_sb2"]).then_inc(b_loaded, 16)
            for t in range(NT):
                sp.wait_ge(done, t + 1)
                sp.dma_start(out_dram[t * P:(t + 1) * P, :], k.x[:, t, :]).then_inc(stored, 16)
            sp.wait_ge(stored, 16 * NT)

        @block.scalar
        def _(act):
            act.wait_ge(b_loaded, 32)
            act.wait_ge(mix_set, 2)
            act.activation(b2_hi[:, :], b2[:, :], ACT.Copy).then_inc(b_high, 1)
            for i in range(4):
                act.wait_ge(turned, i + 1)
                act.activation(mixT_hi[0:E_N, 4 * i:4 * i + 4, :], psC[i][:, :, :], ACT.Copy).then_inc(mix_high, 1)

        @block.tensor
        def _(pe):
            for i in range(4):
                for j in range(4):
                    last = pe.transpose(psC[i][:, j, :], combine[:, 4 * i + j, :], k.ident[:, :])
                last.then_inc(turned, 1)
            pe.wait_ge(b_low, 1)
            for t in range(NT):
                pe.wait_ge(mix_low, t // 4 + 1)
                if t >= 2:
                    pe.wait_ge(b_added, t - 1)
                three_products(pe, psB[t % 2][:, :], [a[:, t, :] for a in (mixT_hi, mixT_lo)], [b2_hi[:, :], b2_lo[:, :]])\
                    .then_inc(b_psum, 1)

        @block.vector
        def _(dve):
            dve.memset(mixT_hi[:, :, :], 1.0).then_inc(mix_set, 1)
            dve.memset(mixT_lo[:, :, :], 0.0).then_inc(mix_set, 1)
            dve.wait_ge(b_high, 1)
            dve.tensor_tensor(b2_lo[:, :], b2[:, :], b2_hi[:, :], ALU.subtract).then_inc(b_low, 1)
            for i in range(4):
                dve.wait_ge(mix_high, i + 1)
                dve.tensor_tensor(mixT_lo[0:E_N, 4 * i:4 * i + 4, :], psC[i][:, :, :], mixT_hi[0:E_N, 4 * i:4 * i + 4, :],
                                  ALU.subtract).then_inc(mix_low, 1)
            for t in range(NT):
                x = k.x[:, t, :]
                dve.wait_ge(b_psum, t + 1)
                dve.tensor_tensor(x, x, psB[t % 2][:, :], ALU.add).then_inc(b_added, 1)
                dve.wait_ge(gathered[t % 4], 32 * (t // 4 + 1))
                dve.wait_ge(b_added, t + 1)
                dve.scalar_tensor_tensor(x, got[t % 4][:, 0, :], share[:, 0, t:t + 1], x, ALU.mult, ALU.add).then_inc(first_added, 1)
                dve.wait_ge(first_added, t + 1)
                dve.scalar_tensor_tensor(x, got[t % 4][:, 1, :], share[:, 1, t:t + 1], x, ALU.mult, ALU.add).then_inc(done, 1)


def build(nc, ins, out, scratch):
    with ExitStack() as ctx:
        k = Kernel(nc, ins, out, scratch, ctx)
        left = lambda stack, name, shape, dt: stack.enter_context(nc.sbuf_tensor(name, shape, dt))
        stage_constants(k)
        with ExitStack() as attention:
            with ExitStack() as context:
                ctxT = context.enter_context(nc.sbuf_tensor("ctxT", [P, DC, TOK], F32, side="right"))
                with ExitStack() as low:
                    k.w1T = left(low, "w1T", [P, DC * FF], BF16)
                    k.w2T = left(low, "w2T", [P, FC * D], BF16)
                    stage_ternary_weights(k)
                    mean, quant, dequant = (left(low, n, [P, NT], F32) for n in ("ffn_mean", "ffn_quant", "ffn_dequant"))
                    with ExitStack() as conv:
                        outT = left(conv, "outT", [P, DC, TOK], F32)
                        with ExitStack() as lower:
                            qT = left(lower, "qT", [P, DC, TOK], F32)
                            stage_transposes(k, ctxT, qT)
                            stage_long_conv(k, ctxT, qT, outT)
                        stage_ffn_entry(k, outT, mean, quant, dequant)
                    stage_ffn(k, mean, quant, dequant)
                k.clear_semaphores()
                ks = scratch["keys"]
                v_hi = left(attention, "v_hi", [P, NT, HEADS, VC], BF16)
                v_lo = left(attention, "v_lo", [P, NT, HEADS, VC], BF16)
                qw, ow = (left(attention, n, [P, 2, DC, D], BF16) for n in ("qw", "ow"))
                x_mean, x_rstd = (left(attention, n, [P, NT], F32) for n in ("x_mean", "x_rstd"))
                sel = left(attention, "sel", [P, 2, P], BF16)
                with ExitStack() as kv:
                    kw, vw = (left(kv, n, [P, 2, DC, D], BF16) for n in ("kw", "vw"))
                    vbias = left(kv, "vbias", [P, D], F32)
                    stage_attention_weights(k, (kw, vw, qw, ow), k.vectors, vbias, x_mean, x_rstd, sel)
                    stage_keys_values(k, ctxT, kw, vw, k.vectors, vbias, ks, v_hi, v_lo)
            stage_attention(k, ks, v_hi, v_lo, qw, ow, k.vectors, x_mean, x_rstd, sel)
        slots = left(ctx, "slots", [P, 2, NT], U32)
        share = left(ctx, "share", [P, 2, NT], F32)
        combine = left(ctx, "combine", [P, NT, E_N], F32)
        wrow = left(ctx, "wrow", [P, NBLK], U32)
        with ExitStack() as moe:
            xf = left(moe, "xf", [P, NT, D], F32)
            xT_hi, xT_lo = (left(moe, n, [P, DC, TOK], BF16) for n in ("xT_hi", "xT_lo"))
            xaff = left(moe, "xaff", [P, NT, E_N], F32)
            sgu = left(moe, "sgu", [P, 2, SH_N, 2, DC * FE], BF16)
            sd = left(moe, "sd", [P, 2, SH_N, F2 * D], BF16)
            stage_router(k, xf, xT_hi, xT_lo, xaff, sgu, sd)
            stage_route_and_shared(k, xf, xT_hi, xT_lo, xaff, sgu, sd, slots, share, combine, wrow)
        stage_experts(k, wrow)
        stage_combine(k, slots, share, combine, out)
        k.open_semaphores.close()


def program(nc, ins, out):
    scratch = {"taps": nc.dram_tensor("taps_padded", [H0, PAD + D], F32, kind="Internal").ap(),
               "keys": nc.dram_tensor("keys_stacked", [B, P, HC, DC, S], BF16, kind="Internal").ap(),
               "rows": nc.dram_tensor("expert_rows", [NBLK * BLK, D], F32, kind="Internal").ap(),
               "results": nc.dram_tensor("expert_results", [NBLK * BLK, D], F32, kind="Internal").ap()}
    build(nc, ins, out, scratch)


INPUTS = ["x", "ctx_2048", "L0_xattn_ssm_kernel", "L0_xattn_D", "L0_ffn_w1", "L0_ffn_b1", "L0_ffn_w2", "L0_ffn_b2",
          "L1_xattn_Wq", "L1_xattn_bq", "L1_xattn_gq", "L1_xattn_Wk_img", "L1_xattn_bk_img", "L1_xattn_gk_img",
          "L1_xattn_Wv_img", "L1_xattn_bv_img", "L1_xattn_Wo", "L1_xattn_bo", "L1_ffn_wa", "L1_ffn_rg", "L1_ffn_rgb",
          "L1_ffn_rw1", "L1_ffn_rb1", "L1_ffn_rw2", "L1_ffn_rb2", "L1_ffn_sg", "L1_ffn_sgb", "L1_ffn_sw1",
          "L1_ffn_sb1", "L1_ffn_sw2", "L1_ffn_sb2"]


def kernel(**inputs):
    import concourse.bacc as _bacc
    from concourse.bass_utils import run_bass_kernel_spmd as _run

    nc = _bacc.Bacc("TRN2", target_bir_lowering=False, num_devices=1)
    arrays, ins = {}, {}
    for name in INPUTS:
        a = np.ascontiguousarray(inputs[name])
        arrays[f"in_{name}"] = a
        ins[name] = nc.dram_tensor(f"in_{name}", a.shape, mybir.dt.from_np(a.dtype), kind="ExternalInput").ap()
    out = nc.dram_tensor("out", (B, S, D), F32, kind="ExternalOutput").ap()
    program(nc, ins, out)
    return _run(nc, [arrays], core_ids=[0]).results[0]["out"]
```

```python
from contextlib import ExitStack, contextmanager

import numpy as np

import concourse.bass as bass
from concourse import mybir
from concourse.alu_op_type import AluOpType as ALU

ACT = mybir.ActivationFunctionType
AX = mybir.AxisListType
F32 = mybir.dt.float32
BF16 = mybir.dt.bfloat16
I32 = mybir.dt.int32
U32 = mybir.dt.uint32

P = 128
B, S, D = 8, 256, 512
TOK = B * S
NT = TOK // P
DC = D // P
TPB = S // P
FF = 2048
FC = FF // P
HD0 = 8
H0 = S // HD0
PAIRS = HD0 * (HD0 + 1) // 2
PAD = 128
LN_EPS = 1e-5
ACT_EPS = 1e-5
W_EPS = 1e-8
ROUND = 12582912.0


class Link:

    def __init__(self, engine, sem):
        self.engine, self.sem, self.start, self.n, self.i, self.per = engine, sem, 0, 0, None, 0

    def at(self):
        return self.start + self.n if self.i is None else self.i * self.per + (self.start + self.n)

    def __call__(self, instruction, wait=True):
        instruction.then_inc(self.sem, 1)
        self.n += 1
        if wait:
            self.engine.wait_ge(self.sem, self.at())

    @contextmanager
    def loop(self, count, per):
        self.start, self.n, self.per = self.start + self.n, 0, per
        with self.engine.Fori(0, count) as i:
            self.i = i
            yield i
        assert self.n == per, f"{self.n} steps in the loop's body"
        self.start, self.n, self.i = self.start + count * per, 0, None


def pair_at(i):
    return i * HD0 - i * (i - 1) // 2


class Kernel:

    def __init__(self, nc, ins, out, scratch, ctx):
        self.nc, self.ins, self.out, self.scratch = nc, ins, out, scratch
        sb = lambda name, shape, dt: ctx.enter_context(nc.sbuf_tensor(name, shape, dt))
        self.x = sb("x_res", [P, NT, D], F32)
        self.ident = sb("ident", [P, P], F32)
        self.ident_b = sb("ident_b", [P, P], BF16)
        self.reverse = sb("reverse", [P, P], F32)
        self.ones = sb("ones", [P, P], F32)
        self.small = sb("small", [P, 8], F32)
        self.pow_half = sb("pow_half", [P, NT], F32)
        self.vectors = sb("vectors", [P, 24], F32)
        self.w1T = self.w2T = None
        self.open_semaphores, self.semaphores = ExitStack(), []

    def semaphore(self, name):
        self.semaphores.append(self.open_semaphores.enter_context(self.nc.semaphore(name)))
        return self.semaphores[-1]

    def clear_semaphores(self):
        used, self.semaphores = self.semaphores, []
        with self.nc.Block() as block:
            @block.gpsimd
            def _(pool):
                for s in used:
                    pool.sem_clear(s)
        self.open_semaphores.close()


def stage_constants_and_ternary_weights(k):
    nc = k.nc
    W = FF * D // P
    HALF = 1024
    with ExitStack() as ctx:
        sb = lambda name, shape, dt: ctx.enter_context(nc.sbuf_tensor(name, shape, dt))
        raw = [sb(f"w_raw{i}", [P, W], F32) for i in range(2)]
        tern = [sb(f"w_tern{i}", [P, W], BF16) for i in range(2)]
        total = sb("w_total", [P, 2, 2], F32)
        taps = sb("taps", [H0, PAD + D], F32)
        forwards = sb("taps_forwards", [H0, D], F32)
        skip = sb("skip", [H0, 1], F32)
        inv = sb("w_inv", [P, 2], F32)
        ps_sum = ctx.enter_context(nc.psum_tensor("ps_sum", [P, 2], F32))
        ps_t = [ctx.enter_context(nc.psum_tensor(f"ps_wt{i}", [P, HALF], BF16)) for i in range(4)]
        sem = k.semaphore
        loaded = [[sem(f"w_loaded{w}{h}") for h in range(2)] for w in range(2)]
        zeroed, made = sem("c_zeroed"), sem("c_made")
        taps_loaded, taps_ready, taps_stored = sem("c_tl"), sem("c_tr"), sem("c_ts")
        CONSTANTS = 7
        abs_summed, sum_ready, inv_ready = sem("w_abs"), sem("w_sum"), sem("w_invr")
        scaled, rounded, transposed, copied = sem("w_scaled"), sem("w_rounded"), sem("w_transposed"), sem("w_copied")
        copied_even, dve_step = sem("w_copied_even"), sem("w_dve")
        x_loaded = sem("w_x")
        block = ctx.enter_context(nc.Block())
        GROUPS = W // HALF

        def group(wi, g):
            for j in range(HALF // P):
                col = g * HALF + j * P
                if wi == 0:
                    c, a = col // FF, col % FF // P
                    yield j, a * D + c * P
                else:
                    c, a = col // D, col % D // P
                    yield j, a * FF + c * P

        @block.sync
        def _(sp):
            def load(wi, h):
                n, name = ((D, "L0_ffn_w1"), (FF, "L0_ffn_w2"))[wi]
                a = W // n // 2
                sp.dma_start(raw[wi][:, h * W // 2:(h + 1) * W // 2].rearrange("p (a n) -> p a n", n=n),
                             k.ins[name].rearrange("(a p) n -> p a n", p=P)[:, h * a:(h + 1) * a, :]).then_inc(loaded[wi][h], 16)

            load(0, 0)
            load(0, 1)
            sp.dma_start(forwards[:, :], k.ins["L0_xattn_ssm_kernel"]).then_inc(taps_loaded, 16)
            sp.dma_start(skip[:, :], k.ins["L0_xattn_D"].rearrange("(h o) -> h o", o=1)).then_inc(taps_loaded, 16)
            load(1, 0)
            load(1, 1)
            x_dram = k.ins["x"].rearrange("b s d -> (b s) d").rearrange("(t p) d -> p t d", p=P)
            sp.dma_start(k.x[:, :, :], x_dram).then_inc(x_loaded, 16)
            sp.wait_ge(taps_ready, 3)
            sp.dma_start(k.scratch["taps"], taps[:, :]).then_inc(taps_stored, 16)
            sp.wait_ge(taps_stored, 16)
            sp.wait_ge(x_loaded, 16)

        @block.gpsimd
        def _(pool):
            pool.memset(k.small[:, 0:3], ROUND).then_inc(made, 1)
            pool.memset(k.small[:, 3:4], LN_EPS).then_inc(made, 1)
            pool.memset(k.ones[:, :], 1.0).then_inc(made, 1)
            pool.memset(k.pow_half[:, :], -0.5).then_inc(made, 1)
            for m in (k.ident, k.ident_b, k.reverse):
                pool.memset(m[:, :], 0.0).then_inc(zeroed, 1)
            pool.wait_ge(zeroed, 3)
            for m, base, step in ((k.ident, 0, -1), (k.ident_b, 0, -1), (k.reverse, 1 - P, 1)):
                pool.affine_select(out=m[:, :], in_=m[:, :], compare_op=ALU.not_equal, fill=1.0, base=base,
                                   pattern=[[step, P]], channel_multiplier=1).then_inc(made, 1)

        @block.scalar
        def _(act):
            act.wait_ge(made, CONSTANTS)
            for wi in range(2):
                for h in range(2):
                    act.wait_ge(loaded[wi][h], 16)
                    half = slice(h * W // 2, (h + 1) * W // 2)
                    act.activation(tern[wi][:, half], raw[wi][:, half], ACT.Abs,
                                   accum_out=total[:, wi, h:h + 1]).then_inc(abs_summed, 1)
                act.wait_ge(inv_ready, wi + 1)
                act.activation(raw[wi][:, :], raw[wi][:, :], ACT.Identity, bias=k.small[:, 2:3],
                               scale=inv[:, wi:wi + 1]).then_inc(scaled, 1)
            for n in range(1, 2 * GROUPS, 2):
                act.wait_ge(transposed, n + 1)
                dst = (k.w1T, k.w2T)[n // GROUPS]
                act.activation(dst[:, n % GROUPS * HALF:(n % GROUPS + 1) * HALF], ps_t[n % 4][:, :],
                               ACT.Copy).then_inc(copied, 1)

        @block.tensor
        def _(pe):
            pe.wait_ge(made, CONSTANTS)
            for wi in range(2):
                pe.wait_ge(abs_summed, 2 * wi + 2)
                if wi:
                    pe.wait_ge(inv_ready, wi)
                for h in range(2):
                    last = pe.matmul(ps_sum[:, wi:wi + 1], k.ones[:, :], total[:, wi, h:h + 1], start=(h == 0), stop=(h == 1))
                last.then_inc(sum_ready, 1)
            for wi in range(2):
                pe.wait_ge(rounded, wi + 1)
                for g in range(GROUPS):
                    n = wi * GROUPS + g
                    if n >= 4:
                        pe.wait_ge(copied if n % 2 else copied_even, (n - 4) // 2 + 1)
                    for j, at in group(wi, g):
                        last = pe.transpose(ps_t[n % 4][:, j * P:(j + 1) * P], tern[wi][:, at:at + P],
                                            k.ident_b[:, :])
                    last.then_inc(transposed, 1)

        @block.vector
        def _(dve):
            dve.memset(taps[:, D:], 0.0).then_inc(taps_ready, 1)
            dve.wait_ge(taps_loaded, 32)
            dve.tensor_copy(taps[:, D - 2::-1], forwards[:, 1:]).then_inc(taps_ready, 1)
            dve.tensor_tensor(taps[:, D - 1:D], forwards[:, 0:1], skip[:, :], ALU.add).then_inc(taps_ready, 1)
            link = Link(dve, dve_step)
            for wi in range(2):
                dve.wait_ge(sum_ready, wi + 1)
                dve.wait_ge(made, CONSTANTS)
                link(dve.tensor_scalar(k.small[:, wi:wi + 1], ps_sum[:, wi:wi + 1], 1.0 / (FF * D), W_EPS,
                                       ALU.mult, ALU.max))
                dve.reciprocal(inv[:, wi:wi + 1], k.small[:, wi:wi + 1]).then_inc(inv_ready, 1)
            for wi in range(2):
                dve.wait_ge(scaled, wi + 1)
                link(dve.tensor_scalar(raw[wi][:, :], raw[wi][:, :], ROUND - 1.0, ROUND + 1.0, ALU.max, ALU.min))
                dve.tensor_scalar(tern[wi][:, :], raw[wi][:, :], ROUND, None, ALU.subtract).then_inc(rounded, 1)
                for n in range(wi * GROUPS, (wi + 1) * GROUPS, 2):
                    dve.wait_ge(transposed, n + 1)
                    dst = (k.w1T, k.w2T)[wi]
                    dve.tensor_copy(dst[:, n % GROUPS * HALF:(n % GROUPS + 1) * HALF], ps_t[n % 4][:, :])\
                       .then_inc(copied_even, 1)


def stage_transposes(k, ctxT, qT):
    nc = k.nc
    with ExitStack() as ctx:
        sb = lambda name, shape, dt: ctx.enter_context(nc.sbuf_tensor(name, shape, dt))
        c_in = [sb(f"c_in{i}", [P, D], F32) for i in range(4)]
        xn = [sb(f"xn{i}", [P, D], F32) for i in range(4)]
        stats = sb("t_stats", [P, NT, 6], F32)
        mean = sb("t_mean", [P, NT], F32)
        var = sb("t_var", [P, NT], F32)
        diff = sb("t_diff", [P, NT], F32)
        rstd = sb("t_rstd", [P, NT], F32)
        ps = [ctx.enter_context(nc.psum_tensor(f"ps_tr{i}", [P, D], F32)) for i in range(4)]
        sem = k.semaphore
        c_loaded = [sem(f"t_c{i}") for i in range(4)]
        c_used, transposed, evacuated = sem("t_cused"), sem("t_transposed"), sem("t_evac")
        var_ready, rstd_ready, xn_ready, dve_step = sem("t_var"), sem("t_rstd"), sem("t_xn"), sem("t_dve")
        block = ctx.enter_context(nc.Block())
        c_dram = k.ins["ctx_2048"].rearrange("b s d -> (b s) d")

        @block.sync
        def _(sp):
            with sp.Fori(0, NT // 4) as i:
                for j in range(4):
                    sp.wait_ge(c_used, i * 4 + (j + 1))
                    sp.dma_start(c_in[j][:, :], c_dram[bass.ds(i * (4 * P) + j * P, P), :]).then_inc(c_loaded[j], 16)

        @block.tensor
        def _(pe):
            pe.sem_inc(c_used, 4)
            with pe.Fori(0, NT // 4) as i:
                for j in range(4):
                    pe.wait_ge(c_loaded[j], i * 16 + 16)
                    pe.wait_ge(evacuated, i * 4 + (j + 1))
                    for c in range(DC):
                        last = pe.transpose(ps[j][:, c * P:(c + 1) * P], c_in[j][:, c * P:(c + 1) * P], k.ident[:, :])
                    last.then_inc(transposed, 1)
                    pe.wait_ge(transposed, i * 4 + (j + 1))
                    pe.sem_inc(c_used, 1)
            with pe.Fori(0, NT // 4) as i:
                for j in range(4):
                    pe.wait_ge(xn_ready, i * 4 + (j + 1))
                    pe.wait_ge(evacuated, i * 4 + (NT + j + 1))
                    for c in range(DC):
                        last = pe.transpose(ps[j][:, c * P:(c + 1) * P], xn[j][:, (DC - 1 - c) * P:(DC - c) * P], k.ident[:, :])
                    last.then_inc(transposed, 1)

        @block.scalar
        def _(act):
            act.sem_inc(evacuated, 4)
            for n, dst in enumerate((ctxT, qT)):
                with act.Fori(0, NT // 4) as i:
                    for j in range(4):
                        act.wait_ge(transposed, i * 4 + (NT * n + j + 1))
                        act.activation(dst[:, :, bass.ds(i * (4 * P) + j * P, P)],
                                       ps[j][:, :].rearrange("p (c t) -> p c t", c=DC), ACT.Copy).then_inc(evacuated, 1)

        @block.vector
        def _(dve):
            link = Link(dve, dve_step)
            for t in range(NT):
                link(dve.bn_stats(stats[:, t, :], k.x[:, t, :]), wait=False)
            dve.wait_ge(dve_step, NT)
            mean_var(link, dve, stats, mean[:, :], var[:, :], diff[:, :], LN_EPS)
            dve.sem_inc(var_ready, 1)
            dve.wait_ge(rstd_ready, 1)
            with dve.Fori(0, NT // 4) as i:
                for j in range(4):
                    dve.wait_ge(transposed, i * 4 + (NT + j - 3))
                    t = bass.ds(i * 4 + j, 1)
                    dve.tensor_scalar(xn[j][:, ::-1], k.x[:, t, :], mean[:, t], rstd[:, t], ALU.subtract, ALU.mult)\
                       .then_inc(xn_ready, 1)

        @block.gpsimd
        def _(pool):
            pool.wait_ge(var_ready, 1)
            pool.tensor_tensor(rstd[:, :], var[:, :], k.pow_half[:, :], ALU.pow).then_inc(rstd_ready, 1)


def stage_long_conv(k, ctxT, qT, outT):
    nc = k.nc
    BP = B * PAIRS
    with ExitStack() as ctx:
        sb = lambda name, shape, dt: ctx.enter_context(nc.sbuf_tensor(name, shape, dt))
        toep = [sb(f"toep{i}", [P, D], F32) for i in range(2)]
        kv = [sb(f"kv{i}", [P, DC, B, PAIRS], F32) for i in range(2)]
        prod = [sb(f"prod{i}", [P, DC, B, HD0, HD0], F32) for i in range(2)]
        Y = [ctx.enter_context(nc.psum_tensor(f"ps_y{i}", [P, DC, 512], F32)) for i in range(2)]
        sem = k.semaphore
        toep_loaded = [sem("a_toep0"), sem("a_toep1")]
        kv_ready, conv_done, y_read, prod_ready, reduced = (sem(f"a_{n}") for n in ("kv", "conv", "yread", "prod", "red"))
        block = ctx.enter_context(nc.Block())
        taps = k.scratch["taps"]
        ctx4 = ctxT[:, :, :].rearrange("p c (b s) -> p c b s", b=B)
        q4 = qT[:, :, :].rearrange("p c (b s) -> p c b s", b=B)
        o4 = outT[:, :, :].rearrange("p c (b s) -> p c b s", b=B)

        @block.sync
        def _(sp):
            with sp.Fori(0, H0 // 2) as i:
                for p in range(2):
                    sp.wait_ge(conv_done, i * 2 + (p + 1))
                    row = taps[bass.ds(i * 2 + p, 1), 0:D]
                    src = bass.AP(tensor=row.tensor, offset=row.offset, ap=[[1, P], [1, D]])
                    sp.dma_start(toep[p][:, :], src).then_inc(toep_loaded[p], 16)

        @block.gpsimd
        def _(pool):
            with pool.Fori(0, H0 // 2) as i:
                for p in range(2):
                    pool.wait_ge(conv_done, i * 2 + (p + 1))
                    for c in range(HD0):
                        n = HD0 - c
                        at = i * (2 * HD0) + (p * HD0 + c)
                        last = pool.tensor_tensor(kv[p][:, :, :, pair_at(c):pair_at(c) + n],
                                                  ctx4[:, :, :, bass.ds(at, 1)].broadcast_to([P, DC, B, n]),
                                                  ctx4[:, :, :, bass.ds(at, n)], ALU.mult)
                    last.then_inc(kv_ready, 1)

        @block.tensor
        def _(pe):
            pe.sem_inc(conv_done, 2)
            with pe.Fori(0, H0 // 2) as i:
                for p in range(2):
                    pe.wait_ge(toep_loaded[p], i * 16 + 16)
                    pe.wait_ge(kv_ready, i * 2 + (p + 1))
                    pe.wait_ge(y_read, i * 2 + (p + 1))
                    for l in range(DC):
                        for m in range(l + 1):
                            last = pe.matmul(Y[p][:, l, 0:BP], toep[p][:, (DC - 1 - l + m) * P:(DC - l + m) * P],
                                             kv[p][:, m, :, :].rearrange("p b n -> p (b n)"),
                                             start=(m == 0), stop=(m == l))
                    last.then_inc(conv_done, 1)

        @block.vector
        def _(dve):
            dve.sem_inc(y_read, 2)
            with dve.Fori(0, H0 // 2) as i:
                for p in range(2):
                    dve.wait_ge(conv_done, i * 2 + (p + 3))
                    y = Y[p][:, :, 0:BP].rearrange("p c (b n) -> p c b n", b=B)
                    for c in range(HD0):
                        n = HD0 - c
                        at = i * (2 * HD0) + (p * HD0 + c)
                        dve.tensor_tensor(prod[p][:, :, :, c:, c], y[:, :, :, pair_at(c):pair_at(c) + n],
                                          q4[:, :, :, bass.ds(at, 1)].broadcast_to([P, DC, B, n]), ALU.mult)\
                           .then_inc(prod_ready, 1)
                        if n > 1:
                            last = dve.tensor_tensor(prod[p][:, :, :, c, c + 1:],
                                                     y[:, :, :, pair_at(c) + 1:pair_at(c) + n],
                                                     q4[:, :, :, bass.ds(at + 1, n - 1)], ALU.mult)
                            last.then_inc(prod_ready, 1)
                    per = 2 * HD0 - 1
                    dve.wait_ge(prod_ready, i * (2 * per) + (p + 1) * per)
                    dve.sem_inc(y_read, 1)
                    dve.tensor_reduce(o4[:, :, :, bass.ds(i * (2 * HD0) + p * HD0, HD0)], prod[p][:, :, :, :, :],
                                      AX.X, ALU.add).then_inc(reduced, 1)


def known(n):
    return isinstance(n, int)


def mean_var(link, dve, stats, mean, var, tmp, eps):
    link(dve.tensor_tensor(mean, stats[:, :, 1], stats[:, :, 4], ALU.add))
    link(dve.tensor_scalar(mean, mean, 0.5, None, ALU.mult))
    link(dve.tensor_tensor(tmp, stats[:, :, 1], stats[:, :, 4], ALU.subtract))
    link(dve.tensor_tensor(tmp, tmp, tmp, ALU.mult))
    link(dve.tensor_tensor(var, stats[:, :, 2], stats[:, :, 5], ALU.add))
    link(dve.tensor_scalar(var, var, 1.0 / D, eps, ALU.mult, ALU.add))
    link(dve.scalar_tensor_tensor(var, tmp, 0.25, var, ALU.mult, ALU.add))


def stage_ffn_entry(k, outT, mean, quant, dequant, b1, b2):
    nc = k.nc
    with ExitStack() as ctx:
        sb = lambda name, shape, dt: ctx.enter_context(nc.sbuf_tensor(name, shape, dt))
        part = [sb(f"e_part{i}", [P, DC, P], F32) for i in range(4)]
        stats = sb("e_stats", [P, NT, 6], F32)
        hi, lo, var, tmp, r1 = (sb(f"e_{n}", [P, NT], F32) for n in ("hi", "lo", "var", "tmp", "r1"))
        ps = [ctx.enter_context(nc.psum_tensor(f"ps_e{i}", [P, D], F32)) for i in range(4)]
        sem = k.semaphore
        staged, transposed, added, seen, dve_step, var_ready, r_ready = (
            sem(f"e_{n}") for n in ("staged", "transposed", "added", "seen", "dve", "varr", "rr"))
        b_loaded = k.semaphore("e_bload")
        block = ctx.enter_context(nc.Block())

        @block.sync
        def _(sp):
            for dst, name, n in ((b1, "L0_ffn_b1", FF), (b2, "L0_ffn_b2", D)):
                sp.dma_start(dst[:, :], broadcast_rows(k.ins[name], n)).then_inc(b_loaded, 16)
            sp.wait_ge(b_loaded, 32)

        @block.scalar
        def _(act):
            with act.Fori(0, NT // 4) as i:
                for j in range(4):
                    act.wait_ge(transposed, i * 4 + (j + 1))
                    act.activation(part[j][:, :, :], outT[:, :, bass.ds(i * (4 * P) + j * P, P)], ACT.Copy).then_inc(staged, 1)

        @block.gpsimd
        def _(pool):
            pool.wait_ge(var_ready, 1)
            pool.tensor_tensor(r1[:, :], var[:, :], k.pow_half[:, :], ALU.pow).then_inc(r_ready, 1)

        @block.tensor
        def _(pe):
            pe.sem_inc(transposed, 4)
            with pe.Fori(0, NT // 4) as i:
                for j in range(4):
                    pe.wait_ge(staged, i * 4 + (j + 1))
                    pe.wait_ge(added, i * 4 + (j + 1))
                    for c in range(DC):
                        last = pe.matmul(ps[j][:, c * P:(c + 1) * P], part[j][:, c, :], k.reverse[:, :], start=True, stop=True)
                    last.then_inc(transposed, 1)

        @block.vector
        def _(dve):
            link = Link(dve, dve_step)
            dve.sem_inc(added, 4)
            with dve.Fori(0, NT // 4) as i:
                for j in range(4):
                    t = bass.ds(i * 4 + j, 1)
                    dve.wait_ge(transposed, i * 4 + (j + 5))
                    dve.tensor_tensor(k.x[:, t, :], k.x[:, t, :], ps[j][:, :].unsqueeze(1), ALU.add).then_inc(added, 1)
                    dve.wait_ge(added, i * 4 + (j + 5))
                    dve.bn_stats(stats[:, t, :], k.x[:, t, :]).then_inc(seen, 1)
                    dve.tensor_reduce(hi[:, t], k.x[:, t, :], AX.X, ALU.max).then_inc(seen, 1)
                    dve.tensor_reduce(lo[:, t], k.x[:, t, :], AX.X, ALU.min).then_inc(seen, 1)
            dve.wait_ge(seen, 3 * NT)
            mean_var(link, dve, stats, mean[:, :], var[:, :], tmp[:, :], 0.0)
            link(dve.tensor_scalar(var[:, :], var[:, :], 1.0 + LN_EPS, LN_EPS * LN_EPS, ALU.mult, ALU.add))
            dve.sem_inc(var_ready, 1)
            link(dve.tensor_tensor(hi[:, :], hi[:, :], mean[:, :], ALU.subtract))
            link(dve.tensor_tensor(lo[:, :], mean[:, :], lo[:, :], ALU.subtract))
            link(dve.tensor_tensor(hi[:, :], hi[:, :], lo[:, :], ALU.max))
            dve.wait_ge(r_ready, 1)
            link(dve.tensor_tensor(hi[:, :], hi[:, :], r1[:, :], ALU.mult))
            link(dve.tensor_scalar(hi[:, :], hi[:, :], ACT_EPS, None, ALU.max))
            link(dve.reciprocal(tmp[:, :], hi[:, :]))
            link(dve.tensor_tensor(tmp[:, :], tmp[:, :], r1[:, :], ALU.mult))
            link(dve.tensor_scalar(quant[:, :], tmp[:, :], 127.0, None, ALU.mult))
            link(dve.tensor_scalar(dequant[:, :], hi[:, :], 1.0 / 127.0, k.small[:, 0:1], ALU.mult, ALU.mult))


def stage_ffn(k, mean, quant, dequant, b1, b2):
    nc = k.nc
    with ExitStack() as ctx:
        sb = lambda name, shape, dt: ctx.enter_context(nc.sbuf_tensor(name, shape, dt))
        scaled = [sb(f"f_scaled{i}", [P, D], F32) for i in range(2)]
        qa = [sb(f"f_qa{i}", [P, D], BF16) for i in range(2)]
        qaT = [sb(f"f_qaT{i}", [P, DC, P], BF16) for i in range(2)]
        h = [sb(f"f_h{i}", [P, FF], F32) for i in range(2)]
        qb = [sb(f"f_qb{i}", [P, FF], BF16) for i in range(2)]
        qbT = [sb(f"f_qbT{i}", [P, FC, P], BF16) for i in range(2)]
        squares = sb("f_squares", [P, FF], BF16)
        SUM, SQUARE_SUM, NEG_MEAN, VAR, RSTD, AMAX, INV, QUANT, DEQUANT = range(9)
        sc = [sb(f"f_sc{i}", [P, 9], F32) for i in range(2)]
        col = lambda p, c: sc[p][:, c:c + 1]
        psT = ctx.enter_context(nc.psum_tensor("ps_fT", [P, DC, P], BF16))
        psH = [ctx.enter_context(nc.psum_tensor(f"ps_fH{i}", [P, 512], F32)) for i in range(DC)]
        psQ = [ctx.enter_context(nc.psum_tensor(f"ps_fQ{i}", [P, 8, P], BF16)) for i in range(2)]
        psY = ctx.enter_context(nc.psum_tensor("ps_fY", [P, D], F32))
        sem = lambda name: k.semaphore(("f_" + name))
        dve_step, zeros_set, zeroed, squared, var_ready = (sem(n) for n in ("dve", "zs", "zd", "sq", "var"))
        zeros = sb("f_zeros", [P, 4 * D], BF16)
        qa_ready, qaT_psum, qaT_ready, h_psum, hb_ready, gelu_done = (
            sem(n) for n in ("qa", "qaTp", "qaT", "hp", "hb", "gelu"))
        mean_ready, rstd_ready, centred, quant_ready, h_scaled, qb_ready = (
            sem(n) for n in ("mean", "rstd", "cent", "quant", "hsc", "qb"))
        qbT_psum, y_psum, y_added, biased = (sem(n) for n in ("qbTp", "yp", "ya", "biased"))
        qbT_ready = [sem("qbT0"), sem("qbT1")]
        block = ctx.enter_context(nc.Block())
        tile = lambda t: k.x[:, bass.ds(t, 1), :]
        one = lambda a, t: a[:, bass.ds(t, 1)]

        runs = lambda n, ahead: not known(n) or 0 <= n + ahead < NT

        @block.sync
        def _(sp):
            sp.wait_ge(zeros_set, 1)
            rows = k.scratch["rows"].rearrange("(j p) d -> j p d", p=2 * P)
            with sp.Fori(0, NBLK * BLK // (2 * P)) as i:
                sp.dma_start(rows[bass.ds(i, 1), :, :].rearrange("o (p s) d -> (o p) (s d)", s=2), zeros[:, :]).then_inc(zeroed, 16)
            sp.wait_ge(zeroed, 16 * (NBLK * BLK // (2 * P)))

        @block.vector
        def _(dve):
            link = Link(dve, dve_step)

            def quantise_x(t, p):
                if not known(t) or t >= 2:
                    dve.wait_ge(qaT_psum, t - 1)
                link(dve.tensor_scalar(scaled[p][:, :], tile(t), one(mean, t), one(quant, t), ALU.subtract, ALU.mult))
                dve.tensor_scalar(qa[p][:, :], scaled[p][:, :], ROUND, ROUND, ALU.add, ALU.subtract).then_inc(qa_ready, 1)

            def add_bias1(t, p):
                dve.wait_ge(h_psum, t + 1)
                if not known(t) or t >= 2:
                    dve.wait_ge(qb_ready, t - 1)
                for c in range(DC):
                    dve.scalar_tensor_tensor(h[p][:, c * 512:(c + 1) * 512], psH[c][:, :], one(dequant, t),
                                             b1[:, c * 512:(c + 1) * 512], ALU.mult, ALU.add).then_inc(hb_ready, 1)

            def mean_of(t, p):
                dve.wait_ge(gelu_done, t + 1)
                dve.tensor_scalar(col(p, NEG_MEAN), col(p, SUM), -1.0 / FF, None, ALU.mult).then_inc(mean_ready, 1)

            def copy_qbT(t, p):
                dve.wait_ge(qbT_psum, t * 2 + 2)
                dve.tensor_copy(qbT[p][:, 8:, :], psQ[1][:, :, :]).then_inc(qbT_ready[1], 1)

            def farthest(t, p):
                dve.wait_ge(centred, t + 1)
                link(dve.tensor_reduce(col(p, AMAX), h[p][:, :], AX.X, ALU.max, apply_absolute_value=True))

            def scale_of(t, p):
                dve.wait_ge(rstd_ready, t + 1)
                link(dve.tensor_scalar(col(p, AMAX), col(p, AMAX), col(p, RSTD), ACT_EPS, ALU.mult, ALU.max))
                link(dve.reciprocal(col(p, INV), col(p, AMAX)))
                dve.tensor_scalar(col(p, QUANT), col(p, INV), 127.0, col(p, RSTD), ALU.mult, ALU.mult).then_inc(quant_ready, 1)
                link(dve.tensor_scalar(col(p, DEQUANT), col(p, AMAX), 1.0 / 127.0, k.small[:, 1:2], ALU.mult, ALU.mult), wait=False)

            def round_h(t, p):
                dve.wait_ge(h_scaled, t + 1)
                dve.tensor_scalar(qb[p][:, :], h[p][:, :], ROUND, None, ALU.subtract).then_inc(qb_ready, 1)

            def add_y(t, p):
                dve.wait_ge(y_psum, t + 1)
                dve.wait_ge(biased, t + 1)
                dve.scalar_tensor_tensor(tile(t), psY[:, :].unsqueeze(1), col(p, DEQUANT), tile(t), ALU.mult, ALU.add)\
                   .then_inc(y_added, 1)

            def step(n, p):
                if runs(n, -2):
                    copy_qbT(n - 2, p)
                if runs(n, -1):
                    farthest(n - 1, 1 - p)
                    scale_of(n - 1, 1 - p)
                if runs(n, 0):
                    add_bias1(n, p)
                if runs(n, -1):
                    round_h(n - 1, 1 - p)
                if runs(n, 2):
                    quantise_x(n + 2, p)
                if runs(n, 0):
                    mean_of(n, p)
                if runs(n, -2):
                    add_y(n - 2, p)

            quantise_x(0, 0)
            quantise_x(1, 1)
            step(0, 0)
            step(1, 1)
            with link.loop((NT - 4) // 2, 10) as i:
                for p in range(2):
                    step(i * 2 + (p + 2), p)
            for n in range(NT - 2, NT + 2):
                step(n, n % 2)

        @block.scalar
        def _(act):
            def copy_qaT(t, p):
                act.wait_ge(qaT_psum, t + 1)
                act.activation(qaT[p][:, :, :], psT[:, :, :], ACT.Copy).then_inc(qaT_ready, 1)

            def gelu(t, p):
                act.wait_ge(hb_ready, t * 4 + 4)
                act.activation(h[p][:, :], h[p][:, :], ACT.Gelu, accum_out=col(p, SUM)).then_inc(gelu_done, 1)

            def square(t, p):
                act.wait_ge(centred, t + 1)
                if not known(t) or t:
                    act.wait_ge(squared, t)
                act.activation(squares[:, :], h[p][:, :], ACT.Square, accum_out=col(p, SQUARE_SUM)).then_inc(squared, 1)
                act.wait_ge(squared, t + 1)
                act.activation(col(p, VAR), col(p, SQUARE_SUM), ACT.Identity, scale=1.0 / FF, bias=k.small[:, 3:4]).then_inc(var_ready, 1)

            def copy_qbT(t, p):
                act.wait_ge(qbT_psum, t * 2 + 1)
                act.activation(qbT[p][:, 0:8, :], psQ[0][:, :, :], ACT.Copy).then_inc(qbT_ready[0], 1)

            def centre(t, p):
                act.wait_ge(mean_ready, t + 1)
                act.activation(h[p][:, :], h[p][:, :], ACT.Identity, bias=col(p, NEG_MEAN)).then_inc(centred, 1)

            def scale(t, p):
                act.wait_ge(quant_ready, t + 1)
                act.activation(h[p][:, :], h[p][:, :], ACT.Identity, bias=k.small[:, 2:3],
                               scale=col(p, QUANT)).then_inc(h_scaled, 1)

            def step(n, p):
                if runs(n, 1):
                    copy_qaT(n + 1, 1 - p)
                if runs(n, -2):
                    copy_qbT(n - 2, p)
                if runs(n, -1):
                    scale(n - 1, 1 - p)
                if runs(n, 0):
                    gelu(n, p)
                    centre(n, p)
                    square(n, p)

            copy_qaT(0, 0)
            step(0, 0)
            step(1, 1)
            with act.Fori(0, (NT - 4) // 2) as i:
                for p in range(2):
                    step(i * 2 + (p + 2), p)
            for n in range(NT - 2, NT + 2):
                step(n, n % 2)

        @block.gpsimd
        def _(pool):
            pool.memset(zeros[:, :], 0.0).then_inc(zeros_set, 1)

            def add_bias2(t, p):
                pool.wait_ge(qa_ready, t + 1)
                pool.tensor_tensor(tile(t), tile(t), b2[:, :].unsqueeze(1), ALU.add).then_inc(biased, 1)

            def step(n, p):
                pool.wait_ge(var_ready, n + 1)
                pool.tensor_tensor(col(p, RSTD), col(p, VAR), k.pow_half[:, 0:1], ALU.pow).then_inc(rstd_ready, 1)
                if runs(n, 2):
                    add_bias2(n + 2, p)

            add_bias2(0, 0)
            add_bias2(1, 1)
            with pool.Fori(0, NT // 2 - 1) as i:
                for p in range(2):
                    step(i * 2 + p, p)
            for n in range(NT - 2, NT):
                step(n, n % 2)

        @block.tensor
        def _(pe):
            def transpose_qa(t, p):
                pe.wait_ge(qa_ready, t + 1)
                if not known(t) or t:
                    pe.wait_ge(qaT_ready, t)
                for c in range(DC):
                    last = pe.transpose(psT[:, c, :], qa[p][:, c * P:(c + 1) * P], k.ident_b[:, :])
                last.then_inc(qaT_psum, 1)

            def up(t, p):
                pe.wait_ge(qaT_ready, t + 1)
                if not known(t) or t:
                    pe.wait_ge(hb_ready, t * 4)
                for f in range(DC):
                    for c in range(DC):
                        last = pe.matmul(psH[f][:, :], qaT[p][:, c, :], k.w1T[:, c * FF + f * 512:c * FF + (f + 1) * 512],
                                         start=(c == 0), stop=(c == DC - 1))
                last.then_inc(h_psum, 1)

            def transpose_qb(t, p):
                pe.wait_ge(qb_ready, t + 1)
                for g in range(2):
                    if not known(t) or t:
                        pe.wait_ge(qbT_ready[g], t)
                    for c in range(8):
                        last = pe.transpose(psQ[g][:, c, :], qb[p][:, (8 * g + c) * P:(8 * g + c + 1) * P], k.ident_b[:, :])
                    last.then_inc(qbT_psum, 1)

            def down(t, p):
                if not known(t) or t:
                    pe.wait_ge(y_added, t)
                for c in range(FC):
                    if c % 8 == 0:
                        pe.wait_ge(qbT_ready[c // 8], t + 1)
                    last = pe.matmul(psY[:, :], qbT[p][:, c, :], k.w2T[:, c * D:(c + 1) * D],
                                     start=(c == 0), stop=(c == FC - 1))
                last.then_inc(y_psum, 1)

            def step(n, p):
                if runs(n, 1):
                    transpose_qa(n + 1, 1 - p)
                if runs(n, -2):
                    down(n - 2, p)
                if runs(n, -1):
                    transpose_qb(n - 1, 1 - p)
                if runs(n, 1):
                    up(n + 1, 1 - p)

            transpose_qa(0, 0)
            up(0, 0)
            step(0, 0)
            step(1, 1)
            with pe.Fori(0, (NT - 4) // 2) as i:
                for p in range(2):
                    step(i * 2 + (p + 2), p)
            for n in range(NT - 2, NT + 2):
                step(n, n % 2)


RMS_EPS = 1e-6
HEADS, HD = 16, 32
HC = P // HD
UNITS = HEADS // 2
VC = HD + 1
ROWS = {"bq": 0, "gq": 4, "bk": 8, "gk": 12, "sgb": 16, "sb1": 20}
SCORE_SCALE = float(HD) ** -0.5


def broadcast_rows(src, n):
    return bass.AP(tensor=src.tensor, offset=0, ap=[[0, P], [1, n]])


def three_products(pe, out, stationary, moving, first=True, last=True):
    for n, (a, b) in enumerate(((0, 0), (0, 1), (1, 0))):
        instruction = pe.matmul(out, stationary[a], moving[b], start=first and n == 0, stop=last and n == 2)
    return instruction


def square_sums(pe, k, out, sq):
    for t in range(TPB):
        for c in range(DC):
            last = pe.matmul(out[:, t:t + 1], sq[:, c, t * P:(t + 1) * P], k.ones[:, 0:1], start=(c == 0), stop=(c == DC - 1))
    return last


def spread_on_diagonals(dve, k, diag, r):
    for t in range(TPB):
        last = dve.tensor_scalar(diag[:, t, :], k.ident[:, :], r[:, t:t + 1], None, ALU.mult)
    return last


KEY_INCS = 16 * 4
STACK_INCS = 16 * HC * 4


def stage_keys_values(k, ctxT, kw, vw, qw, ow, vectors, vbias, ks, v_hi, v_lo, x_mean, x_rstd, sel):
    nc = k.nc
    with ExitStack() as ctx:
        sb = lambda name, shape, dt: ctx.enter_context(nc.sbuf_tensor(name, shape, dt))
        c_hi = [sb(f"kv_chi{i}", [P, DC, S], BF16) for i in range(2)]
        c_lo = [sb(f"kv_clo{i}", [P, DC, S], BF16) for i in range(2)]
        u = [sb(f"kv_u{i}", [P, DC, S], F32) for i in range(2)]
        sq = sb("kv_sq", [P, DC, S], F32)
        v, r = (sb(f"kv_{n}", [P, TPB], F32) for n in ("v", "r"))
        diag = sb("kv_diag", [P, TPB, P], F32)
        kn = sb("kv_kn", [P, DC, S], F32)
        k_hi = [sb(f"kv_khi{i}", [P, DC, S], BF16) for i in range(2)]
        k_lo = [sb(f"kv_klo{i}", [P, DC, S], BF16) for i in range(2)]
        vf = [sb(f"kv_vf{i}", [P, D], F32) for i in range(2)]
        split, names = (kw, vw, qw, ow), ("L1_xattn_Wk_img", "L1_xattn_Wv_img", "L1_xattn_Wq", "L1_xattn_Wo")
        raw = [sb(f"kv_raw{i}", [P, DC, D], F32) for i in range(2)]
        rows = sb("kv_rows", [P, P], F32)
        stats = sb("kv_stats", [P, NT, 6], F32)
        x_var, tmp = (sb(f"kv_{n}", [P, NT], F32) for n in ("xvar", "tmp"))
        psW = ctx.enter_context(nc.psum_tensor("ps_kw", [P, P], F32))
        psK = [ctx.enter_context(nc.psum_tensor(f"ps_k{i}", [P, 2, S], F32)) for i in range(2)]
        psV = [ctx.enter_context(nc.psum_tensor(f"ps_v{i}", [P, D], F32)) for i in range(2)]
        psR = ctx.enter_context(nc.psum_tensor("ps_r", [P, 2, S], F32))
        sem = lambda name: k.semaphore(("k_" + name))
        c_high, c_low, k_psum, v_psum, squared, sum_psum, var_ready, r_ready, diag_ready, r_psum = (
            sem(n) for n in ("ch", "cl", "kp", "vp", "sq", "sp", "vr", "rr", "di", "rp"))
        normed, k_high, k_low, v_full, v_high = (sem(n) for n in ("norm", "kh", "kl", "vf", "vh"))
        stacked, w_loaded = [sem("st0"), sem("st1")], [sem("wl0"), sem("wl1")]
        w_high, w_low, rows_zeroed, rows_loaded, rows_turned, vectors_ready, dve_step, b_loaded, stat_done, x_var_ready, sel_set = (
            sem(n) for n in ("wh", "wlo", "rz", "rl", "rt", "ve", "dve", "bl", "sd", "xv", "sel"))
        block = ctx.enter_context(nc.Block())
        at = lambda b: bass.ds(b * S, S)
        heads = lambda a: a.rearrange("p (o h d) -> p o h d", o=1, d=HD)
        vtile = lambda a, b, t: a[:, bass.ds(b * 2 + t, 1), :, 0:HD]

        def stack_count(b, p):
            return b * (KEY_INCS // 2) + (2 - p) * (KEY_INCS // 2)

        def batches(engine, step, last=B - 1, beside=lambda b: None):
            for b in range(2):
                step(b, b % 2)
                beside(b)
            with engine.Fori(0, (B - 4) // 2) as i:
                for p in range(2):
                    step(i * 2 + (p + 2), p)
            for b in range(B - 2, last + 1):
                step(b, b % 2)
                beside(b)

        first = lambda b: known(b) and b == 0
        exists = lambda b: not known(b) or 0 <= b < B

        @block.gpsimd
        def _(pool):
            pool.memset(rows[:, :], 0.0).then_inc(rows_zeroed, 1)
            pool.memset(v_hi[:, :, :, HD:], 1.0)
            pool.memset(v_lo[:, :, :, HD:], 0.0)
            pool.memset(sel[:, :, :], 1.0).then_inc(sel_set, 1)
            for j in range(2):
                pool.wait_ge(sel_set, 1 + 2 * j)
                pool.affine_select(out=sel[:, j, :], in_=sel[:, j, :], compare_op=ALU.is_ge, fill=0.0,
                                   base=-2 * j, pattern=[[0, P]], channel_multiplier=1).then_inc(sel_set, 1)
                pool.wait_ge(sel_set, 2 + 2 * j)
                pool.affine_select(out=sel[:, j, :], in_=sel[:, j, :], compare_op=ALU.is_ge, fill=0.0,
                                   base=2 * j + 1, pattern=[[0, P]], channel_multiplier=-1).then_inc(sel_set, 1)

            def step(b, p):
                pool.wait_ge(var_ready, b + 1)
                pool.tensor_tensor(r[:, :], v[:, :], k.pow_half[:, 0:TPB], ALU.pow).then_inc(r_ready, 1)

            batches(pool, step)
            pool.wait_ge(x_var_ready, 1)
            pool.tensor_tensor(x_rstd[:, :], x_var[:, :], k.pow_half[:, :], ALU.pow)

        @block.sync
        def _(sp):
            def step(b, p):
                sp.wait_ge(k_low, b + 1)
                for j, part in enumerate((k_hi[p], k_lo[p]) * 2):
                    rows = ks[bass.ds(b, 1), j * HD:(j + 1) * HD, :, :, :].rearrange("o d h c s -> (o h) d (c s)")
                    sp.dma_start(rows, part[:, :, :].rearrange("p c s -> p (c s)")).then_inc(stacked[p], 16)

            def load(n):
                sp.dma_start(raw[n % 2][:, :, :], k.ins[names[n]].rearrange("(c p) n -> p c n", p=P)).then_inc(w_loaded[n % 2], 16)

            load(0)
            load(1)
            sp.wait_ge(rows_zeroed, 1)
            for place, name in (("bk", "L1_xattn_bk_img"), ("gk", "L1_xattn_gk_img"), ("bq", "L1_xattn_bq"), ("gq", "L1_xattn_gq")):
                sp.dma_start(rows[ROWS[place]:ROWS[place] + DC, :], k.ins[name].rearrange("(c p) -> c p", p=P)).then_inc(rows_loaded, 16)
            for place, name in (("sgb", "L1_ffn_sgb"), ("sb1", "L1_ffn_sb1")):
                for e in range(2):
                    row = ROWS[place] + 2 * e
                    sp.dma_start(rows[row:row + 2, :], k.ins[name][e, :].rearrange("(c p) -> c p", p=P)).then_inc(rows_loaded, 16)
            sp.dma_start(vbias[:, :], broadcast_rows(k.ins["L1_xattn_bv_img"], D)).then_inc(b_loaded, 16)
            for n in (2, 3):
                sp.wait_ge(w_low, n - 1)
                load(n)
            for p in range(2):
                sp.sem_inc(stacked[p], KEY_INCS)
            batches(sp, step)
            for p in range(2):
                sp.wait_ge(stacked[p], (B // 2 + 1) * KEY_INCS)

        @block.scalar
        def _(act):
            def split_context(b, p):
                act.activation(c_hi[p][:, :, :], ctxT[:, :, at(b)], ACT.Copy).then_inc(c_high, 1)

            def step(b, p):
                if exists(b):
                    squares(b, p)
                if exists(b - 1):
                    high(b - 1, 1 - p)
                if exists(b):
                    products(b, p)

            def squares(b, p):
                act.wait_ge(k_psum, b + 1)
                if not known(b) or b >= 2:
                    act.wait_ge(normed, b * DC - DC)
                if not first(b):
                    act.wait_ge(sum_psum, b)
                for c in range(DC):
                    bias = vectors[:, ROWS["bk"] + c:ROWS["bk"] + c + 1]
                    act.activation(u[p][:, c, :], psK[c // 2][:, c % 2, :], ACT.Identity, bias=bias).then_inc(squared, 1)
                    act.activation(sq[:, c, :], psK[c // 2][:, c % 2, :], ACT.Square, bias=bias).then_inc(squared, 1)

            def products(b, p):
                for t in range(2):
                    act.wait_ge(v_full, b * 2 + (t + 1))
                    act.activation(vtile(v_hi, b, t), heads(vf[t][:, :]), ACT.Copy).then_inc(v_high, 1)
                if not known(b) or b + 2 < B:
                    act.wait_ge(v_psum, b * 2 + 2)
                    split_context(b + 2, p)

            def high(b, p):
                act.wait_ge(normed, b * DC + DC)
                act.wait_ge(stacked[p], stack_count(b, p))
                act.activation(k_hi[p][:, :, :], kn[:, :, :], ACT.Copy).then_inc(k_high, 1)

            def split_weights(n):
                act.wait_ge(w_loaded[n % 2], 16 * (n // 2 + 1))
                act.activation(split[n][:, 0, :, :], raw[n % 2][:, :, :], ACT.Copy).then_inc(w_high, 1)

            split_context(0, 0)
            split_weights(0)
            split_context(1, 1)
            split_weights(1)
            act.wait_ge(vectors_ready, 1)
            batches(act, step, B, lambda b: split_weights(b + 2) if b < 2 else None)

        @block.vector
        def _(dve):
            def split_context(b, p):
                dve.wait_ge(c_high, b + 1)
                dve.tensor_tensor(c_lo[p][:, :, :], ctxT[:, :, at(b)], c_hi[p][:, :, :], ALU.subtract).then_inc(c_low, 1)

            def step(b, p):
                if exists(b - 1):
                    normalise(b - 1, 1 - p)
                if exists(b):
                    products(b, p)
                    for t in range(TPB):
                        tile = bass.ds(b * TPB + t, 1)
                        dve.bn_stats(stats[:, tile, :], k.x[:, tile, :]).then_inc(stat_done, 1)

            def products(b, p):
                for t in range(2):
                    dve.wait_ge(v_psum, b * 2 + (t + 1))
                    if not known(b) or b:
                        dve.wait_ge(v_high, b * 2 + (t - 1))
                    dve.tensor_tensor(vf[t][:, :], psV[t][:, :], vbias[:, :], ALU.add).then_inc(v_full, 1)
                for t in range(2):
                    dve.wait_ge(v_high, b * 2 + (t + 1))
                    dve.tensor_tensor(vtile(v_lo, b, t), heads(vf[t][:, :]), vtile(v_hi, b, t), ALU.subtract)
                if not known(b) or b + 2 < B:
                    split_context(b + 2, p)
                dve.wait_ge(sum_psum, b + 1)
                dve.tensor_scalar(v[:, :], psR[:, 0, 0:TPB], 1.0 / D, RMS_EPS, ALU.mult, ALU.add).then_inc(var_ready, 1)
                dve.wait_ge(r_ready, b + 1)
                spread_on_diagonals(dve, k, diag, r).then_inc(diag_ready, 1)

            def normalise(b, p):
                if not known(b) or b:
                    dve.wait_ge(k_high, b)
                dve.wait_ge(r_psum, b + 1)
                for c in range(DC):
                    dve.scalar_tensor_tensor(kn[:, c, :], u[p][:, c, :], vectors[:, ROWS["gk"] + c:ROWS["gk"] + c + 1],
                                             psR[:, 1, :], ALU.mult, ALU.mult).then_inc(normed, 1)
                dve.wait_ge(k_high, b + 1)
                dve.tensor_tensor(k_lo[p][:, :, :], kn[:, :, :], k_hi[p][:, :, :], ALU.subtract).then_inc(k_low, 1)

            def split_weights(n):
                dve.wait_ge(w_high, n + 1)
                dve.tensor_tensor(split[n][:, 1, :, :], raw[n % 2][:, :, :], split[n][:, 0, :, :], ALU.subtract).then_inc(w_low, 1)

            def beside(b):
                if b < 2:
                    split_weights(b + 2)
                elif b == B - 1:
                    dve.wait_ge(stat_done, NT)
                    mean_var(link, dve, stats, x_mean[:, :], x_var[:, :], tmp[:, :], LN_EPS)
                    dve.sem_inc(x_var_ready, 1)

            link = Link(dve, dve_step)
            split_context(0, 0)
            split_weights(0)
            split_context(1, 1)
            split_weights(1)
            dve.wait_ge(rows_turned, 1)
            dve.tensor_copy(vectors[:, :], psW[:, 0:vectors.shape[1]]).then_inc(vectors_ready, 1)
            dve.wait_ge(vectors_ready, 1)
            dve.wait_ge(b_loaded, 16)
            batches(dve, step, B, beside)

        @block.tensor
        def _(pe):
            def keys(b, p):
                pe.wait_ge(c_low, b + 1)
                if not first(b):
                    pe.wait_ge(squared, b * (2 * DC))
                for f in range(DC):
                    for c in range(DC):
                        last = three_products(pe, psK[f // 2][:, f % 2, :],
                                              [kw[:, s, c, f * P:(f + 1) * P] for s in range(2)],
                                              [c_hi[p][:, c, :], c_lo[p][:, c, :]], c == 0, c == DC - 1)
                last.then_inc(k_psum, 1)

            def spread(b):
                pe.wait_ge(diag_ready, b + 1)
                pe.matmul(psR[:, 1, :], k.ones[:, :], diag[:, :, :].rearrange("p t q -> p (t q)"), start=True, stop=True)\
                  .then_inc(r_psum, 1)

            def values(b, p, t):
                if not first(b):
                    pe.wait_ge(v_full, b * 2 + (t - 1))
                elif t == 0:
                    pe.wait_ge(w_low, 2)
                for c in range(DC):
                    last = three_products(pe, psV[t][:, :], [a[p][:, c, t * P:(t + 1) * P] for a in (c_hi, c_lo)],
                                          [vw[:, s, c, :] for s in range(2)], c == 0, c == DC - 1)
                last.then_inc(v_psum, 1)

            def sums(b):
                pe.wait_ge(squared, b * (2 * DC) + 2 * DC)
                if not first(b):
                    pe.wait_ge(normed, b * DC)
                square_sums(pe, k, psR[:, 0, :], sq).then_inc(sum_psum, 1)

            def step(b, p):
                if exists(b):
                    keys(b, p)
                if exists(b - 1):
                    spread(b - 1)
                if exists(b):
                    values(b, p, 0)
                    values(b, p, 1)
                    sums(b)

            pe.wait_ge(rows_loaded, 16 * 8)
            pe.transpose(psW[:, :], rows[:, :], k.ident[:, :]).then_inc(rows_turned, 1)
            pe.wait_ge(w_low, 1)
            batches(pe, step, B)


def stage_attention(k, ks, v_hi, v_lo, qw, ow, vectors, x_mean, x_rstd, sel, stats):
    nc = k.nc
    with ExitStack() as ctx:
        sb = lambda name, shape, dt: ctx.enter_context(nc.sbuf_tensor(name, shape, dt))
        two = lambda name, shape, dt: [sb(f"{name}{i}", shape, dt) for i in range(2)]
        bo = sb("at_bo", [P, D], F32)
        xn = two("at_xn", [P, D], F32)
        x_hi, x_lo = sb("at_xhi", [P, DC, S], BF16), sb("at_xlo", [P, DC, S], BF16)
        qn, sq = sb("at_qn", [P, DC, S], F32), sb("at_sq", [P, DC, S], F32)
        v, r = (sb(f"at_{n}", [P, TPB], F32) for n in ("v", "r"))
        diag = sb("at_diag", [P, TPB, P], F32)
        q_hi, q_lo = sb("at_qhi", [P, DC, S], BF16), sb("at_qlo", [P, DC, S], BF16)
        qs = two("at_qs", [P, HC, DC, S], BF16)
        kb = two("at_kb", [P, HC, DC, S], BF16)
        negmax = two("at_negmax", [P, 4], F32)
        maxes = sb("at_maxes", [P, 2, P], BF16)
        maxT = sb("at_maxT", [P, 2, P], BF16)
        pf = two("at_pf", [P, 2, 2, S], F32)
        ph, pl = ([sb(f"at_{n}{i}", [P, 2, 2, S], BF16) for i in range(4)] for n in ("ph", "pl"))
        rden = sb("at_rden", [P, 4], F32)
        o = two("at_o", [P, 2, D], F32)
        o_hi, o_lo = sb("at_ohi", [P, DC, S], BF16), sb("at_olo", [P, DC, S], BF16)
        psS = ctx.enter_context(nc.psum_tensor("ps_s", [P, 2, 2, S], F32))
        psT = ctx.enter_context(nc.psum_tensor("ps_st", [P, 2, 2, S], F32))
        psM = ctx.enter_context(nc.psum_tensor("ps_m", [P, 2, P], BF16))
        psO = ctx.enter_context(nc.psum_tensor("ps_o", [P, 4, VC], F32))
        psP = [ctx.enter_context(nc.psum_tensor(f"ps_p{i}", [P, D], F32)) for i in range(2)]
        sem = lambda name: k.semaphore(("at_" + name))
        b_loaded, dve_step, maxes_zeroed, stat_done = (sem(n) for n in ("bl", "dve", "mz", "sd"))
        s_psum, max_read, maxes_ready, m_psum, maxT_ready, st_psum, exped, p_high, p_low, o_psum, o_read = (
            sem(n) for n in ("sp", "mr", "mx", "mp", "mt", "stp", "ex", "ph", "pl", "op", "od"))
        xn_ready, biased, xt_psum, x_high, x_low, q_psum, squared, normed, q_high, q_low = (
            sem(n) for n in ("xn", "bi", "xtp", "xh", "xl", "qp", "sq", "no", "qh", "ql"))
        sum_psum, var_ready, r_ready, diag_ready, r_psum = (sem(n) for n in ("sup", "var", "rr", "di", "rp"))
        ot_psum, ot_high, ot_low, y_psum, y_added = (sem(n) for n in ("otp", "oth", "otl", "yp", "ya"))
        stacked = [sem("st0"), sem("st1")]
        k_loaded = [sem("kl0"), sem("kl1")]
        block = ctx.enter_context(nc.Block())
        xtile = lambda t: k.x[:, bass.ds(t, 1), :]
        one = lambda a, t: a[:, bass.ds(t, 1)]
        in_q = lambda b, ahead: not known(b) or 0 <= b + ahead < B
        in_g = lambda b, u, off: not known(b) or 0 <= b * UNITS + u + off < B * UNITS
        G = UNITS

        def stack_count(b, p):
            return b * (STACK_INCS // 2) + (2 - p) * (STACK_INCS // 2)

        def steps(engine, step, link=None, per=0):
            for b in range(-2, 2):
                for u in range(UNITS):
                    step(b, b % 2, u)
            with (link.loop((B - 4) // 2, per) if link else engine.Fori(0, (B - 4) // 2)) as i:
                for p in range(2):
                    for u in range(UNITS):
                        step(i * 2 + (p + 2), p, u)
            for b in range(B - 2, B + 1):
                for u in range(UNITS):
                    step(b, b % 2, u)

        @block.sync
        def _(sp):
            sp.dma_start(bo[:, :], broadcast_rows(k.ins["L1_xattn_bo"], D)).then_inc(b_loaded, 16)

            def step(b, p, u):
                if u == 2 and in_q(b, 1):
                    if not known(b) or b >= 1:
                        sp.wait_ge(st_psum, b * G)
                    sp.dma_start(kb[1 - p][:, :, :, :], ks[bass.ds(b + 1, 1), :, :, :, :].rearrange("o p h c s -> (o p) h c s"))\
                      .then_inc(k_loaded[1 - p], 16)
                if u == 3 and in_q(b, 1):
                    for j, part in enumerate((q_hi, q_hi, q_lo, q_lo)):
                        if j % 2 == 0:
                            sp.wait_ge((q_high, q_low)[j // 2], b + 2)
                        for h in range(HC):
                            sp.dma_start(qs[1 - p][j * HD:(j + 1) * HD, h, :, :], part[h * HD:(h + 1) * HD, :, :])\
                              .then_inc(stacked[1 - p], 16)

            steps(sp, step)

        @block.gpsimd
        def _(pool):
            pool.memset(maxes[:, :, :], 0.0).then_inc(maxes_zeroed, 1)
            pool.wait_ge(b_loaded, 16)

            def step(b, p, u):
                if u == 5 and in_q(b, 2):
                    for t in range(2):
                        pool.wait_ge(xn_ready, b * 2 + (4 + t + 1))
                        pool.tensor_tensor(xtile(b * 2 + (4 + t)), xtile(b * 2 + (4 + t)), bo[:, :].unsqueeze(1), ALU.add)\
                            .then_inc(biased, 1)
                if u == 0 and in_q(b, 1):
                    pool.wait_ge(var_ready, b + 2)
                    pool.tensor_tensor(r[:, :], v[:, :], k.pow_half[:, 0:TPB], ALU.pow).then_inc(r_ready, 1)
                if in_g(b, u, 0):
                    g = b * G + u
                    pool.wait_ge(p_high, g + 1)
                    pool.tensor_tensor(pl[u % 4][:, :, :, :], pf[u % 2][:, :, :, :], ph[u % 4][:, :, :, :], ALU.subtract)\
                        .then_inc(p_low, 1)

            steps(pool, step)

        @block.scalar
        def _(act):
            def biased_and_squared(q, c):
                act.wait_ge(q_psum, q * DC + (c + 1))
                if c == 0 and (not known(q) or q):
                    act.wait_ge(normed, q * DC)
                bias = vectors[:, ROWS["bq"] + c:ROWS["bq"] + c + 1]
                act.activation(qn[:, c, :], psP[1 - c % 2][:, 0:S], ACT.Identity, bias=bias).then_inc(squared, 1)
                act.activation(sq[:, c, :], psP[1 - c % 2][:, 0:S], ACT.Square, bias=bias).then_inc(squared, 1)

            def step(b, p, u):
                if u == 0 and in_q(b, 1):
                    biased_and_squared(b + 1, 2)
                    biased_and_squared(b + 1, 3)
                if u == 2 and in_q(b, 1):
                    act.wait_ge(normed, b * DC + 2 * DC)
                    if not known(b) or b + 1 >= 1:
                        act.wait_ge(stacked[p], stack_count(b, p))
                    act.activation(q_hi[:, :, :], qn[:, :, :], ACT.Copy).then_inc(q_high, 1)
                if u == 3 and in_q(b, -1):
                    for t in range(2):
                        act.wait_ge(ot_psum, b * 2 + (t - 1))
                        act.activation(o_hi[:, :, t * P:(t + 1) * P], psP[1 - t][:, :].rearrange("p (c t) -> p c t", c=DC),
                                       ACT.Copy).then_inc(ot_high, 1)
                if u == 6 and in_q(b, 2):
                    for t in range(2):
                        act.wait_ge(xt_psum, b * 2 + (4 + t + 1))
                        act.activation(x_hi[:, :, t * P:(t + 1) * P], psP[1 - t][:, :].rearrange("p (c t) -> p c t", c=DC),
                                       ACT.Copy).then_inc(x_high, 1)
                if u == 7 and in_q(b, 2):
                    biased_and_squared(b + 2, 0)
                    biased_and_squared(b + 2, 1)
                if in_g(b, u, 0):
                    g = b * G + u
                    act.wait_ge(st_psum, g + 1)
                    if not known(b) or g >= 2:
                        act.wait_ge(p_low, g - 1)
                    act.activation(pf[u % 2][:, :, :, :], psT[:, :, :, :], ACT.Exp, scale=SCORE_SCALE).then_inc(exped, 1)
                    act.wait_ge(exped, g + 1)
                    act.activation(ph[u % 4][:, :, :, :], pf[u % 2][:, :, :, :], ACT.Copy).then_inc(p_high, 1)

            steps(act, step)

        @block.vector
        def _(dve):
            link = Link(dve, dve_step)
            dve.wait_ge(maxes_zeroed, 1)

            def step(b, p, u):
                g = b * G + u
                if u == 1 and in_q(b, 1):
                    dve.wait_ge(r_ready, b + 2)
                    spread_on_diagonals(dve, k, diag, r).then_inc(diag_ready, 1)
                for t in range(2):
                    if u == 4 + t and in_q(b, -1):
                        tile = b * 2 + (t - 2)
                        dve.wait_ge(y_psum, b * 2 + (t - 1))
                        dve.wait_ge(biased, b * 2 + (t - 1))
                        dve.tensor_tensor(xtile(tile), xtile(tile), psP[1 - t][:, :].unsqueeze(1), ALU.add).then_inc(y_added, 1)
                if in_g(b, u, 1):
                    dve.wait_ge(m_psum, g + 2)
                    dve.tensor_copy(maxT[:, :, :], psM[:, :, :]).then_inc(maxT_ready, 1)
                if u == 3 and in_q(b, -1):
                    for t in range(2):
                        dve.wait_ge(ot_high, b * 2 + (t - 1))
                        half = slice(t * P, (t + 1) * P)
                        dve.tensor_tensor(o_lo[:, :, half], psP[1 - t][:, :].rearrange("p (c t) -> p c t", c=DC),
                                          o_hi[:, :, half], ALU.subtract).then_inc(ot_low, 1)
                if u == 6 and in_q(b, 2):
                    for t in range(2):
                        dve.wait_ge(x_high, b * 2 + (4 + t + 1))
                        half = slice(t * P, (t + 1) * P)
                        dve.tensor_tensor(x_lo[:, :, half], psP[1 - t][:, :].rearrange("p (c t) -> p c t", c=DC),
                                          x_hi[:, :, half], ALU.subtract).then_inc(x_low, 1)
                if in_g(b, u, 2):
                    n = u % 2
                    dve.wait_ge(s_psum, g + 3)
                    dve.tensor_reduce(negmax[n][:, :].rearrange("p (j q) -> p j q", j=2), psS[:, :, :, :], AX.X, ALU.max,
                                      negate=True).then_inc(max_read, 1)
                    dve.wait_ge(max_read, g + 3)
                    m = negmax[n][:, :].rearrange("p (j q) -> p q j", j=2)
                    link(dve.tensor_copy(maxes[:, :, 0:4:2], m))
                    dve.tensor_tensor(maxes[:, :, 1:4:2], m, maxes[:, :, 0:4:2], ALU.subtract).then_inc(maxes_ready, 1)
                if u == 2 and in_q(b, 1):
                    dve.wait_ge(q_high, b + 2)
                    dve.tensor_tensor(q_lo[:, :, :], qn[:, :, :], q_hi[:, :, :], ALU.subtract).then_inc(q_low, 1)
                if in_g(b, u, -2):
                    dve.wait_ge(o_psum, g - 1)
                    uo = (u - 2) % UNITS
                    po = p if u >= 2 else 1 - p
                    link(dve.reciprocal(rden[:, :], psO[:, :, HD]))
                    dst = o[po][:, :, uo * 2 * HD:(uo + 1) * 2 * HD].rearrange("p q (j d) -> p j q d", j=2)
                    dve.tensor_tensor(dst, psO[:, :, 0:HD].rearrange("p (j q) d -> p j q d", j=2),
                                      rden[:, :].rearrange("p (j q) -> p j q", j=2).unsqueeze(3).broadcast_to([P, 2, 2, HD]),
                                      ALU.mult).then_inc(o_read, 1)
                if u == 0 and in_q(b, 1):
                    dve.wait_ge(sum_psum, b + 2)
                    dve.tensor_scalar(v[:, :], psP[0][:, 0:TPB], 1.0 / D, RMS_EPS, ALU.mult, ALU.add).then_inc(var_ready, 1)
                if u == 1 and in_q(b, 1):
                    dve.wait_ge(r_psum, b + 2)
                    for c in range(DC):
                        dve.scalar_tensor_tensor(qn[:, c, :], qn[:, c, :], vectors[:, ROWS["gq"] + c:ROWS["gq"] + c + 1],
                                                 psP[0][:, S:], ALU.mult, ALU.mult).then_inc(normed, 1)
                for t in range(2):
                    if u == 4 + t and in_q(b, -1):
                        dve.wait_ge(y_added, b * 2 + (t - 1))
                        dve.bn_stats(stats[:, bass.ds(b * 2 + (t - 2), 1), :], xtile(b * 2 + (t - 2))).then_inc(stat_done, 1)
                if u == 4 and in_q(b, 2):
                    for t in range(2):
                        tile = b * 2 + (4 + t)
                        if not known(b) or b + 2 >= 1:
                            dve.wait_ge(xt_psum, tile - 1)
                        dve.tensor_scalar(xn[t][:, :], xtile(tile), one(x_mean, tile), one(x_rstd, tile),
                                          ALU.subtract, ALU.mult).then_inc(xn_ready, 1)

            steps(dve, step, link, 2 * (8 * 2))

        @block.tensor
        def _(pe):
            def scores(b, p, u, g):
                if u == 0:
                    pe.wait_ge(stacked[p], stack_count(b, p))
                    pe.wait_ge(k_loaded[p], b * 8 + 8 * (2 - p))
                if not known(g) or g:
                    pe.wait_ge(max_read, g)
                c, h0 = u // 2, 2 * (u % 2)
                for j in range(2):
                    for q in range(2):
                        last = pe.matmul(psS[:, j, q, :], qs[p][:, h0 + j, c, q * P:(q + 1) * P], kb[p][:, h0 + j, c, :],
                                         start=True, stop=True)
                last.then_inc(s_psum, 1)

            def turn_maxes(g):
                pe.wait_ge(maxes_ready, g + 1)
                if not known(g) or g:
                    pe.wait_ge(maxT_ready, g)
                for q in range(2):
                    last = pe.transpose(psM[:, q, :], maxes[:, q, :], k.ident_b[:, :])
                last.then_inc(m_psum, 1)

            def values(b, u, g):
                pe.wait_ge(p_low, g + 1)
                if not known(g) or g:
                    pe.wait_ge(o_read, g)
                for j in range(2):
                    for q in range(2):
                        cols = slice(q * P, (q + 1) * P)
                        for n, (pr, vv) in enumerate(((ph, v_hi), (ph, v_lo), (pl, v_hi))):
                            for kc in range(2):
                                last = pe.matmul(psO[:, 2 * j + q, :], pr[u % 4][:, j, kc, cols],
                                                 vv[:, bass.ds(b * 2 + kc, 1), 2 * u + j, :].rearrange("p o d -> p (o d)"),
                                                 start=(n == 0 and kc == 0), stop=(n == 2 and kc == 1))
                last.then_inc(o_psum, 1)

            def transposed_scores(b, p, u, g):
                pe.wait_ge(maxT_ready, g + 1)
                if not known(g) or g:
                    pe.wait_ge(exped, g)
                c, h0 = u // 2, 2 * (u % 2)
                for j in range(2):
                    for kc in range(2):
                        pe.matmul(psT[:, j, kc, :], kb[p][:, h0 + j, c, kc * P:(kc + 1) * P], qs[p][:, h0 + j, c, :],
                                  start=True, stop=False)
                        last = pe.matmul(psT[:, j, kc, :], sel[:, j, :], maxT[:, :, :].rearrange("p q t -> p (q t)"),
                                         start=False, stop=True)
                last.then_inc(st_psum, 1)

            def queries(q, c):
                if c == 0:
                    pe.wait_ge(x_high, q * 2 + 2)
                    pe.wait_ge(x_low, q * 2 + 1)
                if c >= 2:
                    pe.wait_ge(squared, q * (2 * DC) + 2 * (c - 1))
                cols = slice(c * P, (c + 1) * P)
                for kc in range(DC):
                    pe.matmul(psP[1 - c % 2][:, 0:S], qw[:, 0, kc, cols], x_hi[:, kc, :], start=(kc == 0), stop=False)
                    pe.matmul(psP[1 - c % 2][:, 0:S], qw[:, 1, kc, cols], x_hi[:, kc, :], start=False, stop=False)
                if c == 0:
                    pe.wait_ge(x_low, q * 2 + 2)
                for kc in range(DC):
                    last = pe.matmul(psP[1 - c % 2][:, 0:S], qw[:, 0, kc, cols], x_lo[:, kc, :], start=False, stop=(kc == DC - 1))
                last.then_inc(q_psum, 1)

            def step(b, p, u):
                g = b * G + u
                if in_g(b, u, 0):
                    transposed_scores(b, p, u, g)
                if in_g(b, u, 2):
                    nb, np_, nu = (b, p, u + 2) if u + 2 < UNITS else (b + 1, 1 - p, u + 2 - UNITS)
                    scores(nb, np_, nu, g + 2)
                if in_g(b, u, 1):
                    turn_maxes(g + 1)
                if u == 5 and in_q(b, 2):
                    for t in range(2):
                        pe.wait_ge(xn_ready, b * 2 + (4 + t + 1))
                        if not known(b) or b >= 1:
                            pe.wait_ge(y_added, b * 2 + (t - 1))
                        for c in range(DC):
                            last = pe.transpose(psP[1 - t][:, c * P:(c + 1) * P], xn[t][:, c * P:(c + 1) * P], k.ident[:, :])
                        last.then_inc(xt_psum, 1)
                if in_g(b, u, -2):
                    ob, ou = (b, u - 2) if u >= 2 else (b - 1, u + UNITS - 2)
                    values(ob, ou, g - 2)
                if u == 0 and in_q(b, 1):
                    pe.wait_ge(squared, b * (2 * DC) + 4 * DC)
                    square_sums(pe, k, psP[0], sq).then_inc(sum_psum, 1)
                if u == 1 and in_q(b, 1):
                    pe.wait_ge(diag_ready, b + 2)
                    pe.matmul(psP[0][:, S:], k.ones[:, :], diag[:, :, :].rearrange("p t q -> p (t q)"), start=True, stop=True)\
                      .then_inc(r_psum, 1)
                if u == 2 and in_q(b, -1):
                    pe.wait_ge(o_read, b * G)
                    if in_q(b, 1):
                        pe.wait_ge(normed, b * DC + 2 * DC)
                    for t in range(2):
                        for c in range(DC):
                            last = pe.transpose(psP[1 - t][:, c * P:(c + 1) * P], o[1 - p][:, t, c * P:(c + 1) * P], k.ident[:, :])
                        last.then_inc(ot_psum, 1)
                for t in range(2):
                    if u == 3 + t and in_q(b, -1):
                        pe.wait_ge(ot_low, b * 2 + (t - 1))
                        for c in range(DC):
                            last = three_products(pe, psP[1 - t][:, :], [a[:, c, t * P:(t + 1) * P] for a in (o_hi, o_lo)],
                                                  [ow[:, s, c, :] for s in range(2)], c == 0, c == DC - 1)
                        last.then_inc(y_psum, 1)
                if u == 6 and in_q(b, 2):
                    queries(b + 2, 0)
                    queries(b + 2, 1)
                if u == 7 and in_q(b, 2):
                    queries(b + 2, 2)
                    queries(b + 2, 3)

            steps(pe, step)


E_N = 16
SH_N = 2
FE = 256
F2 = FE // P
BLK = 256
ST = BLK // P
NBLK = (2 * TOK + E_N * (BLK - 1)) // BLK
FLOOR = 0.498


def stage_router(k, stats, xf, xT_hi, xT_lo, xaff, sgu, sd):
    nc = k.nc
    with ExitStack() as ctx:
        sb = lambda name, shape, dt: ctx.enter_context(nc.sbuf_tensor(name, shape, dt))
        two = lambda name, shape, dt: [sb(f"{name}{i}", shape, dt) for i in range(2)]
        wa = sb("r_wa", [P, DC, E_N], F32)
        mean, var, tmp, rstd = (sb(f"r_{n}", [P, NT], F32) for n in ("mean", "var", "tmp", "rstd"))
        xn, xT = two("r_xn", [P, D], F32), two("r_xT", [P, DC, P], F32)
        ex = sb("r_exp", [P, NT, E_N], F32)
        psX = [ctx.enter_context(nc.psum_tensor(f"ps_rx{i}", [P, D], F32)) for i in range(2)]
        psL = ctx.enter_context(nc.psum_tensor("ps_rl", [P, NT * E_N], F32))
        raw = [sb(f"r_raw{i}", [P, 1024], F32) for i in range(6)]
        w_loaded, w_high = [k.semaphore(f"r_w{i}") for i in range(6)], k.semaphore("r_whi")
        rows_high, rows_low = k.semaphore("r_rh"), k.semaphore("r_rl")
        dst = [(sgu, e, m) for e in range(SH_N) for m in range(2)] + [(sd, e, 0) for e in range(SH_N)]
        place = lambda n, s: (dst[n][0][:, s, dst[n][1], dst[n][2], :] if n < 4 else dst[n][0][:, s, dst[n][1], :])
        sem = lambda name: k.semaphore(("r_" + name))
        wa_loaded, dve_step, var_ready, rstd_ready, xn_ready, added, x_psum, xT_ready, x_high, x_low, logits, exped = (
            sem(n) for n in ("wa", "dve", "var", "rstd", "xn", "add", "xp", "xT", "xh", "xl", "log", "ex"))
        block = ctx.enter_context(nc.Block())
        row = lambda a, t: a[:, bass.ds(t, 1), :]
        cols = lambda a, t: a[:, :, bass.ds(t * P, P)]
        chunks = lambda a: a.rearrange("p (c t) -> p c t", c=DC)

        @block.sync
        def _(sp):
            sp.dma_start(wa[:, :, :], k.ins["L1_ffn_wa"].rearrange("(c p) e -> p c e", p=P)).then_inc(wa_loaded, 16)
            for n in range(6):
                src = k.ins[("L1_ffn_sg", "L1_ffn_sw1")[dst[n][2]] if n < 4 else "L1_ffn_sw2"][dst[n][1], :, :]
                sp.dma_start(raw[n][:, :].rearrange("p (c n) -> p c n", c=D // P if n < 4 else F2),
                             src.rearrange("(c p) n -> p c n", p=P)).then_inc(w_loaded[n], 16)

        @block.gpsimd
        def _(pool):
            pool.wait_ge(var_ready, 1)
            pool.tensor_tensor(rstd[:, :], var[:, :], k.pow_half[:, :], ALU.pow).then_inc(rstd_ready, 1)
            with pool.Fori(0, NT // 2) as i:
                for p in range(2):
                    t = i * 2 + p
                    pool.wait_ge(xn_ready, i * 2 + (p + 1))
                    pool.tensor_tensor(row(k.x, t), row(k.x, t), xn[p][:, :].unsqueeze(1), ALU.add).then_inc(added, 1)

        @block.vector
        def _(dve):
            link = Link(dve, dve_step)
            mean_var(link, dve, stats, mean[:, :], var[:, :], tmp[:, :], LN_EPS)
            dve.sem_inc(var_ready, 1)
            dve.wait_ge(rstd_ready, 1)

            def normalise(t, p):
                if not known(t) or t >= 2:
                    dve.wait_ge(rows_low, t - 1)
                    dve.wait_ge(added, t - 1)
                    dve.wait_ge(x_psum, t - 1)
                scale = (mean[:, bass.ds(t, 1)], rstd[:, bass.ds(t, 1)], ALU.subtract, ALU.mult)
                dve.tensor_scalar(xn[p][:, :], row(k.x, t), *scale).then_inc(xn_ready, 1)

            def split(t, p):
                dve.wait_ge(rows_high, t + 1)
                dve.tensor_tensor(xf[:, bass.ds(t, 1), 1, :], xn[p][:, :].unsqueeze(1), xf[:, bass.ds(t, 1), 0, :], ALU.subtract)\
                   .then_inc(rows_low, 1)
                dve.wait_ge(x_high, t + 1)
                dve.tensor_tensor(cols(xT_lo, t), xT[p][:, :, :], cols(xT_hi, t), ALU.subtract).then_inc(x_low, 1)

            normalise(0, 0)
            normalise(1, 1)
            with dve.Fori(0, NT // 2 - 1) as i:
                for p in range(2):
                    split(i * 2 + p, p)
                    normalise(i * 2 + (p + 2), p)
            for t in range(NT - 2, NT):
                split(t, t % 2)
            dve.wait_ge(exped, 1)
            link(dve.tensor_scalar(ex[:, :, :], ex[:, :, :], 1.0, None, ALU.add))
            dve.reciprocal(xaff[:, :, :], ex[:, :, :])
            for n in range(6):
                dve.wait_ge(w_high, n + 1)
                dve.tensor_tensor(place(n, 1), raw[n][:, :], place(n, 0), ALU.subtract)

        @block.tensor
        def _(pe):
            def turn(t, p):
                pe.wait_ge(xn_ready, t + 1)
                if not known(t) or t >= 2:
                    pe.wait_ge(xT_ready, t - 1)
                for c in range(DC):
                    last = pe.transpose(psX[p][:, c * P:(c + 1) * P], xn[p][:, c * P:(c + 1) * P], k.ident[:, :])
                last.then_inc(x_psum, 1)

            def score(t, p):
                pe.wait_ge(xT_ready, t + 1)
                for c in range(DC):
                    last = pe.matmul(psL[:, bass.ds(t * E_N, E_N)], xT[p][:, c, :], wa[:, c, :],
                                     start=(c == 0), stop=(c == DC - 1))
                last.then_inc(logits, 1)

            pe.wait_ge(wa_loaded, 16)
            turn(0, 0)
            turn(1, 1)
            with pe.Fori(0, NT // 2 - 1) as i:
                for p in range(2):
                    score(i * 2 + p, p)
                    turn(i * 2 + (p + 2), p)
            for t in range(NT - 2, NT):
                score(t, t % 2)

        @block.scalar
        def _(act):
            act.sem_inc(logits, 2)
            act.sem_inc(x_low, 2)
            with act.Fori(0, NT // 2) as i:
                for p in range(2):
                    t = i * 2 + p
                    act.wait_ge(xn_ready, t + 1)
                    act.activation(xf[:, bass.ds(t, 1), 0, :], xn[p][:, :].unsqueeze(1), ACT.Copy).then_inc(rows_high, 1)
                    act.wait_ge(x_psum, t + 1)
                    act.wait_ge(logits, i * 2 + (p + 1))
                    act.wait_ge(x_low, i * 2 + (p + 1))
                    act.activation(xT[p][:, :, :], chunks(psX[p][:, :]), ACT.Copy).then_inc(xT_ready, 1)
                    act.wait_ge(xT_ready, t + 1)
                    act.activation(cols(xT_hi, t), xT[p][:, :, :], ACT.Copy).then_inc(x_high, 1)
            act.wait_ge(logits, NT + 2)
            act.activation(ex[:, :, :].rearrange("p t e -> p (t e)"), psL[:, :], ACT.Exp, scale=-1.0).then_inc(exped, 1)
            for n in range(6):
                act.wait_ge(w_loaded[n], 16)
                act.activation(place(n, 0), raw[n][:, :], ACT.Copy).then_inc(w_high, 1)


def stage_route_and_shared(k, xf, xT_hi, xT_lo, xaff, sgu, sd, slots, share, combine, wrow):
    nc = k.nc
    with ExitStack() as ctx:
        sb = lambda name, shape, dt: ctx.enter_context(nc.sbuf_tensor(name, shape, dt))
        two = lambda name, shape, dt: [sb(f"{name}{i}", shape, dt) for i in range(2)]
        best = sb("s_best", [P, NT, 8], F32)
        index = sb("s_index", [P, NT, 8], U32)
        indexf = sb("s_indexf", [P, NT, 8], F32)
        iota_e = sb("s_iota_e", [P, E_N], F32)
        iota_j = sb("s_iota_j", [P, NBLK], F32)
        iota_p = sb("s_iota_p", [P, 1], F32)
        hot = [sb(f"s_hot{i}", [P, NT, E_N], F32) for i in range(2)]
        both = sb("s_both", [P, NT, E_N], F32)
        before = sb("s_before", [P, P], F32)
        pos = sb("s_pos", [P, NT, E_N], F32)
        run = [sb(f"s_run{i}", [P, NT + 1, E_N], F32) for i in range(2)]
        blocks = [sb(f"s_blocks{i}", [P, E_N], F32) for i in range(2)]
        start = sb("s_start", [P, E_N], F32)
        slotf = sb("s_slotf", [P, 2, NT], F32)
        le = sb("s_le", [P, NBLK, E_N], F32)
        wf = sb("s_wf", [P, NBLK], F32)
        total = sb("s_total", [P, NT], F32)
        warm = sb("s_warm", [P, 1], F32)
        gf, yf = two("s_gf", [P, F2, BLK], F32), two("s_yf", [P, F2, BLK], F32)
        y_hi, y_lo = sb("s_yhi", [P, SH_N, F2, BLK], BF16), sb("s_ylo", [P, SH_N, F2, BLK], BF16)
        psR = ctx.enter_context(nc.psum_tensor("ps_sr", [P, 2, NT * E_N], F32))
        psG = [ctx.enter_context(nc.psum_tensor(f"ps_sg{i}", [P, F2, BLK], F32)) for i in range(2)]
        psU = [ctx.enter_context(nc.psum_tensor(f"ps_su{i}", [P, F2, BLK], F32)) for i in range(2)]
        psD = [ctx.enter_context(nc.psum_tensor(f"ps_sd{i}", [P, D], F32)) for i in range(ST)]
        sem = lambda name: k.semaphore(("s_" + name))
        consts, both_ready, counted, dve_step, slots_ready, scattered = (sem(n) for n in ("co", "bo", "ct", "dve", "sl", "sc"))
        gu_psum, gelu_done, y_full, y_high, y_low, d_psum, d_added = (
            sem(n) for n in ("gu", "ge", "yf", "yh", "yl", "dp", "da"))
        block = ctx.enter_context(nc.Block())
        CH = TOK // BLK

        @block.gpsimd
        def _(pool):
            pool.iota(iota_e[:, :], [[1, E_N]], base=0, channel_multiplier=0, allow_small_or_imprecise_dtypes=True).then_inc(consts, 1)
            pool.iota(iota_j[:, :], [[1, NBLK]], base=0, channel_multiplier=0, allow_small_or_imprecise_dtypes=True).then_inc(consts, 1)
            pool.iota(iota_p[:, :], [[0, 1]], base=0, channel_multiplier=1, allow_small_or_imprecise_dtypes=True).then_inc(consts, 1)
            pool.affine_select(out=before[:, :], in_=k.ones[:, :], compare_op=ALU.is_gt, fill=0.0, base=0,
                               pattern=[[1, P]], channel_multiplier=-1).then_inc(consts, 1)
            pool.wait_ge(slots_ready, 1)
            for s in range(2):
                for t in range(NT):
                    pool.indirect_dma_start(out=k.scratch["rows"], out_offset=bass.IndirectOffsetOnAxis(ap=slots[:, s, t:t + 1], axis=0),
                                            in_=xf[:, t, :, :].rearrange("p s d -> p (s d)"), in_offset=None).then_inc(scattered, 16)
            pool.wait_ge(scattered, 16 * 2 * NT)

        @block.vector
        def _(dve):
            link = Link(dve, dve_step)
            for t in range(NT):
                link(dve.max(best[:, t, :], xaff[:, t, :]), wait=False)
            dve.wait_ge(dve_step, NT)
            for t in range(NT):
                link(dve.max_index(index[:, t, :], best[:, t, :], xaff[:, t, :]), wait=False)
            dve.wait_ge(dve_step, 2 * NT)
            link(dve.tensor_copy(indexf[:, :, :], index[:, :, :]))
            dve.wait_ge(consts, 4)
            for s in range(2):
                link(dve.tensor_tensor(hot[s][:, :, :], iota_e[:, :].unsqueeze(1).broadcast_to([P, NT, E_N]),
                                       indexf[:, :, s:s + 1].broadcast_to([P, NT, E_N]), ALU.is_equal))
            dve.tensor_tensor(both[:, :, :], hot[0][:, :, :], hot[1][:, :, :], ALU.add).then_inc(both_ready, 1)
            link(dve.tensor_tensor(total[:, :], best[:, :, 0], best[:, :, 1], ALU.add))
            link(dve.reciprocal(total[:, :], total[:, :]))
            for s in range(2):
                link(dve.tensor_tensor(share[:, s, :], best[:, :, s], total[:, :], ALU.mult))
                link(dve.tensor_tensor(le[:, 0:NT, :] if s else combine[:, :, :], hot[s][:, :, :],
                                       share[:, s, :].unsqueeze(2).broadcast_to([P, NT, E_N]), ALU.mult))
            link(dve.tensor_tensor(combine[:, :, :], combine[:, :, :], le[:, 0:NT, :], ALU.add))
            dve.wait_ge(counted, 1)
            link(dve.memset(run[0][:, 0:1, :], 0.0))
            link(dve.tensor_copy(run[0][:, 1:, :], psR[:, 1, :].rearrange("p (t e) -> p t e", e=E_N)))
            a, step = 0, 1
            while step <= NT:
                link(dve.tensor_tensor(run[1 - a][:, step:, :], run[a][:, step:, :], run[a][:, 0:NT + 1 - step, :], ALU.add))
                link(dve.tensor_copy(run[1 - a][:, 0:step, :], run[a][:, 0:step, :]))
                a, step = 1 - a, 2 * step
            link(dve.tensor_scalar(blocks[0][:, :], run[a][:, NT, :], 1.0 / BLK, (BLK - 1.0) / BLK - FLOOR, ALU.mult, ALU.add))
            link(dve.tensor_scalar(blocks[0][:, :], blocks[0][:, :], ROUND, ROUND, ALU.add, ALU.subtract))
            link(dve.tensor_copy(start[:, :], blocks[0][:, :]))
            b, step = 0, 1
            while step < E_N:
                link(dve.tensor_tensor(blocks[1 - b][:, step:], blocks[b][:, step:], blocks[b][:, 0:E_N - step], ALU.add))
                link(dve.tensor_copy(blocks[1 - b][:, 0:step], blocks[b][:, 0:step]))
                b, step = 1 - b, 2 * step
            link(dve.tensor_tensor(start[:, :], blocks[b][:, :], start[:, :], ALU.subtract))
            link(dve.tensor_tensor(pos[:, :, :], psR[:, 0, :].rearrange("p (t e) -> p t e", e=E_N), run[a][:, 0:NT, :], ALU.add))
            link(dve.tensor_scalar(blocks[b][:, :], start[:, :], float(BLK), None, ALU.mult))
            link(dve.tensor_tensor(pos[:, :, :], pos[:, :, :], blocks[b][:, :].unsqueeze(1).broadcast_to([P, NT, E_N]), ALU.add))
            for s in range(2):
                link(dve.tensor_tensor(both[:, :, :], pos[:, :, :], hot[s][:, :, :], ALU.mult))
                link(dve.tensor_reduce(slotf[:, s, :], both[:, :, :], AX.X, ALU.add))
            dve.tensor_copy(slots[:, :, :], slotf[:, :, :]).then_inc(slots_ready, 1)
            link(dve.tensor_tensor(le[:, :, :], start[:, :].unsqueeze(1).broadcast_to([P, NBLK, E_N]),
                                   iota_j[:, :].unsqueeze(2).broadcast_to([P, NBLK, E_N]), ALU.is_le))
            link(dve.tensor_reduce(wf[:, :], le[:, :, :], AX.X, ALU.add))
            link(dve.tensor_scalar(wf[:, :], wf[:, :], float(P), -float(P), ALU.mult, ALU.add))
            link(dve.tensor_scalar(wf[:, :], wf[:, :], iota_p[:, :], None, ALU.add))
            link(dve.tensor_copy(wrow[:, :], wf[:, :]))

            dve.sem_inc(d_added, ST)

            def hidden(i):
                for e in range(SH_N):
                    dve.wait_ge(gelu_done, i * SH_N + (e + 1))
                    for f in range(F2):
                        last = dve.scalar_tensor_tensor(yf[e][:, f, :], psU[e][:, f, :],
                                                        k.vectors[:, ROWS["sb1"] + 2 * e + f:ROWS["sb1"] + 2 * e + f + 1],
                                                        gf[e][:, f, :], ALU.add, ALU.mult)
                    last.then_inc(y_full, 1)
                    dve.wait_ge(y_high, i * SH_N + (e + 1))
                    dve.tensor_tensor(y_lo[:, e, :, :], yf[e][:, :, :], y_hi[:, e, :, :], ALU.subtract).then_inc(y_low, 1)

            def add_sums(i):
                for s in range(ST):
                    dve.wait_ge(d_psum, i * ST + (s + 2))
                    x = k.x[:, bass.ds(i * ST + s, 1), :]
                    dve.tensor_tensor(x, x, psD[s][:, :].unsqueeze(1), ALU.add).then_inc(d_added, 1)

            hidden(0)
            with dve.Fori(0, CH - 1) as i:
                hidden(i + 1)
                add_sums(i)
            add_sums(CH - 1)

        @block.scalar
        def _(act):
            act.sem_inc(y_low, SH_N)
            act.activation(warm[:, :], k.small[:, 2:3], ACT.Gelu)
            with act.Fori(0, CH) as i:
                for e in range(SH_N):
                    act.wait_ge(gu_psum, i * SH_N + (e + 1 + SH_N))
                    act.wait_ge(y_low, i * SH_N + (e + 1))
                    for f in range(F2):
                        last = act.activation(gf[e][:, f, :], psG[e][:, f, :], ACT.Gelu,
                                              bias=k.vectors[:, ROWS["sgb"] + 2 * e + f:ROWS["sgb"] + 2 * e + f + 1])
                    last.then_inc(gelu_done, 1)
                    act.wait_ge(y_full, i * SH_N + (e + 1))
                    act.wait_ge(d_psum, i * ST + 1)
                    act.activation(y_hi[:, e, :, :], yf[e][:, :, :], ACT.Copy).then_inc(y_high, 1)

        @block.tensor
        def _(pe):
            pe.sem_inc(gu_psum, SH_N)
            pe.sem_inc(d_psum, 1)
            pe.wait_ge(both_ready, 1)
            pe.wait_ge(consts, 4)
            flat = both[:, :, :].rearrange("p t e -> p (t e)")
            pe.matmul(psR[:, 0, :], before[:, :], flat, start=True, stop=True)
            pe.matmul(psR[:, 1, :], k.ones[:, :], flat, start=True, stop=True).then_inc(counted, 1)

            def up(i, e):
                for ps, m in ((psG, 0), (psU, 1)):
                    for f in range(F2):
                        for c in range(DC):
                            col = c * FE + f * P
                            last = three_products(pe, ps[e][:, f, :], [sgu[:, s, e, m, col:col + P] for s in range(2)],
                                                  [a[:, c, bass.ds(i * BLK, BLK)] for a in (xT_hi, xT_lo)], c == 0, c == DC - 1)
                last.then_inc(gu_psum, 1)

            def down(i):
                for e in range(SH_N):
                    pe.wait_ge(y_low, i * SH_N + (e + 1 + SH_N))
                for s in range(ST):
                    pe.wait_ge(d_added, i * ST + (s + 1))
                    for e in range(SH_N):
                        for f in range(F2):
                            last = three_products(pe, psD[s][:, :], [a[:, e, f, s * P:(s + 1) * P] for a in (y_hi, y_lo)],
                                                  [sd[:, h, e, f * D:(f + 1) * D] for h in range(2)],
                                                  e == 0 and f == 0, e == SH_N - 1 and f == F2 - 1)
                    last.then_inc(d_psum, 1)

            for e in range(SH_N):
                up(0, e)
            with pe.Fori(0, CH - 1) as i:
                for e in range(SH_N):
                    pe.wait_ge(y_full, i * SH_N + (e + 1))
                    up(i + 1, e)
                down(i)
            down(CH - 1)


def stage_experts(k, wrow):
    nc = k.nc
    with ExitStack() as ctx:
        sb = lambda name, shape, dt: ctx.enter_context(nc.sbuf_tensor(name, shape, dt))
        two = lambda name, shape, dt: [sb(f"{name}{i}", shape, dt) for i in range(2)]
        raw = [two(f"e_raw{m}", [P, DC * FE], F32) for m in range(3)]
        wb = [two(f"e_wb{m}", [P, F2], F32) for m in range(2)]
        hi, lo = ([two(f"e_{n}{m}", [P, DC * FE], BF16) for m in range(3)] for n in ("hi", "lo"))
        rows = two("e_rows", [P, ST, 2, D], BF16)
        x_hi, x_lo = two("e_xhi", [P, DC, BLK], BF16), two("e_xlo", [P, DC, BLK], BF16)
        gf, yf = two("e_gf", [P, F2, BLK], F32), two("e_yf", [P, F2, BLK], F32)
        y_hi, y_lo = two("e_yhi", [P, F2, BLK], BF16), two("e_ylo", [P, F2, BLK], BF16)
        yo = two("e_yo", [P, ST, D], F32)
        psX = [ctx.enter_context(nc.psum_tensor(f"ps_ex{i}", [P, DC, ST, P], BF16)) for i in range(2)]
        psG = [ctx.enter_context(nc.psum_tensor(f"ps_eg{i}", [P, F2, BLK], F32)) for i in range(2)]
        psU = [ctx.enter_context(nc.psum_tensor(f"ps_eu{i}", [P, F2, BLK], F32)) for i in range(2)]
        psD = [ctx.enter_context(nc.psum_tensor(f"ps_ed{i}", [P, D], F32)) for i in range(ST)]
        sem = lambda name: k.semaphore(("e_" + name))
        up_loaded, down_loaded, biases_loaded, rows_loaded, stored = (
            [sem(f"{n}{i}") for i in range(2)] for n in ("ul", "dl", "bl", "rl", "st"))
        up_high, up_low, down_high, down_low, x_psum, x_high, x_low, gu_psum, gelu_done, y_full, y_high, y_low = (
            sem(n) for n in ("uh", "ulo", "dh", "dlo", "xp", "xh", "xl", "gu", "ge", "yf", "yh", "yl"))
        d_psum, out_ready, row_ready, gather_turn = (sem(n) for n in ("dp", "or", "rr", "turn"))
        wrow_p = two("e_wrow", [P, 1], U32)
        block = ctx.enter_context(nc.Block())
        tables = (k.ins["L1_ffn_rg"].rearrange("e (p c) f -> (e p) (c f)", c=DC),
                  k.ins["L1_ffn_rw1"].rearrange("e (p c) f -> (e p) (c f)", c=DC),
                  k.ins["L1_ffn_rw2"].rearrange("e (p c) f -> (e p) (c f)", c=F2))
        bias_tables = (k.ins["L1_ffn_rgb"].rearrange("e (p c) -> (e p) c", c=F2),
                       k.ins["L1_ffn_rb1"].rearrange("e (p c) -> (e p) c", c=F2))
        rows_dram = k.scratch["rows"].rearrange("(j s p) d -> j p s d", s=ST, p=P)
        out_dram = k.scratch["results"].rearrange("(j s p) d -> j p s d", s=ST, p=P)

        def steps(engine, step):
            for n in range(-2, 4):
                step(n, n % 2)
            with engine.Fori(0, (NBLK - 6) // 2) as i:
                for p in range(2):
                    step(i * 2 + (p + 4), p)
            for n in range(4 + (NBLK - 6) // 2 * 2, NBLK + 2):
                step(n, n % 2)

        exists = lambda j: not known(j) or 0 <= j < NBLK
        first = lambda j: known(j) and j < 2
        half = lambda j, p, n: j * (n // 2) - p * (n // 2)

        @block.gpsimd
        def _(pool):
            def gather(p, dst, src, done):
                idx = bass.IndirectOffsetOnAxis(ap=wrow_p[p][:, :], axis=0)
                pool.indirect_dma_start(out=dst[:, :], out_offset=None, in_=src, in_offset=idx).then_inc(done, 16)

            def gathers(j, p):
                if not first(j):
                    pool.wait_ge(biases_loaded[p], half(j, p, 32))
                pool.tensor_copy(wrow_p[p][:, :], wrow[:, bass.ds(j, 1)]).then_inc(row_ready, 1)
                pool.wait_ge(row_ready, j + 1)
                if not first(j):
                    pool.wait_ge(up_low, j * 2 - 2)
                pool.sem_inc(gather_turn, 1)
                for m in range(2):
                    gather(p, raw[m][p], tables[m], up_loaded[p])
                if not first(j):
                    pool.wait_ge(down_low, j - 1)
                pool.sem_inc(gather_turn, 1)
                gather(p, raw[2][p], tables[2], down_loaded[p])
                if not first(j):
                    pool.wait_ge(y_full, j - 1)
                pool.sem_inc(gather_turn, 1)
                for m in range(2):
                    gather(p, wb[m][p], bias_tables[m], biases_loaded[p])

            def step(n, p):
                if exists(n + 2):
                    gathers(n + 2, p)

            steps(pool, step)

        @block.sync
        def _(sp):
            def load(j, p):
                if not first(j):
                    sp.wait_ge(x_psum, j * 2 - 2)
                sp.dma_start(rows[p][:, :, :, :].rearrange("p s h d -> p s (h d)"), rows_dram[bass.ds(j, 1), :, :, :].rearrange("o p s d -> (o p) s d"))\
                  .then_inc(rows_loaded[p], 16)

            def store(j, p):
                sp.wait_ge(out_ready, j + 1)
                sp.dma_start(out_dram[bass.ds(j, 1), :, :, :].rearrange("o p s d -> (o p) s d"), yo[p][:, :, :])\
                  .then_inc(stored[p], 16)

            def step(n, p):
                if exists(n + 2):
                    load(n + 2, p)
                if exists(n - 2):
                    store(n - 2, p)

            steps(sp, step)
            for p in range(2):
                sp.wait_ge(stored[p], 16 * ((NBLK + 1 - p) // 2))

        def up_weight(a):
            return a[:, :].rearrange("p (c q f) -> p c f q", c=DC, f=F2)

        def up_split(a):
            return a[:, :].rearrange("p (c f q) -> p c f q", c=DC, f=F2)

        @block.scalar
        def _(act):
            def gelu(j, p):
                act.wait_ge(gu_psum, j + 1)
                act.wait_ge(biases_loaded[p], half(j, p, 32) + 32)
                if not first(j):
                    act.wait_ge(y_full, j - 1)
                for f in range(F2):
                    last = act.activation(gf[p][:, f, :], psG[p][:, f, :], ACT.Gelu, bias=wb[0][p][:, f:f + 1])
                last.then_inc(gelu_done, 1)

            def x_split(j, p):
                act.wait_ge(x_psum, j * 2 + 1)
                if not first(j):
                    act.wait_ge(gu_psum, j - 1)
                act.activation(x_hi[p][:, :, :], psX[0][:, :, :, :].rearrange("p c s t -> p c (s t)"), ACT.Copy).then_inc(x_high, 1)

            def y_split(j, p):
                act.wait_ge(y_full, j + 1)
                if not first(j):
                    act.wait_ge(d_psum, j * ST - ST)
                act.activation(y_hi[p][:, :, :], yf[p][:, :, :], ACT.Copy).then_inc(y_high, 1)

            def up_weights(j, p):
                act.wait_ge(up_loaded[p], half(j, p, 32) + 32)
                if not first(j):
                    act.wait_ge(gu_psum, j - 1)
                for m in range(2):
                    act.activation(up_split(hi[m][p]), up_weight(raw[m][p]), ACT.Copy).then_inc(up_high, 1)

            def down_weights(j, p):
                act.wait_ge(down_loaded[p], half(j, p, 16) + 16)
                if not first(j):
                    act.wait_ge(d_psum, j * ST - ST)
                act.activation(hi[2][p][:, :], raw[2][p][:, :], ACT.Copy).then_inc(down_high, 1)

            def step(n, p):
                if exists(n - 1):
                    gelu(n - 1, 1 - p)
                if exists(n + 1):
                    x_split(n + 1, 1 - p)
                if exists(n - 1):
                    y_split(n - 1, 1 - p)
                if exists(n + 1):
                    up_weights(n + 1, 1 - p)
                if exists(n):
                    down_weights(n, p)

            steps(act, step)

        @block.vector
        def _(dve):
            def out_rows(j, p):
                if not first(j):
                    dve.wait_ge(stored[p], half(j, p, 16))
                for s in range(ST):
                    dve.wait_ge(d_psum, j * ST + (s + 1))
                    last = dve.tensor_copy(yo[p][:, s, :], psD[s][:, :])
                last.then_inc(out_ready, 1)

            def gate(j, p):
                dve.wait_ge(gelu_done, j + 1)
                if not first(j):
                    dve.wait_ge(y_high, j - 1)
                for f in range(F2):
                    last = dve.scalar_tensor_tensor(yf[p][:, f, :], psU[p][:, f, :], wb[1][p][:, f:f + 1],
                                                    gf[p][:, f, :], ALU.add, ALU.mult)
                last.then_inc(y_full, 1)

            def x_split(j, p):
                dve.wait_ge(x_psum, j * 2 + 2)
                if not first(j):
                    dve.wait_ge(gu_psum, j - 1)
                dve.tensor_copy(x_lo[p][:, :, :], psX[1][:, :, :, :].rearrange("p c s t -> p c (s t)")).then_inc(x_low, 1)

            def y_split(j, p):
                dve.wait_ge(y_high, j + 1)
                dve.tensor_tensor(y_lo[p][:, :, :], yf[p][:, :, :], y_hi[p][:, :, :], ALU.subtract).then_inc(y_low, 1)

            def up_weights(j, p):
                for m in range(2):
                    dve.wait_ge(up_high, j * 2 + (m + 1))
                    dve.tensor_tensor(up_split(lo[m][p]), up_weight(raw[m][p]), up_split(hi[m][p]), ALU.subtract)\
                       .then_inc(up_low, 1)

            def down_weights(j, p):
                dve.wait_ge(down_high, j + 1)
                dve.tensor_tensor(lo[2][p][:, :], raw[2][p][:, :], hi[2][p][:, :], ALU.subtract).then_inc(down_low, 1)

            def step(n, p):
                if exists(n - 2):
                    out_rows(n - 2, p)
                if exists(n - 1):
                    gate(n - 1, 1 - p)
                if exists(n + 1):
                    x_split(n + 1, 1 - p)
                if exists(n - 1):
                    y_split(n - 1, 1 - p)
                if exists(n + 1):
                    up_weights(n + 1, 1 - p)
                if exists(n):
                    down_weights(n, p)

            steps(dve, step)

        @block.tensor
        def _(pe):
            def turn(j, p):
                pe.wait_ge(rows_loaded[p], half(j, p, 16) + 16)
                for h in range(2):
                    if not known(j) or j:
                        pe.wait_ge((x_high, x_low)[h], j)
                    for s in range(ST):
                        for c in range(DC):
                            last = pe.transpose(psX[h][:, c, s, :], rows[p][:, s, h, c::DC], k.ident_b[:, :])
                    last.then_inc(x_psum, 1)

            def up(j, p):
                pe.wait_ge(x_high, j + 1)
                pe.wait_ge(x_low, j + 1)
                if not first(j):
                    pe.wait_ge(y_full, j - 1)
                for m, ps in ((0, psG), (1, psU)):
                    pe.wait_ge(up_low, j * 2 + (m + 1))
                    for f in range(F2):
                        for c in range(DC):
                            col = (c * F2 + f) * P
                            last = three_products(pe, ps[p][:, f, :], [a[m][p][:, col:col + P] for a in (hi, lo)],
                                                  [a[p][:, c, :] for a in (x_hi, x_lo)], c == 0, c == DC - 1)
                last.then_inc(gu_psum, 1)

            def down(j, p):
                pe.wait_ge(y_low, j + 1)
                pe.wait_ge(down_low, j + 1)
                if not known(j) or j:
                    pe.wait_ge(out_ready, j)
                for s in range(ST):
                    for f in range(F2):
                        last = three_products(pe, psD[s][:, :], [a[p][:, f, s * P:(s + 1) * P] for a in (y_hi, y_lo)],
                                              [a[2][p][:, f * D:(f + 1) * D] for a in (hi, lo)], f == 0, f == F2 - 1)
                    last.then_inc(d_psum, 1)

            def step(n, p):
                if exists(n + 1):
                    turn(n + 1, 1 - p)
                if exists(n):
                    up(n, p)
                if exists(n - 1):
                    down(n - 1, 1 - p)

            steps(pe, step)


def stage_combine(k, slots, share, combine, out):
    nc = k.nc
    with ExitStack() as ctx:
        sb = lambda name, shape, dt: ctx.enter_context(nc.sbuf_tensor(name, shape, dt))
        ALL_N = E_N + SH_N
        b2 = sb("m_b2", [ALL_N, D], F32)
        b2_hi, b2_lo = sb("m_b2hi", [ALL_N, D], BF16), sb("m_b2lo", [ALL_N, D], BF16)
        mixT_hi, mixT_lo = (sb(f"m_mix{n}", [ALL_N, NT, P], BF16) for n in ("h", "l"))
        mix_set = k.semaphore("m_ms")
        got = [sb(f"m_got{i}", [P, 2, D], F32) for i in range(4)]
        psC = [ctx.enter_context(nc.psum_tensor(f"ps_mc{i}", [E_N, 4, P], F32)) for i in range(4)]
        psB = [ctx.enter_context(nc.psum_tensor(f"ps_mb{i}", [P, D], F32)) for i in range(2)]
        sem = lambda name: k.semaphore(("m_" + name))
        b_loaded, b_high, b_low, turned, mix_high, mix_low, b_psum, b_added, first_added, done = (
            sem(n) for n in ("bl", "bh", "blo", "tu", "mh", "ml", "bp", "ba", "fa", "do"))
        gathered = [sem(f"g{i}") for i in range(4)]
        stored = sem("st")
        block = ctx.enter_context(nc.Block())
        out_dram = out.rearrange("b s d -> (b s) d")

        @block.gpsimd
        def _(pool):
            for t in range(NT):
                if t >= 4:
                    pool.wait_ge(done, t - 3)
                for s in range(2):
                    pool.indirect_dma_start(out=got[t % 4][:, s, :], out_offset=None, in_=k.scratch["results"],
                                            in_offset=bass.IndirectOffsetOnAxis(ap=slots[:, s, t:t + 1], axis=0))\
                        .then_inc(gathered[t % 4], 16)

        @block.sync
        def _(sp):
            sp.dma_start(b2[0:E_N, :], k.ins["L1_ffn_rb2"]).then_inc(b_loaded, 16)
            sp.dma_start(b2[E_N:, :], k.ins["L1_ffn_sb2"]).then_inc(b_loaded, 16)
            for t in range(NT):
                sp.wait_ge(done, t + 1)
                sp.dma_start(out_dram[t * P:(t + 1) * P, :], k.x[:, t, :]).then_inc(stored, 16)
            sp.wait_ge(stored, 16 * NT)

        @block.scalar
        def _(act):
            act.wait_ge(b_loaded, 32)
            act.wait_ge(mix_set, 2)
            act.activation(b2_hi[:, :], b2[:, :], ACT.Copy).then_inc(b_high, 1)
            for i in range(4):
                act.wait_ge(turned, i + 1)
                act.activation(mixT_hi[0:E_N, 4 * i:4 * i + 4, :], psC[i][:, :, :], ACT.Copy).then_inc(mix_high, 1)

        @block.tensor
        def _(pe):
            for i in range(4):
                for j in range(4):
                    last = pe.transpose(psC[i][:, j, :], combine[:, 4 * i + j, :], k.ident[:, :])
                last.then_inc(turned, 1)
            pe.wait_ge(b_low, 1)
            for t in range(NT):
                pe.wait_ge(mix_low, t // 4 + 1)
                if t >= 2:
                    pe.wait_ge(b_added, t - 1)
                three_products(pe, psB[t % 2][:, :], [a[:, t, :] for a in (mixT_hi, mixT_lo)], [b2_hi[:, :], b2_lo[:, :]])\
                    .then_inc(b_psum, 1)

        @block.vector
        def _(dve):
            dve.memset(mixT_hi[:, :, :], 1.0).then_inc(mix_set, 1)
            dve.memset(mixT_lo[:, :, :], 0.0).then_inc(mix_set, 1)
            dve.wait_ge(b_high, 1)
            dve.tensor_tensor(b2_lo[:, :], b2[:, :], b2_hi[:, :], ALU.subtract).then_inc(b_low, 1)
            for i in range(4):
                dve.wait_ge(mix_high, i + 1)
                dve.tensor_tensor(mixT_lo[0:E_N, 4 * i:4 * i + 4, :], psC[i][:, :, :], mixT_hi[0:E_N, 4 * i:4 * i + 4, :],
                                  ALU.subtract).then_inc(mix_low, 1)
            for t in range(NT):
                x = k.x[:, t, :]
                dve.wait_ge(b_psum, t + 1)
                dve.tensor_tensor(x, x, psB[t % 2][:, :], ALU.add).then_inc(b_added, 1)
                dve.wait_ge(gathered[t % 4], 32 * (t // 4 + 1))
                dve.wait_ge(b_added, t + 1)
                dve.scalar_tensor_tensor(x, got[t % 4][:, 0, :], share[:, 0, t:t + 1], x, ALU.mult, ALU.add).then_inc(first_added, 1)
                dve.wait_ge(first_added, t + 1)
                dve.scalar_tensor_tensor(x, got[t % 4][:, 1, :], share[:, 1, t:t + 1], x, ALU.mult, ALU.add).then_inc(done, 1)


def build(nc, ins, out, scratch):
    with ExitStack() as ctx:
        k = Kernel(nc, ins, out, scratch, ctx)
        left = lambda stack, name, shape, dt: stack.enter_context(nc.sbuf_tensor(name, shape, dt))
        stats = left(ctx, "stats", [P, NT, 6], F32)
        with ExitStack() as attention:
            with ExitStack() as context:
                ctxT = context.enter_context(nc.sbuf_tensor("ctxT", [P, DC, TOK], F32, side="right"))
                with ExitStack() as low:
                    k.w1T = left(low, "w1T", [P, DC * FF], BF16)
                    k.w2T = left(low, "w2T", [P, FC * D], BF16)
                    stage_constants_and_ternary_weights(k)
                    mean, quant, dequant = (left(low, n, [P, NT], F32) for n in ("ffn_mean", "ffn_quant", "ffn_dequant"))
                    with ExitStack() as conv:
                        outT = left(conv, "outT", [P, DC, TOK], F32)
                        with ExitStack() as lower:
                            qT = left(lower, "qT", [P, DC, TOK], F32)
                            stage_transposes(k, ctxT, qT)
                            stage_long_conv(k, ctxT, qT, outT)
                        b1, b2 = (low.enter_context(nc.sbuf_tensor(n, [P, w], F32, side="right"))
                                  for n, w in (("ffn_b1", FF), ("ffn_b2", D)))
                        stage_ffn_entry(k, outT, mean, quant, dequant, b1, b2)
                    stage_ffn(k, mean, quant, dequant, b1, b2)
                k.clear_semaphores()
                ks = scratch["keys"]
                v_hi = left(attention, "v_hi", [P, NT, HEADS, VC], BF16)
                v_lo = left(attention, "v_lo", [P, NT, HEADS, VC], BF16)
                qw, ow = (left(attention, n, [P, 2, DC, D], BF16) for n in ("qw", "ow"))
                x_mean, x_rstd = (left(attention, n, [P, NT], F32) for n in ("x_mean", "x_rstd"))
                sel = left(attention, "sel", [P, 2, P], BF16)
                with ExitStack() as kv:
                    kw, vw = (left(kv, n, [P, 2, DC, D], BF16) for n in ("kw", "vw"))
                    vbias = left(kv, "vbias", [P, D], F32)
                    stage_keys_values(k, ctxT, kw, vw, qw, ow, k.vectors, vbias, ks, v_hi, v_lo, x_mean, x_rstd, sel)
            stage_attention(k, ks, v_hi, v_lo, qw, ow, k.vectors, x_mean, x_rstd, sel, stats)
        slots = left(ctx, "slots", [P, 2, NT], U32)
        share = left(ctx, "share", [P, 2, NT], F32)
        combine = left(ctx, "combine", [P, NT, E_N], F32)
        wrow = left(ctx, "wrow", [P, NBLK], U32)
        with ExitStack() as moe:
            xf = left(moe, "xf", [P, NT, 2, D], BF16)
            xT_hi, xT_lo = (left(moe, n, [P, DC, TOK], BF16) for n in ("xT_hi", "xT_lo"))
            xaff = left(moe, "xaff", [P, NT, E_N], F32)
            sgu = left(moe, "sgu", [P, 2, SH_N, 2, DC * FE], BF16)
            sd = left(moe, "sd", [P, 2, SH_N, F2 * D], BF16)
            stage_router(k, stats, xf, xT_hi, xT_lo, xaff, sgu, sd)
            stage_route_and_shared(k, xf, xT_hi, xT_lo, xaff, sgu, sd, slots, share, combine, wrow)
        stage_experts(k, wrow)
        stage_combine(k, slots, share, combine, out)
        k.open_semaphores.close()


def program(nc, ins, out):
    scratch = {"taps": nc.dram_tensor("taps_padded", [H0, PAD + D], F32, kind="Internal").ap(),
               "keys": nc.dram_tensor("keys_stacked", [B, P, HC, DC, S], BF16, kind="Internal").ap(),
               "rows": nc.dram_tensor("expert_rows", [NBLK * BLK, 2 * D], BF16, kind="Internal").ap(),
               "results": nc.dram_tensor("expert_results", [NBLK * BLK, D], F32, kind="Internal").ap()}
    build(nc, ins, out, scratch)


INPUTS = ["x", "ctx_2048", "L0_xattn_ssm_kernel", "L0_xattn_D", "L0_ffn_w1", "L0_ffn_b1", "L0_ffn_w2", "L0_ffn_b2",
          "L1_xattn_Wq", "L1_xattn_bq", "L1_xattn_gq", "L1_xattn_Wk_img", "L1_xattn_bk_img", "L1_xattn_gk_img",
          "L1_xattn_Wv_img", "L1_xattn_bv_img", "L1_xattn_Wo", "L1_xattn_bo", "L1_ffn_wa", "L1_ffn_rg", "L1_ffn_rgb",
          "L1_ffn_rw1", "L1_ffn_rb1", "L1_ffn_rw2", "L1_ffn_rb2", "L1_ffn_sg", "L1_ffn_sgb", "L1_ffn_sw1",
          "L1_ffn_sb1", "L1_ffn_sw2", "L1_ffn_sb2"]


def kernel(**inputs):
    import concourse.bacc as _bacc
    from concourse.bass_utils import run_bass_kernel_spmd as _run

    nc = _bacc.Bacc("TRN2", target_bir_lowering=False, num_devices=1)
    arrays, ins = {}, {}
    for name in INPUTS:
        a = np.ascontiguousarray(inputs[name])
        arrays[f"in_{name}"] = a
        ins[name] = nc.dram_tensor(f"in_{name}", a.shape, mybir.dt.from_np(a.dtype), kind="ExternalInput").ap()
    out = nc.dram_tensor("out", (B, S, D), F32, kind="ExternalOutput").ap()
    program(nc, ins, out)
    return _run(nc, [arrays], core_ids=[0]).results[0]["out"]
```
